# Optimizing a Trainium2 kernel written in Bass

```python
import numpy as np
import jax
import jax.numpy as jnp

def _softmax(x, axis=-1):
    return jax.nn.softmax(x, axis=axis)

def _gelu(x):
    return jax.nn.gelu(x, approximate=True)

def _silu(x):
    return jax.nn.silu(x)

def _sigmoid(x):
    return jax.nn.sigmoid(x)

def _layernorm(x, axis=-1, eps=1e-05):
    m = jnp.mean(x, axis=axis, keepdims=True)
    v = jnp.var(x, axis=axis, keepdims=True)
    return (x - m) / jnp.sqrt(v + eps)

def _scatter_add(tgt, idx, src, axis=0):
    return tgt.at[idx].add(src)

def _segment_sum(src, seg, n):
    return jax.ops.segment_sum(src, seg, n)
kernel_name = 'mk_adaln_attn_ffn_d1_seqx_r8_2afba5'

def setup_inputs(seed: int=0):
    np.random.seed(seed)
    _w = jnp.asarray

    def _rec_inputs():
        import jax
        import jax.numpy as jnp
        _rk = jax.random.key(seed)
        x = -0.0003929 + 0.9999 * jax.random.normal(jax.random.fold_in(_rk, 1), (64, 32, 512), jnp.float32)
        _lenS = 32 - jax.random.randint(jax.random.fold_in(_rk, 7), (64,), 0, max(1, 32 // 4) + 1, jnp.int32)
        _lenS2 = 32 - jax.random.randint(jax.random.fold_in(_rk, 8), (64,), 0, max(1, 32 // 4) + 1, jnp.int32)
        pos_BxS = jnp.broadcast_to(jnp.arange(32, dtype=jnp.int32), (64, 32))
        itok_B_0_7 = jax.random.randint(jax.random.fold_in(_rk, 13), (64,), 0, 8, jnp.int32)
        _validS = jnp.arange(32)[None, :] < _lenS[:, None]
        _validS2 = jnp.arange(32)[None, :] < _lenS2[:, None]
        _causal = jnp.tril(jnp.ones((32, 32), dtype=bool))
        mask_BxS_bf1 = jnp.ones((64, 32), dtype=bool)
        return (x, pos_BxS, itok_B_0_7, mask_BxS_bf1)
    x, pos_BxS, itok_B_0_7, mask_BxS_bf1 = _rec_inputs()

    def _L0_cond_setup():
        import jax, jax.numpy as jnp
        import numpy as np
        H, HKV, D, HID = (32, 8, 128, 512)
        THETA = 500000.0
        NAD, R = (8, 16)
        BATCH, T = (4, 128)

        def apply_rope(x, positions, head_dim, theta):
            half = head_dim // 2
            freq = theta ** (-jnp.arange(half, dtype=jnp.float32) / half)
            ang = positions.astype(jnp.float32)[..., None] * freq
            cos = jnp.cos(ang)[:, :, None, :]
            sin = jnp.sin(ang)[:, :, None, :]
            x1, x2 = jnp.split(x, 2, axis=-1)
            out = jnp.concatenate([x1 * cos - x2 * sin, x2 * cos + x1 * sin], axis=-1)
            return out.astype(x.dtype)

        def lora_linear(x, w, a, b, adapter_indices):
            base = jnp.einsum('bti,io->bto', x, w)
            ax = jnp.einsum('bti,bir->btr', x, a[adapter_indices])
            return base + jnp.einsum('btr,bro->bto', ax, b[adapter_indices])
        key = jax.random.key(seed)
        ks = jax.random.split(key, 16)
        s = 0.02
        inp = {'x': jax.random.normal(ks[0], (BATCH, T, HID), jnp.float32), 'attention_mask': jnp.ones((BATCH, T), bool), 'positions': jnp.tile(jnp.arange(T, dtype=jnp.int32)[None, :], (BATCH, 1)), 'adapter_indices': jax.random.randint(ks[1], (BATCH,), 0, NAD, jnp.int32), 'wq': jax.random.normal(ks[2], (HID, H * D), jnp.float32) * s, 'wk': jax.random.normal(ks[3], (HID, HKV * D), jnp.float32) * s, 'wv': jax.random.normal(ks[4], (HID, HKV * D), jnp.float32) * s, 'wo': jax.random.normal(ks[5], (H * D, HID), jnp.float32) * s, 'aq': jax.random.normal(ks[6], (NAD, HID, R), jnp.float32) * 0.01, 'bq': jax.random.normal(ks[7], (NAD, R, H * D), jnp.float32) * 0.01, 'ak': jax.random.normal(ks[8], (NAD, HID, R), jnp.float32) * 0.01, 'bk': jax.random.normal(ks[9], (NAD, R, HKV * D), jnp.float32) * 0.01, 'av': jax.random.normal(ks[10], (NAD, HID, R), jnp.float32) * 0.01, 'bv': jax.random.normal(ks[11], (NAD, R, HKV * D), jnp.float32) * 0.01, 'ao': jax.random.normal(ks[12], (NAD, H * D, R), jnp.float32) * 0.01, 'bo': jax.random.normal(ks[13], (NAD, R, HID), jnp.float32) * 0.01}
        return inp
    _L0_cond_all = _L0_cond_setup()
    _L0_cond_in = {k: v for k, v in _L0_cond_all.items() if k in ('wq', 'wk', 'wv', 'wo', 'aq', 'bq', 'ak', 'bk', 'av', 'bv', 'ao', 'bo')}
    del _L0_cond_all

    def _L0_attn_setup():
        import jax, jax.numpy as jnp
        import numpy as np
        HIDDEN = 512
        HEADS = 32
        D_K = HIDDEN // HEADS
        key = jax.random.key(seed)
        ks = jax.random.split(key, 5)
        scale = 1.0 / np.sqrt(HIDDEN)
        x = jax.random.normal(ks[0], (2, 256, HIDDEN), dtype=jnp.float32)
        w_q = jax.random.uniform(ks[1], (HIDDEN, HIDDEN), jnp.float32, -scale, scale)
        w_k = jax.random.uniform(ks[2], (HIDDEN, HIDDEN), jnp.float32, -scale, scale)
        w_v = jax.random.uniform(ks[3], (HIDDEN, HIDDEN), jnp.float32, -scale, scale)
        w_o = jax.random.uniform(ks[4], (HIDDEN, HIDDEN), jnp.float32, -scale, scale)
        return {'x': x, 'w_q': w_q, 'w_k': w_k, 'w_v': w_v, 'w_o': w_o}
    _L0_attn_all = _L0_attn_setup()
    _L0_attn_in = {k: v for k, v in _L0_attn_all.items() if k in ('w_q', 'w_k', 'w_v', 'w_o')}
    del _L0_attn_all

    def _L0_cond2_setup():
        import jax, jax.numpy as jnp
        import numpy as np
        TOP_K = 2
        LANG_BIAS = 5.0
        SCALING = 32.0 / 16.0
        LANGUAGE_PAD_ID = -1
        key = jax.random.key(seed)
        ks = jax.random.split(key, 6)
        B, T, D, O, E, R = (4, 256, 512, 512, 8, 16)
        x = jax.random.normal(ks[0], (B, T, D), dtype=jnp.float32)
        language_ids = jax.random.randint(ks[1], (B,), 0, E).astype(jnp.int64)
        W = jax.random.normal(ks[2], (O, D), dtype=jnp.float32) * (1.0 / np.sqrt(D))
        Wr = jax.random.normal(ks[3], (E, D), dtype=jnp.float32) * (1.0 / np.sqrt(D))
        A = jax.random.normal(ks[4], (E, R, D), dtype=jnp.float32) * (1.0 / np.sqrt(D))
        Bm = jax.random.normal(ks[5], (O, R), dtype=jnp.float32) * 0.0
        Bm = jnp.broadcast_to(Bm, (E, O, R)) + jax.random.normal(ks[5], (E, O, R), dtype=jnp.float32) * 0.02
        return {'x': x, 'language_ids': language_ids, 'W': W, 'Wr': Wr, 'A': A, 'B': Bm}
    _L0_cond2_all = _L0_cond2_setup()
    _L0_cond2_in = {k: v for k, v in _L0_cond2_all.items() if k in ('W', 'Wr', 'A', 'B')}
    del _L0_cond2_all

    def _L0_ffn_setup():
        import jax, jax.numpy as jnp
        import numpy as np
        D_IN = 512
        D_OUT = 512
        RANK = 16
        NUM_EXPERTS = 8
        TOP_K = 2
        SCALING = 32.0 / RANK
        key = jax.random.key(seed)
        ks = jax.random.split(key, 6)
        x = jax.random.normal(ks[0], (4, 256, D_IN), dtype=jnp.float32)
        W_base = jax.random.normal(ks[1], (D_OUT, D_IN), dtype=jnp.float32) * (1.0 / np.sqrt(D_IN))
        b_base = jax.random.normal(ks[2], (D_OUT,), dtype=jnp.float32) * 0.01
        W_router = jax.random.normal(ks[3], (NUM_EXPERTS, D_IN), dtype=jnp.float32) * 0.01
        A_stack = jax.random.uniform(ks[4], (NUM_EXPERTS, RANK, D_IN), dtype=jnp.float32, minval=-1.0, maxval=1.0) * (1.0 / np.sqrt(D_IN))
        B_stack = jax.random.normal(ks[5], (NUM_EXPERTS, D_OUT, RANK), dtype=jnp.float32) * 0.02
        return {'x': x, 'W_base': W_base, 'b_base': b_base, 'W_router': W_router, 'A_stack': A_stack, 'B_stack': B_stack}
    _L0_ffn_all = _L0_ffn_setup()
    _L0_ffn_in = {k: v for k, v in _L0_ffn_all.items() if k in ('W_base', 'b_base', 'W_router', 'A_stack', 'B_stack')}
    del _L0_ffn_all
    return {'x': x, 'pos_BxS': pos_BxS, 'itok_B_0_7': itok_B_0_7, 'mask_BxS_bf1': mask_BxS_bf1, 'L0_cond_wq': _L0_cond_in['wq'], 'L0_cond_wk': _L0_cond_in['wk'], 'L0_cond_wv': _L0_cond_in['wv'], 'L0_cond_wo': _L0_cond_in['wo'], 'L0_cond_aq': _L0_cond_in['aq'], 'L0_cond_bq': _L0_cond_in['bq'], 'L0_cond_ak': _L0_cond_in['ak'], 'L0_cond_bk': _L0_cond_in['bk'], 'L0_cond_av': _L0_cond_in['av'], 'L0_cond_bv': _L0_cond_in['bv'], 'L0_cond_ao': _L0_cond_in['ao'], 'L0_cond_bo': _L0_cond_in['bo'], 'L0_attn_w_q': _L0_attn_in['w_q'], 'L0_attn_w_k': _L0_attn_in['w_k'], 'L0_attn_w_v': _L0_attn_in['w_v'], 'L0_attn_w_o': _L0_attn_in['w_o'], 'L0_cond2_W': _L0_cond2_in['W'], 'L0_cond2_Wr': _L0_cond2_in['Wr'], 'L0_cond2_A': _L0_cond2_in['A'], 'L0_cond2_B': _L0_cond2_in['B'], 'L0_ffn_W_base': _L0_ffn_in['W_base'], 'L0_ffn_b_base': _L0_ffn_in['b_base'], 'L0_ffn_W_router': _L0_ffn_in['W_router'], 'L0_ffn_A_stack': _L0_ffn_in['A_stack'], 'L0_ffn_B_stack': _L0_ffn_in['B_stack']}

def reference(x, pos_BxS, itok_B_0_7, mask_BxS_bf1, L0_cond_wq, L0_cond_wk, L0_cond_wv, L0_cond_wo, L0_cond_aq, L0_cond_bq, L0_cond_ak, L0_cond_bk, L0_cond_av, L0_cond_bv, L0_cond_ao, L0_cond_bo, L0_attn_w_q, L0_attn_w_k, L0_attn_w_v, L0_attn_w_o, L0_cond2_W, L0_cond2_Wr, L0_cond2_A, L0_cond2_B, L0_ffn_W_base, L0_ffn_b_base, L0_ffn_W_router, L0_ffn_A_stack, L0_ffn_B_stack):
    import jax
    import jax.numpy as jnp

    def _L0_cond_ref(x, attention_mask, positions, adapter_indices, wq, wk, wv, wo, aq, bq, ak, bk, av, bv, ao, bo):
        import jax, jax.numpy as jnp
        import numpy as np
        H, HKV, D, HID = (32, 8, 128, 512)
        THETA = 500000.0
        NAD, R = (8, 16)
        BATCH, T = (4, 128)

        def apply_rope(x, positions, head_dim, theta):
            half = head_dim // 2
            freq = theta ** (-jnp.arange(half, dtype=jnp.float32) / half)
            ang = positions.astype(jnp.float32)[..., None] * freq
            cos = jnp.cos(ang)[:, :, None, :]
            sin = jnp.sin(ang)[:, :, None, :]
            x1, x2 = jnp.split(x, 2, axis=-1)
            out = jnp.concatenate([x1 * cos - x2 * sin, x2 * cos + x1 * sin], axis=-1)
            return out.astype(x.dtype)

        def lora_linear(x, w, a, b, adapter_indices):
            base = jnp.einsum('bti,io->bto', x, w)
            ax = jnp.einsum('bti,bir->btr', x, a[adapter_indices])
            return base + jnp.einsum('btr,bro->bto', ax, b[adapter_indices])
        B, Tt, _ = x.shape
        G = H // HKV
        q = lora_linear(x, wq, aq, bq, adapter_indices).reshape(B, Tt, H, D)
        k = lora_linear(x, wk, ak, bk, adapter_indices).reshape(B, Tt, HKV, D)
        v = lora_linear(x, wv, av, bv, adapter_indices).reshape(B, Tt, HKV, D)
        q = apply_rope(q, positions, D, THETA)
        k = apply_rope(k, positions, D, THETA)
        qg = q.reshape(B, Tt, HKV, G, D)
        scale = 1.0 / np.sqrt(D)
        logits = jnp.einsum('bqhgd,bkhd->bhgqk', qg, k) * scale
        causal = jnp.tril(jnp.ones((Tt, Tt), bool))
        mask = causal[None, None, None] & attention_mask[:, None, None, None, :]
        logits = jnp.where(mask, logits, jnp.finfo(logits.dtype).min)
        p = jax.nn.softmax(logits, axis=-1)
        o = jnp.einsum('bhgqk,bkhd->bqhgd', p, v).reshape(B, Tt, H * D)
        return lora_linear(o, wo, ao, bo, adapter_indices)

    def _L0_attn_ref(x, w_q, w_k, w_v, w_o):
        import jax, jax.numpy as jnp
        import numpy as np
        HIDDEN = 512
        HEADS = 32
        D_K = HIDDEN // HEADS
        B, S, _ = x.shape

        def proj(w):
            y = jnp.einsum('bsd,ed->bse', x, w)
            return y.reshape(B, S, HEADS, D_K).transpose(0, 2, 1, 3)
        q, k, v = (proj(w_q), proj(w_k), proj(w_v))
        scores = jnp.einsum('bhqd,bhkd->bhqk', q, k) / jnp.sqrt(jnp.float32(D_K))
        attn = jax.nn.softmax(scores, axis=-1)
        out = jnp.einsum('bhqk,bhkd->bhqd', attn, v)
        out = out.transpose(0, 2, 1, 3).reshape(B, S, HIDDEN)
        return jnp.einsum('bse,oe->bso', out, w_o)

    def _L0_cond2_ref(x, language_ids, W, Wr, A, B):
        import jax, jax.numpy as jnp
        import numpy as np
        TOP_K = 2
        LANG_BIAS = 5.0
        SCALING = 32.0 / 16.0
        LANGUAGE_PAD_ID = -1
        base = jnp.einsum('btd,od->bto', x, W)
        E = Wr.shape[0]
        logits = jnp.einsum('btd,ed->bte', x.astype(jnp.float32), Wr.astype(jnp.float32))
        expert_targets = language_ids
        valid = expert_targets >= 0
        tgt = jnp.where(valid, expert_targets, 0)
        bias = jax.nn.one_hot(tgt, E, dtype=logits.dtype) * LANG_BIAS
        bias = jnp.where(valid[:, None], bias, 0.0)
        logits = logits + bias[:, None, :]
        topw, topi = jax.lax.top_k(logits, TOP_K)
        weights = jax.nn.softmax(topw, axis=-1)
        gates = jnp.sum(jax.nn.one_hot(topi, E, dtype=weights.dtype) * weights[..., None], axis=-2)
        gates = gates.astype(x.dtype)
        h = jnp.einsum('btd,erd->bter', x, A)
        lora_out = jnp.einsum('bter,bte,eor->bto', h, gates, B)
        return base + SCALING * lora_out

    def _L0_ffn_ref(x, W_base, b_base, W_router, A_stack, B_stack):
        import jax, jax.numpy as jnp
        import numpy as np
        D_IN = 512
        D_OUT = 512
        RANK = 16
        NUM_EXPERTS = 8
        TOP_K = 2
        SCALING = 32.0 / RANK
        orig_shape = x.shape
        xf = x.reshape(-1, D_IN)
        logits = xf @ W_router.T
        probs = jax.nn.softmax(logits, axis=-1)
        topk_p, topk_i = jax.lax.top_k(probs, TOP_K)
        topk_p = topk_p / jnp.sum(topk_p, axis=-1, keepdims=True)
        combine = jnp.sum(jax.nn.one_hot(topk_i, NUM_EXPERTS, dtype=xf.dtype) * topk_p[..., None], axis=1)
        h = jnp.einsum('nd,erd->ner', xf, A_stack)
        h = h * combine[..., None]
        lora_out = jnp.einsum('ner,eor->no', h, B_stack) * SCALING
        base_out = xf @ W_base.T + b_base
        out = base_out + lora_out
        return out.reshape(orig_shape[:-1] + (D_OUT,))
    x = x + _L0_attn_ref(_L0_cond_ref(x, mask_BxS_bf1, pos_BxS, itok_B_0_7, L0_cond_wq, L0_cond_wk, L0_cond_wv, L0_cond_wo, L0_cond_aq, L0_cond_bq, L0_cond_ak, L0_cond_bk, L0_cond_av, L0_cond_bv, L0_cond_ao, L0_cond_bo), L0_attn_w_q, L0_attn_w_k, L0_attn_w_v, L0_attn_w_o)
    x = x + _L0_ffn_ref(_L0_cond2_ref(x, itok_B_0_7, L0_cond2_W, L0_cond2_Wr, L0_cond2_A, L0_cond2_B), L0_ffn_W_base, L0_ffn_b_base, L0_ffn_W_router, L0_ffn_A_stack, L0_ffn_B_stack)
    return x

_drawn_inputs = setup_inputs


def setup_inputs(seed=0):
    import zlib

    import numpy as np

    out = dict(_drawn_inputs(seed))
    spreads = {}
    factors = {'L0_cond_wq': 8.0,
     'L0_cond_wk': 8.0,
     'L0_cond_aq': 8.0,
     'L0_cond_bq': 8.0,
     'L0_cond_ak': 8.0,
     'L0_cond_bk': 8.0,
     'L0_cond_av': 8.0,
     'L0_cond_bv': 8.0,
     'L0_cond_ao': 8.0,
     'L0_cond_bo': 8.0,
     'L0_attn_w_q': 8.0,
     'L0_attn_w_k': 8.0,
     'L0_cond2_Wr': 5.096,
     'L0_ffn_b_base': 8.0}
    for name, (base, spread) in spreads.items():
        noise = np.random.default_rng([zlib.crc32(name.encode()), seed]).standard_normal(out[name].shape)
        drawn = base * np.exp(spread * noise) if base else spread * noise
        out[name] = jnp.asarray(drawn.astype(out[name].dtype))
    for name, factor in factors.items():
        out[name] = (out[name] * factor).astype(out[name].dtype)
    return out
```

```python
from contextlib import ExitStack

import numpy as np
import concourse.bass as bass
from concourse import mybir

ALU = mybir.AluOpType
ACT = mybir.ActivationFunctionType
AX = mybir.AxisListType
F32 = mybir.dt.float32
F32R = mybir.dt.float32r
I32 = mybir.dt.int32
U8 = mybir.dt.uint8

B, T, DM = 64, 32, 512
TOKENS = B * T
P = 128
CT = 512
CHUNKS = TOKENS // CT
TILES = CT // P
KC = DM // P
KVH, GROUP, HD = 8, 4, 128
E, R = 8, 16
HEADS2, HD2 = 32, 16
THETA = 500000.0
LANG_BIAS, SCALING = 5.0, 2.0
FLT_MAX = 3.4028234663852886e38
PIECE = 5 * P

SLOTS = 11
RAWS = 3
PRIMED = 1
CONTENTS = [13, 13, 13, 10, 10, 10, 10, 9, 10, 10, 10]
SLOT_BASE = [sum(CONTENTS[:s]) for s in range(SLOTS)]
LORA_A_SLOTS = [8, 9, 10]
WO_FIRST = {6: 0, 7: 0, 8: 1, 9: 1, 10: 1}
QKV2_FIRST = 8
OUT2_PIECES = [(3, 8), (4, 8), (5, 8), (7, 8)]
BO_PIECE = (6, 8)
ROUTED = [
    ((8, 9), [(9, 9), (10, 9), (0, 12), (1, 12)]),
    ((2, 12), [(3, 9), (4, 9), (5, 9), (6, 9)]),
]
HEAD_ORDER = [8, 9, 10, 0, 1, 2, 3, 4, 5]
EPI_ORDER = [6, 7, 8, 9, 10]
MID_ORDER = [3, 4, 5, 6]

def _per_raw(n):
    return [len(range(r, n, RAWS)) for r in range(RAWS)]


RAW_HEAD, RAW_STEP, RAW_EPI, RAW_B, RAW_MID = map(_per_raw, (9, SLOTS, 5, 3, 4))
RAW_CHUNK = [8 * s + e + 4 * b + m + h
             for s, e, b, m, h in zip(RAW_STEP, RAW_EPI, RAW_B, RAW_MID, RAW_HEAD)]


def raw_use(c, part, j, k=0):
    r = j % RAWS
    before = j // RAWS
    if part == "prologue":
        return r, before
    n = before + RAW_HEAD[r] + c * RAW_CHUNK[r]
    if part == "step":
        return r, n + k * RAW_STEP[r]
    n = n + KVH * RAW_STEP[r]
    if part == "epi":
        return r, n
    n = n + RAW_EPI[r]
    if part == "b":
        return r, n + k * RAW_B[r]
    n = n + KC * RAW_B[r]
    if part == "mid":
        return r, n
    return r, n + RAW_MID[r]


PROJ = {"k": (0, 0), "v": (1, 0), "q0": (2, 0), "q1": (3, 0), "q2": (0, 1), "q3": (1, 1), "vT": (2, 1)}
WOUT = {"y0": (3, 0), "y1": (0, 0), "y2": (1, 0), "y3": (2, 0), "ho": (3, 1)}
N_LORA, N_PROJ, N_WO, N_ROUTE = [1, 1, 1, 0], [2, 2, 2, 1], [1, 1, 1, 2], [1, 1, 1, 0]
RING_CHUNK = [a + KVH * (b + w) + 1 + KC + 1 + 2 * r
              for a, b, w, r in zip(N_LORA, N_PROJ, N_WO, N_ROUTE)]


def ring_use(c, part, which, k=0):
    if part == "proj":
        b, at = PROJ[which]
        done = 0 if isinstance(k, int) and k == 0 else k - 1
        n = k * N_PROJ[b] + done * N_WO[b] + at + N_LORA[b]
    elif part == "wo":
        b, at = WOUT[which]
        n = (KVH if isinstance(k, int) and k == KVH else k + 1) * N_PROJ[b] + (k - 1) * N_WO[b] + at + N_LORA[b]
    elif part == "lora":
        b, n = which, 0
    else:
        b = which
        n = N_LORA[b] + KVH * (N_PROJ[b] + N_WO[b])
        if part != "bo":
            n = n + 1
            if part == "b":
                n = n + k
            else:
                n = n + KC
                if part == "route":
                    n = n + 1 + k * N_ROUTE[b]
    return b, n + c * RING_CHUNK[b]


C_FREQ, C_SIGN, C_EID, C_EVEN, C_ODD = range(5)
C_HM = 5
C_TIE = 13
C_E = 21
C_CAUSAL = 29
C_IDENT = 61
C_COLS = C_IDENT + P


def constants():
    p = np.arange(P)
    half = HD // 2
    c = np.zeros((P, C_COLS), np.float32)
    freq = np.float32(THETA) ** (-np.arange(half, dtype=np.float32) / np.float32(half))
    c[:, C_FREQ] = freq[p % half]
    c[:, C_SIGN] = np.where(p < half, -1.0, 1.0)
    c[:, C_EID] = p // R
    c[:, C_EVEN] = (p // HD2) % 2 == 0
    c[:, C_ODD] = (p // HD2) % 2 == 1
    c[:, C_HM:C_HM + 8] = (p // HD2)[:, None] == np.arange(8)
    c[:, C_TIE:C_TIE + 8] = 8 - np.arange(8)
    c[:, C_E:C_E + 8] = np.arange(8)
    c[:, C_CAUSAL:C_CAUSAL + T] = (p % T)[:, None] >= np.arange(T)
    c[:, C_IDENT:] = np.eye(P)
    return c


TWO_PI = 2 * np.pi
ROUND = 1.5 * 2.0 ** 23
PI_A = 6.28125
PI_B = float(np.float32(np.float32((TWO_PI - PI_A) * 2 ** 20).astype(np.int64) / 2 ** 20))
PI_C = float(np.float32(TWO_PI - PI_A - PI_B))
PI_IN = 3.1415925

N_TABLE = 16
N_ROUTING = 17


class Chain:

    def __init__(self, eng, sem, base):
        self.eng, self.sem, self.base, self.n = eng, sem, base, 0

    def then(self, ins):
        ins.then_inc(self.sem, 1)
        self.n += 1
        self.eng.wait_ge(self.sem, self.base + self.n)


def build(nc, xT, pos, idx, idx_tile, mask, bias, consts, stream, outT):
    with ExitStack() as ctx:
        def sb(name, shape, dt=F32):
            return ctx.enter_context(nc.sbuf_tensor(name, shape, dt))

        def sem(name):
            return ctx.enter_context(nc.semaphore(name))

        w_hi_t = [sb(f"w_hi{s}", [P, PIECE], F32R) for s in range(SLOTS)]
        w_lo_t = [sb(f"w_lo{s}", [P, PIECE], F32R) for s in range(SLOTS)]
        raw = [sb(f"raw{r}", [P, PIECE]) for r in range(RAWS)]
        act_hi = [sb(f"act_hi{i}", [P, KC, CT], F32R) for i in range(2)]
        act_lo = [sb(f"act_lo{i}", [P, KC, CT], F32R) for i in range(2)]
        q_hi, q_lo = sb("q_hi", [P, GROUP, CT], F32R), sb("q_lo", [P, GROUP, CT], F32R)
        k_hi, k_lo = sb("k_hi", [P, CT], F32R), sb("k_lo", [P, CT], F32R)
        v_hi, v_lo = sb("v_hi", [P, TILES, P], F32R), sb("v_lo", [P, TILES, P], F32R)
        p_hi, p_lo = sb("p_hi", [P, TILES * GROUP, 4, T], F32R), sb("p_lo", [P, TILES * GROUP, 4, T], F32R)
        o_hi, o_lo = sb("o_hi", [P, GROUP, CT], F32R), sb("o_lo", [P, GROUP, CT], F32R)
        h_hi, h_lo = sb("h_hi", [P, 3, CT], F32R), sb("h_lo", [P, 3, CT], F32R)
        x_res = sb("x_res", [P, KC, CT])
        y_acc = sb("y_acc", [P, KC + 1, CT])
        cos_t, sin_t = sb("cos_t", [P, CT]), sb("sin_t", [P, CT])
        own = sb("own", [P, CT])
        r_cos, r_sin = sb("r_cos", [P, 2, CT]), sb("r_sin", [P, 2, CT])
        roped = r_cos
        q2_f = r_cos[:, 0, :]
        odd_f, o2_f = r_sin[:, 0, :], r_sin[:, 1, :]
        h_f = sb("h_f", [P, 2, CT])
        v_f = h_f[:, 0, :]
        sT = sb("sT", [P, TILES * GROUP, T])
        sc = sb("sc", [P, TILES * GROUP, T])
        pT = sb("pT", [P, TILES * GROUP, T])
        pos_i = pT[:, :, :].rearrange("p a b -> p (a b)").bitcast(I32)
        idx_i = sc[:, :, :].rearrange("p a b -> p (a b)").bitcast(I32)
        s_max, s_sum, s_inv = (sb(n, [P, TILES * GROUP]) for n in ("s_max", "s_sum", "s_inv"))
        mask_u = sb("mask_u", [P, TILES, T], U8)
        mask_f = sb("mask_f", [P, TILES, T])
        cst = sb("cst", [P, C_COLS])
        ffn_b = sb("ffn_b", [P, KC])
        idx_ti = sb("idx_ti", [P, TILES], I32)
        idx_tf = sb("idx_tf", [P, TILES])
        lang = sb("lang", [P, TILES, E])
        rt = {n: sb("rt_" + n, [P, TILES, E]) for n in ("l", "eq", "one", "l2", "two", "gate")}
        rs = {n: sb("rs_" + n, [P, TILES]) for n in ("m1", "m2", "c", "d", "e", "s", "w1", "w2")}
        gate_x, gate_t = sT[:, :, :].rearrange("p a (e r) -> p (a e) r", e=2)\
            .rearrange("p (a e) r -> p a e r", a=TILES), pT[:, :, :].rearrange("p a b -> p (a b)")

        ring = [ctx.enter_context(nc.psum_tensor(f"ring{b}", [P, CT], F32)) for b in range(4)]
        att = ctx.enter_context(nc.psum_tensor("att", [P, TILES, CT], F32))

        ring_full = [sem(f"ring_full{b}") for b in range(4)]
        ring_free = [sem(f"ring_free{b}") for b in range(4)]
        raw_full = [sem(f"raw_full{r}") for r in range(RAWS)]
        raw_free = [sem(f"raw_free{r}") for r in range(RAWS)]
        w_hi_ok = [sem(f"w_hi_ok{s}") for s in range(SLOTS)]
        w_ok = [sem(f"w_ok{s}") for s in range(SLOTS)]
        ld_const, ld_x, ld_pos, ld_idx = (sem(n) for n in ("ld_const", "ld_x", "ld_pos", "ld_idx"))
        ld_mask, ld_tile, stored = (sem(n) for n in ("ld_mask", "ld_tile", "stored"))
        act_hi_ok = [sem(f"act_hi_ok{i}") for i in range(2)]
        act_ok = [sem(f"act_ok{i}") for i in range(2)]
        y_zero, table, zeroed, trig_ok = (sem(n) for n in ("y_zero", "table", "zeroed", "trig_ok"))
        h_f_ok, h_hi_ok, h_ok = (sem(n) for n in ("h_f_ok", "h_hi_ok", "h_ok"))
        rope_part, rope_sum, qk_hi_ok, qk_ok = (sem(n) for n in ("rope_part", "rope_sum", "qk_hi_ok", "qk_ok"))
        v_hi_ok, s_full, s_evac, smax, exp_ok = (sem(n) for n in ("v_hi_ok", "s_full", "s_evac", "smax", "exp_ok"))
        p_hi_ok, p_ok, pv_full, o_hi_ok, o_ok = (sem(n) for n in ("p_hi_ok", "p_ok", "pv_full", "o_hi_ok", "o_ok"))
        y_sum, x_sum = sem("y_sum"), sem("x_sum")
        q2_ok, k2_hi_ok, qx_hi_ok, qx_ok = (sem(n) for n in ("q2_ok", "k2_hi_ok", "qx_hi_ok", "qx_ok"))
        pv2_full, odd_ok, o2_ok, o2_hi_ok, o2_lo_ok = (sem(n) for n in ("pv2_full", "odd_ok", "o2_ok", "o2_hi_ok", "o2_lo_ok"))
        routing, gating, route_exp, gate_ok, base_full, f_sum = (sem(n) for n in ("routing", "gating", "route_exp", "gate_ok", "base_full", "f_sum"))

        ident = cst[:, C_IDENT:C_IDENT + P]
        QK = {"k": 0, "q0": 1, "q1": 2, "q2": 3, "q3": 4}

        def f(ap):
            return ap.bitcast(F32)

        def w_count(c, s, content):
            return c * CONTENTS[s] + (content + 1)

        def step_of(c, k):
            return c * KVH + k

        def soft(c, group):
            return c * 16 + group

        block = ctx.enter_context(nc.Block())

        @block.sync
        def _(sp):
            def load(c, part, j, slot, content, k=0):
                r, n = raw_use(c, part, j, k)
                sp.wait_ge(raw_free[r], n + PRIMED)
                src = stream[bass.ds(content + SLOT_BASE[slot], 1)].rearrange("o p n -> (o p) n")
                sp.dma_start(raw[r][:, :], src).then_inc(raw_full[r], 16)

            def load_head(c, part):
                for j, s in enumerate(HEAD_ORDER):
                    load(c, part, j, s, 0)

            sp.dma_start(cst[:, :], consts).then_inc(ld_const, 16)
            sp.dma_start(ffn_b[:, :], bias).then_inc(ld_const, 16)

            def load_chunk(c):
                sp.wait_ge(f_sum, c * KC + PRIMED)
                sp.dma_start(x_res[:, :, :].rearrange("p a t -> p (a t)"),
                             xT[bass.ds(c, 1)].rearrange("o p n -> (o p) n")).then_inc(ld_x, 16)
                for dst, src, s in ((idx_i, idx, ld_idx), (pos_i, pos, ld_pos)):
                    sp.dma_start(dst, src[bass.ds(c, 1)].rearrange("o p n -> (o p) n")).then_inc(s, 16)
                sp.dma_start(mask_u[:, :, :].rearrange("p a t -> p (a t)"),
                             mask[bass.ds(c, 1)].rearrange("o p n -> (o p) n")).then_inc(ld_mask, 16)
                sp.dma_start(idx_ti[:, :], idx_tile[bass.ds(c, 1)].rearrange("o p n -> (o p) n")).then_inc(ld_tile, 16)

            sp.sem_inc(stored, 16 * PRIMED)
            load_head(0, "prologue")
            with sp.Fori(0, CHUNKS) as c:
                load_chunk(c)

                def step(k):
                    for s in range(6):
                        load(c, "step", s, s, k + 1, k)
                    for s in range(6, SLOTS):
                        load(c, "step", s, s, k + WO_FIRST[s], k)

                step(0)
                with sp.Fori(1, KVH) as k:
                    step(k)
                for j, s in enumerate(EPI_ORDER):
                    load(c, "epi", j, s, KVH + WO_FIRST[s])
                with sp.Fori(0, KC) as hb:
                    for s in range(3):
                        load(c, "b", s, s, hb + QKV2_FIRST + 1, hb)
                for j, s in enumerate(MID_ORDER):
                    load(c, "mid", j, s, 9)
                load_head(c, "head")
                sp.wait_ge(f_sum, c * KC + KC + PRIMED)
                sp.dma_start(outT[bass.ds(c, 1)].rearrange("o p n -> (o p) n"),
                             y_acc[:, 0:KC, :].rearrange("p a t -> p (a t)")).then_inc(stored, 16)
            sp.wait_ge(stored, 16 * (CHUNKS + PRIMED))

        @block.tensor
        def _(pe):
            def three(out, w, x, start, stop):
                nc.tensor.matmul(out, w[0], x[0], start=start, stop=False)
                nc.tensor.matmul(out, w[1], x[0], start=False, stop=False)
                return nc.tensor.matmul(out, w[0], x[1], start=False, stop=stop)

            def w(s, a, n=P):
                return w_hi_t[s][:, a:a + n], w_lo_t[s][:, a:a + n]

            def open_bank(use):
                b, n = use
                pe.wait_ge(ring_free[b], n + PRIMED)
                return ring[b]

            def weights(c, s, content):
                pe.wait_ge(w_ok[s], w_count(c, s, content))

            def block_of(out, s, x, first=0, start=True, stop=True, n=KC):
                for a in range(n):
                    last = three(out, w(s, (first + a) * P), (x[0][:, a, :], x[1][:, a, :]),
                                 start and a == 0, stop and a == n - 1)
                return last

            def scores_and(kh, kl, count):
                for t in range(TILES):
                    cols = slice(t * P, (t + 1) * P)
                    last = three(att[:, t, :], (kh[:, cols], kl[:, cols]),
                                 (q_hi[:, :, cols], q_lo[:, :, cols]), True, True)
                last.then_inc(s_full, 1)

            def values(t):
                cols = slice(t * GROUP, (t + 1) * GROUP)
                return three(att[:, t, :], (v_hi[:, t, :], v_lo[:, t, :]),
                             (p_hi[:, cols, :, :], p_lo[:, cols, :, :]), True, True)

            def turn_v(use):
                out = open_bank(use)
                for t in range(TILES):
                    last = nc.tensor.transpose(out[:, t * P:(t + 1) * P], v_f[:, t * P:(t + 1) * P], ident)
                last.then_inc(ring_full[use[0]], 1)

            def wo_block(c, k, name):
                j = int(name[1]) if name != "ho" else 4
                s = 6 + j
                use = ring_use(c, "wo", name, k)
                out = open_bank(use)
                weights(c, s, k - 1 + WO_FIRST[s])
                block_of(out[:, :], s, (o_hi, o_lo)).then_inc(ring_full[use[0]], 1)

            def pv(c, k):
                pe.wait_ge(p_ok, soft(c, k) * 4)
                pe.wait_ge(s_evac, soft(c, k))
                b, n = ring_use(c, "proj", "vT", k - 1)
                pe.wait_ge(ring_free[b], n + 1 + PRIMED)
                for t in range(TILES):
                    values(t).then_inc(pv_full, 1)

            pe.wait_ge(ld_const, 32)
            pe.wait_ge(zeroed, 2)
            with pe.Fori(0, CHUNKS) as c:
                pe.wait_ge(act_ok[0], c * 8 + KC)
                for j, s in enumerate(LORA_A_SLOTS):
                    use = ring_use(c, "lora", j)
                    out = open_bank(use)
                    weights(c, s, 0)
                    block_of(out[:, :], s, (act_hi[0], act_lo[0])).then_inc(ring_full[use[0]], 1)
                pe.wait_ge(h_ok, c * 6 + 3)

                def proj(k, name, slot, lora):
                    use = ring_use(c, "proj", name, k)
                    out = open_bank(use)
                    weights(c, slot, k)
                    block_of(out[:, :], slot, (act_hi[0], act_lo[0]), stop=False)
                    three(out[:, :], w(slot, KC * P), (h_hi[:, lora, :], h_lo[:, lora, :]),
                          False, True).then_inc(ring_full[use[0]], 1)

                def step(k, first=False):
                    proj(k, "k", 0, 1)
                    proj(k, "v", 1, 2)
                    proj(k, "q0", 2, 0)
                    proj(k, "q1", 3, 0)
                    if not first:
                        pv(c, k)
                    proj(k, "q2", 4, 0)
                    proj(k, "q3", 5, 0)
                    b, n = ring_use(c, "proj", "v", k)
                    pe.wait_ge(ring_free[b], n + 1 + PRIMED)
                    turn_v(ring_use(c, "proj", "vT", k))
                    if not first:
                        pe.wait_ge(o_ok, (step_of(c, k)) * TILES)
                        wo_block(c, k, "y0")
                        wo_block(c, k, "y1")
                    pe.wait_ge(qk_ok, step_of(c, k) * 5 + 5)
                    scores_and(k_hi, k_lo, None)
                    if not first:
                        wo_block(c, k, "y2")
                        wo_block(c, k, "y3")
                        wo_block(c, k, "ho")

                step(0, True)
                with pe.Fori(1, KVH) as k:
                    step(k)
                pv(c, KVH)
                pe.wait_ge(o_ok, (step_of(c, KVH)) * TILES)
                for name in WOUT:
                    wo_block(c, KVH, name)

                pe.wait_ge(h_ok, c * 6 + 4)
                s, content = BO_PIECE
                weights(c, s, content)
                for j in range(KC):
                    use = ring_use(c, "bo", j)
                    out = open_bank(use)
                    three(out[:, :], w(s, j * P), (h_hi[:, 0, :], h_lo[:, 0, :]), True, True)\
                        .then_inc(ring_full[use[0]], 1)

                with pe.Fori(0, KC) as hb:
                    pe.wait_ge(act_ok[1], c * 8 + KC)
                    for s in range(3):
                        use = ring_use(c, "b", s, hb)
                        out = open_bank(use)
                        weights(c, s, hb + QKV2_FIRST)
                        block_of(out[:, :], s, (act_hi[1], act_lo[1])).then_inc(ring_full[use[0]], 1)
                    b, n = ring_use(c, "b", 2, hb)
                    pe.wait_ge(ring_free[b], n + 1 + PRIMED)
                    turn_v(ring_use(c, "b", 3, hb))
                    b, n = ring_use(c, "b", 1, hb)
                    pe.wait_ge(ring_free[b], n + 1 + PRIMED)
                    quad = (c * KC + hb) * 2
                    for q in range(2):
                        pe.wait_ge(qx_ok, quad + q + 1)
                        if q:
                            pe.wait_ge(s_evac, soft(c, hb * 2 + 8 + q))
                        scores_and(k_hi, k_lo, None)
                    b, n = ring_use(c, "b", 3, hb)
                    pe.wait_ge(ring_free[b], n + 1 + PRIMED)
                    for q in range(2):
                        pe.wait_ge(p_ok, soft(c, hb * 2 + 9 + q) * 4)
                        pe.wait_ge(s_evac, soft(c, hb * 2 + 10))
                        if q:
                            pe.wait_ge(o2_ok, (quad + q) * 2)
                        for t in range(TILES):
                            last = values(t)
                        last.then_inc(pv2_full, 1)
                    pe.wait_ge(o2_ok, (quad + 2) * 2)
                pe.wait_ge(o2_lo_ok, (c + 1) * KC + PRIMED)
                for j, (s, content) in enumerate(OUT2_PIECES):
                    use = ring_use(c, "out2", j)
                    out = open_bank(use)
                    weights(c, s, content)
                    block_of(out[:, :], s, (o_hi, o_lo)).then_inc(ring_full[use[0]], 1)

                for layer, ((sa, ca), pieces) in enumerate(ROUTED):
                    xh, xl = act_hi[layer], act_lo[layer]
                    pe.wait_ge(act_ok[layer], c * 8 + 8)
                    weights(c, sa, ca)
                    use = ring_use(c, "route", 0, layer)
                    out = open_bank(use)
                    for t in range(TILES):
                        cols = slice(t * P, (t + 1) * P)
                        for a in range(KC):
                            last = three(out[:, t * E:(t + 1) * E], (xh[:, a, cols], xl[:, a, cols]),
                                         w(sa, KC * P + a * E, E), a == 0, a == KC - 1)
                    last.then_inc(ring_full[use[0]], 1)
                    use = ring_use(c, "route", 1, layer)
                    out = open_bank(use)
                    block_of(out[:, :], sa, (xh, xl)).then_inc(ring_full[use[0]], 1)
                    for j, (s, content) in enumerate(pieces):
                        weights(c, s, content)
                        block_of(att[:, j, :], s, (xh, xl), stop=False)
                    use = ring_use(c, "route", 2, layer)
                    out = open_bank(use)
                    pe.wait_ge(gate_ok, c * 2 + layer + 1)
                    for t in range(TILES):
                        last = nc.tensor.transpose(out[:, t * P:(t + 1) * P],
                                                   gate_x[:, t, :, :].rearrange("p e r -> p (e r)"), ident)
                    last.then_inc(ring_full[use[0]], 1)
                    pe.wait_ge(h_ok, c * 6 + 5 + layer)
                    for j, (s, content) in enumerate(pieces):
                        three(att[:, j, :], w(s, KC * P), (h_hi[:, 1 + layer, :], h_lo[:, 1 + layer, :]),
                              False, True).then_inc(base_full, 1)

        @block.scalar
        def _(act):
            def copy(out, in_, scale=1.0):
                return nc.scalar.activation(out, in_, ACT.Copy, scale=scale)

            def split(c, part, j, slot, content, k=0):
                r, n = raw_use(c, part, j, k)
                act.wait_ge(raw_full[r], (n + 1) * 16)
                copy(w_hi_t[slot][:, :], raw[r][:, :]).then_inc(w_hi_ok[slot], 1)

            def split_head(c, part, which):
                for j, s in enumerate(HEAD_ORDER):
                    if s in which:
                        split(c, part, j, s, 0)

            def full(use):
                act.wait_ge(ring_full[use[0]], use[1] + 1)
                return ring[use[0]]

            def hidden(c, fill, at):
                act.wait_ge(h_f_ok, c * 6 + fill + 1)
                copy(h_hi[:, at, :], h_f[:, fill % 2, :]).then_inc(h_hi_ok, 1)

            def turned_v(use):
                out = full(use)
                copy(v_hi[:, :, :], out[:, :].rearrange("p (t d) -> p t d", t=TILES)).then_inc(v_hi_ok, 1)

            def scores_out(group, scale):
                act.wait_ge(s_full, group + 1)
                for b in range(4):
                    rows = slice(T * b, T * b + T)
                    src = att[rows, :, :].rearrange("p a (g t) -> p (a g) t", g=GROUP)[:, :, T * b:T * b + T]
                    last = copy(sT[rows, :, :], src, scale)
                last.then_inc(s_evac, 1)

            def exponent(group):
                act.wait_ge(smax, group * 8 + 4)
                nc.scalar.activation(sc[:, :, :], sc[:, :, :], ACT.Exp).then_inc(exp_ok, 1)

            def probs_hi(group):
                act.wait_ge(smax, group * 8 + 8)
                for b in range(4):
                    rows = slice(T * b, T * b + T)
                    last = copy(p_hi[rows, :, b, :], pT[rows, :, :])
                last.then_inc(p_hi_ok, 1)

            split_head(0, "prologue", HEAD_ORDER)
            act.wait_ge(ld_const, 32)
            act.wait_ge(zeroed, 2)
            with act.Fori(0, CHUNKS) as c:
                act.wait_ge(ld_x, (c + 1) * 16)
                for a in range(KC):
                    copy(act_hi[0][:, a, :], x_res[:, a, :]).then_inc(act_hi_ok[0], 1)
                act.wait_ge(table, c * N_TABLE + N_TABLE)
                nc.scalar.activation(sin_t[:, :], r_sin[:, 0, :], ACT.Sin, scale=cst[:, C_SIGN:C_SIGN + 1])\
                    .then_inc(trig_ok, 1)
                nc.scalar.activation(cos_t[:, :], r_sin[:, 1, :], ACT.Sin).then_inc(trig_ok, 1)
                for j in range(3):
                    hidden(c, j, j)

                def attention_out(k):
                    for t in range(TILES):
                        act.wait_ge(pv_full, step_of(c, k - 1) * TILES + t + 1)
                        copy(o_hi[:, :, t * P:(t + 1) * P],
                             att[:, t, :].rearrange("p (g n) -> p g n", g=GROUP)).then_inc(o_hi_ok, 1)

                def qk_out(k, name, dst):
                    act.wait_ge(rope_sum, step_of(c, k) * 5 + QK[name] + 1)
                    copy(dst, roped[:, QK[name] % 2, :]).then_inc(qk_hi_ok, 1)

                def step(k, first=False):
                    qk_out(k, "k", k_hi[:, :])
                    split(c, "step", 0, 0, k + 1, k)
                    use = ring_use(c, "proj", "v", k)
                    copy(v_f, full(use)[:, :]).then_inc(ring_free[use[0]], 1)
                    split(c, "step", 1, 1, k + 1, k)
                    qk_out(k, "q0", q_hi[:, 0, :])
                    split(c, "step", 2, 2, k + 1, k)
                    qk_out(k, "q1", q_hi[:, 1, :])
                    if not first:
                        attention_out(k)
                    split(c, "step", 3, 3, k + 1, k)
                    qk_out(k, "q2", q_hi[:, 2, :])
                    split(c, "step", 4, 4, k + 1, k)
                    qk_out(k, "q3", q_hi[:, 3, :])
                    turned_v(ring_use(c, "proj", "vT", k))
                    split(c, "step", 5, 5, k + 1, k)
                    for j, s in ((0, 6), (1, 7)):
                        if not first:
                            full(ring_use(c, "wo", f"y{j}", k))
                        split(c, "step", s, s, None, k)
                    group = soft(c, k)
                    scores_out(group, HD ** -0.5)
                    exponent(group)
                    for j, s in ((2, 8), (3, 9)):
                        if not first:
                            full(ring_use(c, "wo", f"y{j}", k))
                        split(c, "step", s, s, None, k)
                    probs_hi(group)
                    if not first:
                        full(ring_use(c, "wo", "ho", k))
                    split(c, "step", 10, 10, None, k)

                step(0, True)
                with act.Fori(1, KVH) as k:
                    step(k)
                attention_out(KVH)
                for j, name in enumerate(WOUT):
                    full(ring_use(c, "wo", name, KVH))
                    split(c, "epi", j, EPI_ORDER[j], None)

                hidden(c, 3, 0)
                for j in range(KC):
                    act.wait_ge(y_sum, c * KC + j + 1)
                    copy(act_hi[1][:, j, :], y_acc[:, j, :]).then_inc(act_hi_ok[1], 1)

                with act.Fori(0, KC) as hb:
                    use = ring_use(c, "b", 0, hb)
                    copy(q2_f, full(use)[:, :]).then_inc(ring_free[use[0]], 1)
                    split(c, "b", 0, 0, None, hb)
                    act.wait_ge(ring_free[use[0]], use[1] + 1 + PRIMED)
                    quad = (c * KC + hb) * 2
                    use = ring_use(c, "b", 1, hb)
                    copy(k_hi[:, :], full(use)[:, :]).then_inc(k2_hi_ok, 1)
                    split(c, "b", 1, 1, None, hb)

                    def spread(q):
                        for h in range(GROUP):
                            col = C_HM + GROUP * q + h
                            last = copy(q_hi[:, h, :], q2_f, cst[:, col:col + 1])
                        last.then_inc(qx_hi_ok, 1)

                    spread(0)
                    use = ring_use(c, "b", 2, hb)
                    copy(v_f, full(use)[:, :]).then_inc(ring_free[use[0]], 1)
                    split(c, "b", 2, 2, None, hb)
                    turned_v(ring_use(c, "b", 3, hb))
                    group = soft(c, hb * 2 + 8)
                    scores_out(group, HD2 ** -0.5)
                    spread(1)
                    exponent(group)
                    probs_hi(group)
                    scores_out(group + 1, HD2 ** -0.5)
                    exponent(group + 1)
                    for q in range(2):
                        act.wait_ge(pv2_full, quad + q + 1)
                        if q == 0:
                            probs_hi(group + 1)
                        for j in range(2):
                            rows = slice(64 * q + 32 * j, 64 * q + 32 * j + 32)
                            src = att[rows, :, (2 * j + 1) * P:(2 * j + 2) * P]
                            copy(odd_f[rows, :].rearrange("p (a n) -> p a n", a=TILES), src,
                                 cst[rows, C_ODD:C_ODD + 1]).then_inc(odd_ok, 1)
                    act.wait_ge(o2_ok, (quad + 2) * 2)
                    copy(o_hi[:, bass.ds(hb, 1), :], o2_f.unsqueeze(1)).then_inc(o2_hi_ok, 1)

                for j in range(KC):
                    act.wait_ge(x_sum, c * KC + j + 1)
                    copy(act_hi[0][:, j, :], x_res[:, j, :]).then_inc(act_hi_ok[0], 1)
                for j, s in enumerate(MID_ORDER):
                    split(c, "mid", j, s, None)

                def routed(layer):
                    act.wait_ge(routing, (c * 2 + layer) * N_ROUTING + 12)
                    nc.scalar.activation(rs["e"][:, :], rs["d"][:, :], ACT.Exp).then_inc(route_exp, 1)
                    use = ring_use(c, "route", 2, layer)
                    copy(gate_t, full(use)[:, :]).then_inc(ring_free[use[0]], 1)
                    hidden(c, 4 + layer, 1 + layer)

                routed(0)
                for j in range(KC):
                    act.wait_ge(base_full, c * 8 + j + 1)
                    copy(act_hi[1][:, j, :], att[:, j, :]).then_inc(act_hi_ok[1], 1)
                split_head(c, "head", HEAD_ORDER[:5])
                routed(1)
                act.wait_ge(base_full, c * 8 + 8)
                split_head(c, "head", HEAD_ORDER[5:])

        @block.vector
        def _(dve):
            tt, ts, stt = nc.vector.tensor_tensor, nc.vector.tensor_scalar, nc.vector.scalar_tensor_tensor

            def full(use):
                dve.wait_ge(ring_full[use[0]], use[1] + 1)
                return ring[use[0]]

            def softmax_first(group, masked):
                chain = Chain(dve, smax, group * 8)
                dve.wait_ge(s_evac, group + 1)
                nc.vector.transpose(sc[:, :, :], sT[:, :, :]).then_inc(smax, 1 if masked else 2)
                dve.wait_ge(smax, group * 8 + (1 if masked else 2))
                chain.n = 1 if masked else 2
                if masked:
                    s4 = sc[:, :, :].rearrange("p (a g) s -> p a g s", a=TILES)
                    chain.then(tt(s4, s4, mask_f[:, :, :].unsqueeze(2).to_broadcast([P, TILES, GROUP, T]), ALU.add))
                chain.then(nc.vector.tensor_reduce(s_max[:, :], sc[:, :, :], AX.X, ALU.max))
                tt(sc[:, :, :], sc[:, :, :], s_max[:, :].unsqueeze(2).to_broadcast([P, TILES * GROUP, T]),
                   ALU.subtract).then_inc(smax, 1)

            def softmax_second(group):
                chain = Chain(dve, smax, group * 8 + 4)
                dve.wait_ge(exp_ok, group + 1)
                chain.then(nc.vector.tensor_reduce(s_sum[:, :], sc[:, :, :], AX.X, ALU.add))
                chain.then(nc.vector.reciprocal(s_inv[:, :], s_sum[:, :]))
                chain.then(tt(sc[:, :, :], sc[:, :, :], s_inv[:, :].unsqueeze(2).to_broadcast([P, TILES * GROUP, T]),
                              ALU.mult))
                nc.vector.transpose(pT[:, :, :], sc[:, :, :]).then_inc(smax, 1)

            def own_hidden(c, fill, src, gate, freed):
                if fill >= 2:
                    dve.wait_ge(h_ok, c * 6 + fill - 1)
                ins = tt(h_f[:, fill % 2, :], src, gate, ALU.mult)
                ins.then_inc(h_f_ok, 1)
                if freed is not None:
                    dve.wait_ge(h_f_ok, c * 6 + fill + 1)
                    dve.sem_inc(ring_free[freed], 1)

            for primed in ring_free + [f_sum]:
                dve.sem_inc(primed, PRIMED)
            for part in (p_hi, p_lo):
                nc.vector.memset(f(part[:, :, :, :]), 0.0).then_inc(zeroed, 1)
            dve.wait_ge(ld_const, 32)
            with dve.Fori(0, CHUNKS) as c:
                for a in range(KC):
                    dve.wait_ge(act_hi_ok[0], c * 8 + a + 1)
                    tt(act_lo[0][:, a, :], x_res[:, a, :], f(act_hi[0][:, a, :]), ALU.subtract).then_inc(act_ok[0], 1)
                chain = Chain(dve, table, c * N_TABLE)
                dve.wait_ge(ld_idx, (c + 1) * 16)
                chain.then(ts(own[:, :], idx_i, cst[:, C_EID:C_EID + 1], None, ALU.is_equal))
                dve.wait_ge(ld_pos, (c + 1) * 16)
                ang, turns, cosa = r_cos[:, 0, :], r_cos[:, 1, :], r_sin[:, 1, :]
                chain.then(ts(ang, pos_i, cst[:, C_FREQ:C_FREQ + 1], None, ALU.mult))
                chain.then(ts(turns, ang, 1 / TWO_PI, ROUND, ALU.mult, ALU.add))
                chain.then(ts(turns, turns, -ROUND, None, ALU.add))
                for part in (PI_A, PI_B, PI_C):
                    chain.then(stt(out=ang, in0=turns, scalar=-part, in1=ang, op0=ALU.mult, op1=ALU.add))
                chain.then(ts(r_sin[:, 0, :], ang, PI_IN, -PI_IN, ALU.min, ALU.max))
                chain.then(ts(ang, ang, float(np.pi / 2), None, ALU.add))
                chain.then(ts(turns, ang, float(np.pi), -TWO_PI, ALU.is_gt, ALU.mult))
                chain.then(tt(ang, ang, turns, ALU.add))
                dve.wait_ge(ld_mask, (c + 1) * 16)
                causal = cst[:, C_CAUSAL:C_CAUSAL + T].unsqueeze(1).to_broadcast([P, TILES, T])
                chain.then(tt(mask_f[:, :, :], mask_u[:, :, :], causal, ALU.mult))
                chain.then(ts(mask_f[:, :, :], mask_f[:, :, :], -1.0, FLT_MAX, ALU.add, ALU.mult))
                dve.wait_ge(ld_tile, (c + 1) * 16)
                chain.then(nc.vector.tensor_copy(idx_tf[:, :], idx_ti[:, :]))
                chain.then(tt(lang[:, :, :], cst[:, C_E:C_E + E].unsqueeze(1).to_broadcast([P, TILES, E]),
                              idx_tf[:, :].unsqueeze(2).to_broadcast([P, TILES, E]), ALU.is_equal))
                chain.then(ts(cosa, ang, PI_IN, -PI_IN, ALU.min, ALU.max))
                assert chain.n == N_TABLE
                dve.wait_ge(stored, (c + PRIMED) * 16)
                nc.vector.memset(y_acc[:, :, :], 0.0).then_inc(y_zero, 1)
                for j in range(3):
                    b, _ = use = ring_use(c, "lora", j)
                    own_hidden(c, j, full(use)[:, :], own[:, :], b)
                dve.wait_ge(trig_ok, c * 2 + 2)

                def rope(k, name):
                    at = step_of(c, k) * 5 + QK[name]
                    half = QK[name] % 2
                    use = ring_use(c, "proj", name, k)
                    src = full(use)
                    if QK[name] >= 2:
                        dve.wait_ge(qk_ok, at - 1)
                    elif QK[name] == 1:
                        if not (isinstance(k, int) and k == 0):
                            dve.wait_ge(qk_ok, at - 1)
                    elif not (isinstance(k, int) and k == 0):
                        dve.wait_ge(qk_ok, at)
                    tt(r_cos[:, half, :], src[:, :], cos_t[:, :], ALU.mult).then_inc(rope_part, 1)
                    tt(r_sin[0:64, half, :], src[64:128, :], sin_t[0:64, :], ALU.mult).then_inc(rope_part, 1)
                    tt(r_sin[64:128, half, :], src[0:64, :], sin_t[64:128, :], ALU.mult).then_inc(ring_free[use[0]], 1)
                    dve.wait_ge(rope_part, at * 2 + 2)
                    dve.wait_ge(ring_free[use[0]], use[1] + 1 + PRIMED)
                    tt(roped[:, half, :], r_cos[:, half, :], r_sin[:, half, :], ALU.add).then_inc(rope_sum, 1)

                def attention_lo(k):
                    for t in range(TILES):
                        dve.wait_ge(o_hi_ok, step_of(c, k - 1) * TILES + t + 1)
                        cols = slice(t * P, (t + 1) * P)
                        tt(o_lo[:, :, cols], att[:, t, :].rearrange("p (g n) -> p g n", g=GROUP),
                           f(o_hi[:, :, cols]), ALU.subtract).then_inc(o_ok, 1)

                def add_y(k, name):
                    j = 4 if name == "ho" else int(name[1])
                    use = ring_use(c, "wo", name, k)
                    src = full(use)
                    tt(y_acc[:, j, :], src[:, :], y_acc[:, j, :], ALU.add).then_inc(ring_free[use[0]], 1)

                def turned_v_lo(use, count):
                    dve.wait_ge(v_hi_ok, count)
                    src = ring[use[0]][:, :].rearrange("p (t d) -> p t d", t=TILES)
                    tt(v_lo[:, :, :], src, f(v_hi[:, :, :]), ALU.subtract).then_inc(ring_free[use[0]], 1)

                def step(k, first=False):
                    group = soft(c, k)
                    rope(k, "k")
                    rope(k, "q0")
                    rope(k, "q1")
                    if not first:
                        attention_lo(k)
                    rope(k, "q2")
                    rope(k, "q3")
                    turned_v_lo(ring_use(c, "proj", "vT", k), c * (KVH + KC) + k + 1)
                    if not first:
                        add_y(k, "y0")
                        add_y(k, "y1")
                    softmax_first(group, True)
                    if not first:
                        add_y(k, "y2")
                    softmax_second(group)
                    if not first:
                        add_y(k, "y3")
                        add_y(k, "ho")

                dve.wait_ge(y_zero, c + 1)
                step(0, True)
                with dve.Fori(1, KVH) as k:
                    step(k)
                attention_lo(KVH)
                for name in WOUT:
                    add_y(KVH, name)
                b, n = ring_use(c, "wo", "ho", KVH)
                dve.wait_ge(ring_free[b], n + 1 + PRIMED)
                own_hidden(c, 3, y_acc[:, KC, :], own[:, :], None)
                for j in range(KC):
                    use = ring_use(c, "bo", j)
                    tt(y_acc[:, j, :], full(use)[:, :], y_acc[:, j, :], ALU.add).then_inc(ring_free[use[0]], 1)
                    dve.wait_ge(ring_free[use[0]], use[1] + 1 + PRIMED)
                    dve.sem_inc(y_sum, 1)

                with dve.Fori(0, KC) as hb:
                    quad = (c * KC + hb) * 2
                    use = ring_use(c, "b", 1, hb)
                    dve.wait_ge(k2_hi_ok, c * KC + hb + 1)
                    tt(k_lo[:, :], ring[use[0]][:, :], f(k_hi[:, :]), ALU.subtract).then_inc(ring_free[use[0]], 1)

                    def spread_lo(q):
                        dve.wait_ge(qx_hi_ok, quad + q + 1)
                        for h in range(GROUP):
                            col = C_HM + GROUP * q + h
                            last = stt(out=q_lo[:, h, :], in0=q2_f, scalar=cst[:, col:col + 1],
                                       in1=f(q_hi[:, h, :]), op0=ALU.mult, op1=ALU.subtract)
                        last.then_inc(qx_ok, 1)

                    spread_lo(0)
                    turned_v_lo(ring_use(c, "b", 3, hb), c * (KVH + KC) + hb + KVH + 1)
                    group = soft(c, hb * 2 + 8)
                    softmax_first(group, False)
                    spread_lo(1)
                    softmax_second(group)
                    softmax_first(group + 1, False)

                    def extract(q):
                        for j in range(2):
                            rows = slice(64 * q + 32 * j, 64 * q + 32 * j + 32)
                            dve.wait_ge(odd_ok, (quad + q) * 2 + j + 1)
                            stt(out=o2_f[rows, :].rearrange("p (a n) -> p a n", a=TILES),
                                in0=att[rows, :, 2 * j * P:(2 * j + 1) * P], scalar=cst[rows, C_EVEN:C_EVEN + 1],
                                in1=odd_f[rows, :].rearrange("p (a n) -> p a n", a=TILES),
                                op0=ALU.mult, op1=ALU.add).then_inc(o2_ok, 1)

                    dve.wait_ge(p_ok, group * 4 + 4)
                    softmax_second(group + 1)
                    dve.wait_ge(o2_lo_ok, c * KC + hb + PRIMED)
                    extract(0)
                    extract(1)

                for j in range(KC):
                    use = ring_use(c, "out2", j)
                    tt(x_res[:, j, :], full(use)[:, :], x_res[:, j, :], ALU.add).then_inc(ring_free[use[0]], 1)
                    dve.wait_ge(ring_free[use[0]], use[1] + 1 + PRIMED)
                    dve.sem_inc(x_sum, 1)

                def routed(layer):
                    chain = Chain(dve, routing, (c * 2 + layer) * N_ROUTING)
                    use = ring_use(c, "route", 0, layer)
                    src = full(use)[:, 0:TILES * E].rearrange("p (a e) -> p a e", a=TILES)

                    def wide(ap):
                        return ap[:, :].unsqueeze(2).to_broadcast([P, TILES, E])

                    tie = cst[:, C_TIE:C_TIE + E].unsqueeze(1).to_broadcast([P, TILES, E])
                    if layer == 0:
                        ins = stt(out=rt["l"][:, :, :], in0=lang[:, :, :], scalar=LANG_BIAS, in1=src,
                                  op0=ALU.mult, op1=ALU.add)
                    else:
                        ins = nc.vector.tensor_copy(rt["l"][:, :, :], src)
                    chain.then(ins)
                    dve.sem_inc(ring_free[use[0]], 1)

                    def largest(logits, m, chosen):
                        chain.then(nc.vector.tensor_reduce(rs[m][:, :], logits[:, :, :], AX.X, ALU.max))
                        chain.then(tt(rt["eq"][:, :, :], logits[:, :, :], wide(rs[m]), ALU.is_equal))
                        chain.then(tt(rt["eq"][:, :, :], rt["eq"][:, :, :], tie, ALU.mult))
                        chain.then(nc.vector.tensor_reduce(rs["c"][:, :], rt["eq"][:, :, :], AX.X, ALU.max))
                        chain.then(tt(rt[chosen][:, :, :], tie, wide(rs["c"]), ALU.is_equal))

                    largest(rt["l"], "m1", "one")
                    chain.then(stt(out=rt["l2"][:, :, :], in0=rt["one"][:, :, :], scalar=-3e38,
                                   in1=rt["l"][:, :, :], op0=ALU.mult, op1=ALU.add))
                    chain.then(nc.vector.tensor_reduce(rs["m2"][:, :], rt["l2"][:, :, :], AX.X, ALU.max))
                    chain.then(tt(rt["eq"][:, :, :], rt["l2"][:, :, :], wide(rs["m2"]), ALU.is_equal))
                    chain.then(tt(rt["eq"][:, :, :], rt["eq"][:, :, :], tie, ALU.mult))
                    chain.then(nc.vector.tensor_reduce(rs["c"][:, :], rt["eq"][:, :, :], AX.X, ALU.max))
                    chain.then(tt(rs["d"][:, :], rs["m2"][:, :], rs["m1"][:, :], ALU.subtract))
                    assert chain.n == 12
                    chain.then(tt(rt["two"][:, :, :], tie, wide(rs["c"]), ALU.is_equal))
                    dve.wait_ge(route_exp, c * 2 + layer + 1)
                    chain.then(ts(rs["s"][:, :], rs["e"][:, :], 1.0, None, ALU.add))
                    chain.then(nc.vector.reciprocal(rs["w1"][:, :], rs["s"][:, :]))
                    chain.then(stt(out=rs["w2"][:, :], in0=rs["e"][:, :], scalar=SCALING, in1=rs["w1"][:, :],
                                   op0=ALU.mult, op1=ALU.mult))
                    chain.then(ts(rs["w1"][:, :], rs["w1"][:, :], SCALING, None, ALU.mult))
                    assert chain.n == N_ROUTING
                    gate_chain = Chain(dve, gating, (c * 2 + layer) * 3)
                    gate_chain.then(tt(rt["one"][:, :, :], rt["one"][:, :, :], wide(rs["w1"]), ALU.mult))
                    gate_chain.then(tt(rt["two"][:, :, :], rt["two"][:, :, :], wide(rs["w2"]), ALU.mult))
                    gate_chain.then(tt(rt["gate"][:, :, :], rt["one"][:, :, :], rt["two"][:, :, :], ALU.add))
                    nc.vector.tensor_copy(gate_x[:, :, :, :], rt["gate"][:, :, :].unsqueeze(3)
                                          .to_broadcast([P, TILES, E, R])).then_inc(gate_ok, 1)
                    b, n = ring_use(c, "route", 2, layer)
                    dve.wait_ge(ring_free[b], n + 1 + PRIMED)
                    use = ring_use(c, "route", 1, layer)
                    own_hidden(c, 4 + layer, full(use)[:, :], gate_t, use[0])

                routed(0)
                for j in range(KC):
                    dve.wait_ge(act_hi_ok[1], c * 8 + KC + j + 1)
                    tt(act_lo[1][:, j, :], att[:, j, :], f(act_hi[1][:, j, :]), ALU.subtract).then_inc(act_ok[1], 1)
                routed(1)
                for j in range(KC):
                    dve.wait_ge(base_full, c * 8 + KC + j + 1)
                    stt(out=y_acc[:, j, :], in0=att[:, j, :], scalar=ffn_b[:, j:j + 1], in1=x_res[:, j, :],
                        op0=ALU.add, op1=ALU.add).then_inc(f_sum, 1)

        @block.gpsimd
        def _(pool):
            def lo(out, whole, hi):
                return nc.gpsimd.tensor_tensor(out, whole, f(hi), ALU.subtract)

            def split(c, part, j, slot, content, k=0):
                r, n = raw_use(c, part, j, k)
                pool.wait_ge(w_hi_ok[slot], w_count(c, slot, content))
                lo(w_lo_t[slot][:, :], raw[r][:, :], w_hi_t[slot][:, :]).then_inc(w_ok[slot], 1)
                pool.wait_ge(w_ok[slot], w_count(c, slot, content))
                pool.sem_inc(raw_free[r], 1)

            def split_head(c, part, which, of):
                for j, s in enumerate(HEAD_ORDER):
                    if s in which:
                        split(c, part, j, s, CONTENTS[s] * of)

            def hidden(c, fill, at):
                pool.wait_ge(h_hi_ok, c * 6 + fill + 1)
                lo(h_lo[:, at, :], h_f[:, fill % 2, :], h_hi[:, at, :]).then_inc(h_ok, 1)

            def probs_lo(group):
                pool.wait_ge(p_hi_ok, group + 1)
                for b in range(4):
                    rows = slice(T * b, T * b + T)
                    lo(p_lo[rows, :, b, :], pT[rows, :, :], p_hi[rows, :, b, :]).then_inc(p_ok, 1)
                pool.wait_ge(p_ok, group * 4 + 4)

            for primed in raw_free + [o2_lo_ok]:
                pool.sem_inc(primed, PRIMED)
            split_head(0, "prologue", HEAD_ORDER, 0)
            pool.wait_ge(zeroed, 2)
            with pool.Fori(0, CHUNKS) as c:
                for j in range(3):
                    hidden(c, j, j)

                def step(k):
                    def qk_lo(name, dst, hi):
                        pool.wait_ge(qk_hi_ok, step_of(c, k) * 5 + QK[name] + 1)
                        lo(dst, roped[:, QK[name] % 2, :], hi).then_inc(qk_ok, 1)

                    qk_lo("k", k_lo[:, :], k_hi[:, :])
                    split(c, "step", 0, 0, k + 1, k)
                    split(c, "step", 1, 1, k + 1, k)
                    for g in range(GROUP):
                        qk_lo(f"q{g}", q_lo[:, g, :], q_hi[:, g, :])
                        split(c, "step", 2 + g, 2 + g, k + 1, k)
                    for s in (6, 7, 8, 9):
                        split(c, "step", s, s, k + WO_FIRST[s], k)
                    probs_lo(soft(c, k))
                    split(c, "step", 10, 10, k + WO_FIRST[10], k)

                step(0)
                with pool.Fori(1, KVH) as k:
                    step(k)
                for j, s in enumerate(EPI_ORDER):
                    split(c, "epi", j, s, KVH + WO_FIRST[s])
                hidden(c, 3, 0)
                for j in range(KC):
                    pool.wait_ge(act_hi_ok[1], c * 8 + j + 1)
                    lo(act_lo[1][:, j, :], y_acc[:, j, :], act_hi[1][:, j, :]).then_inc(act_ok[1], 1)
                with pool.Fori(0, KC) as hb:
                    for s in range(3):
                        split(c, "b", s, s, hb + QKV2_FIRST + 1, hb)
                    probs_lo(soft(c, hb * 2 + 8))
                    probs_lo(soft(c, hb * 2 + 9))
                    pool.wait_ge(o2_hi_ok, c * KC + hb + 1)
                    lo(o_lo[:, bass.ds(hb, 1), :], o2_f.unsqueeze(1), o_hi[:, bass.ds(hb, 1), :]).then_inc(o2_lo_ok, 1)
                for j in range(KC):
                    pool.wait_ge(act_hi_ok[0], c * 8 + KC + j + 1)
                    lo(act_lo[0][:, j, :], x_res[:, j, :], act_hi[0][:, j, :]).then_inc(act_ok[0], 1)
                for j, s in enumerate(MID_ORDER):
                    split(c, "mid", j, s, 9)
                hidden(c, 4, 1)
                split_head(c, "head", HEAD_ORDER[:5], 1)
                hidden(c, 5, 2)
                split_head(c, "head", HEAD_ORDER[5:], 1)


def weight_stream(a):
    out = np.zeros((sum(CONTENTS), P, 5, P), np.float32)

    def put(slot, content, blocks, at=0):
        out[SLOT_BASE[slot] + content, :, at:at + len(blocks)] = np.transpose(blocks, (1, 0, 2))

    def rows(w, cols):
        return w[:, cols].reshape(-1, P, P)

    up = {n: a["L0_cond_b" + n].reshape(E * R, -1) for n in "qkvo"}
    down = {n: np.transpose(a["L0_cond_a" + n], (1, 0, 2)).reshape(-1, E * R) for n in "qkvo"}
    for s, n in zip(LORA_A_SLOTS, "qkv"):
        put(s, 0, rows(down[n], slice(None)))
    for k in range(KVH):
        for slot, n, h in [(0, "k", k), (1, "v", k)] + [(2 + g, "q", k * GROUP + g) for g in range(GROUP)]:
            cols = slice(h * HD, (h + 1) * HD)
            put(slot, k, rows(a["L0_cond_w" + n], cols))
            put(slot, k, up[n][None, :, cols], KC)
        mine = slice(k * GROUP * HD, (k + 1) * GROUP * HD)
        for j in range(KC):
            put(6 + j, k + WO_FIRST[6 + j], rows(a["L0_cond_wo"][mine], slice(j * P, (j + 1) * P)))
        put(10, k + WO_FIRST[10], rows(down["o"][mine], slice(None)))
    put(*BO_PIECE, up["o"].reshape(P, KC, P).transpose(1, 0, 2))
    for hb in range(KC):
        for s, n in enumerate("qkv"):
            put(s, QKV2_FIRST + hb, rows(a["L0_attn_w_" + n].T, slice(hb * P, (hb + 1) * P)))
    for j, (s, content) in enumerate(OUT2_PIECES):
        put(s, content, rows(a["L0_attn_w_o"].T, slice(j * P, (j + 1) * P)))
    layers = [("L0_cond2_W", "L0_cond2_Wr", "L0_cond2_A", "L0_cond2_B"),
              ("L0_ffn_W_base", "L0_ffn_W_router", "L0_ffn_A_stack", "L0_ffn_B_stack")]
    for (wb, wr, wa, wu), ((sa, ca), pieces) in zip(layers, ROUTED):
        put(sa, ca, rows(a[wa].reshape(E * R, DM).T, slice(None)))
        router = a[wr].T.reshape(KC, P, E).transpose(1, 0, 2)
        out[SLOT_BASE[sa] + ca, :, KC, 0:KC * E] = router.reshape(P, KC * E)
        up2 = np.transpose(a[wu], (0, 2, 1)).reshape(E * R, DM)
        for j, (s, content) in enumerate(pieces):
            cols = slice(j * P, (j + 1) * P)
            put(s, content, rows(a[wb].T, cols))
            put(s, content, up2[None, :, cols], KC)
    return out.reshape(-1, P, PIECE)


def layouts(a):
    x = a["x"].reshape(CHUNKS, CT, KC, P).transpose(0, 3, 2, 1).reshape(CHUNKS, P, KC * CT)

    def over_partitions(v):
        return np.broadcast_to(v.reshape(CHUNKS, 1, CT), (CHUNKS, P, CT))

    idx = a["itok_B_0_7"]
    idx_tok = np.repeat(idx, T)
    m = a["mask_BxS_bf1"].view(np.uint8).reshape(CHUNKS, TILES, 4, 1, T)
    m = np.broadcast_to(m, (CHUNKS, TILES, 4, T, T)).transpose(0, 2, 3, 1, 4).reshape(CHUNKS, P, TILES * T)
    return {
        "xT": x,
        "pos": over_partitions(a["pos_BxS"]),
        "idx": over_partitions(idx_tok),
        "idx_tile": idx_tok.reshape(CHUNKS, TILES, P).transpose(0, 2, 1),
        "mask": m,
        "bias": a["L0_ffn_b_base"].reshape(KC, P).T,
        "consts": constants(),
        "stream": weight_stream(a),
    }


def kernel(**inputs):
    from concourse import bacc
    from concourse.bass_utils import run_bass_kernel_spmd

    a = {n: np.asarray(v) for n, v in inputs.items()}
    nc = bacc.Bacc("TRN2", target_bir_lowering=False, num_devices=1)
    arrays, args = {}, {}
    for name, v in layouts(a).items():
        v = np.ascontiguousarray(v)
        arrays[f"in_{name}"] = v
        args[name] = nc.dram_tensor(f"in_{name}", v.shape, mybir.dt.from_np(v.dtype), kind="ExternalInput").ap()
    args["outT"] = nc.dram_tensor("out_T", (CHUNKS, P, KC * CT), F32, kind="ExternalOutput").ap()
    build(nc, **args)
    r = run_bass_kernel_spmd(nc, [arrays], core_ids=[0])
    got = r.results[0]["out_T"].reshape(CHUNKS, P, KC, CT).transpose(0, 3, 2, 1)
    return np.ascontiguousarray(got.reshape(B, T, DM))
```

```python
from contextlib import ExitStack

import numpy as np
import concourse.bass as bass
from concourse import mybir

ALU = mybir.AluOpType
ACT = mybir.ActivationFunctionType
AX = mybir.AxisListType
F32 = mybir.dt.float32
F32R = mybir.dt.float32r
I32 = mybir.dt.int32
U8 = mybir.dt.uint8

B, T, DM = 64, 32, 512
TOKENS = B * T
P = 128
CT = 512
CHUNKS = TOKENS // CT
TILES = CT // P
KC = DM // P
KVH, GROUP, HD = 8, 4, 128
E, R = 8, 16
HEADS2, HD2 = 32, 16
THETA = 500000.0
LANG_BIAS, SCALING = 5.0, 2.0
FLT_MAX = 3.4028234663852886e38
PIECE = 5 * P

SLOTS = 11
RAWS = 3
PRIMED = 1
CONTENTS = [13, 13, 13, 10, 10, 10, 9, 9, 10, 10, 11]
SLOT_BASE = [sum(CONTENTS[:s]) for s in range(SLOTS)]
LORA_A_SLOTS = [8, 9, 10]
WO_FIRST = {6: 0, 7: 0, 8: 1, 9: 1, 10: 1}
QKV2_FIRST = 8
OUT2_PIECES = [(3, 8), (4, 8), (5, 8), (7, 8)]
BO_PIECE = (10, 9)
ROUTED = [
    ((8, 9), [(9, 9), (6, 8), (0, 12), (1, 12)]),
    ((2, 12), [(3, 9), (4, 9), (5, 9), (10, 10)]),
]
HEAD_ORDER = [8, 9, 0, 1, 10, 2, 3, 4, 5]
STEP_ORDER = [0, 1, 2, 3, 4, 5, 10, 6, 7, 8, 9]
EPI_ORDER = [10, 6, 7, 8, 9]
MID_PIECES = [(3, 9), (4, 9), (5, 9), (10, 10)]

def _per_raw(n):
    return [len(range(r, n, RAWS)) for r in range(RAWS)]


RAW_HEAD, RAW_STEP, RAW_EPI, RAW_B, RAW_MID = map(_per_raw, (9, SLOTS, 5, 3, 4))
RAW_CHUNK = [8 * s + e + 4 * b + m + h
             for s, e, b, m, h in zip(RAW_STEP, RAW_EPI, RAW_B, RAW_MID, RAW_HEAD)]


def raw_use(c, part, j, k=0):
    r = j % RAWS
    before = j // RAWS
    if part == "prologue":
        return r, before
    n = before + RAW_HEAD[r] + c * RAW_CHUNK[r]
    if part == "step":
        return r, n + k * RAW_STEP[r]
    n = n + KVH * RAW_STEP[r]
    if part == "epi":
        return r, n
    n = n + RAW_EPI[r]
    if part == "b":
        return r, n + k * RAW_B[r]
    n = n + KC * RAW_B[r]
    if part == "mid":
        return r, n
    return r, n + RAW_MID[r]


PROJ = {"k": (0, 0), "v": (1, 0), "q0": (2, 0), "q1": (3, 0), "q2": (0, 1), "q3": (1, 1), "vT": (2, 1)}
WOUT = {"ho": (3, 0), "y0": (0, 0), "y1": (1, 0), "y2": (2, 0), "y3": (3, 1)}
N_LORA, N_PROJ, N_WO, N_ROUTE = [1, 1, 1, 0], [2, 2, 2, 1], [1, 1, 1, 2], [1, 1, 1, 1]
RING_CHUNK = [a + KVH * (b + w) + KC + 1 + 2 * r
              for a, b, w, r in zip(N_LORA, N_PROJ, N_WO, N_ROUTE)]


def ring_use(c, part, which, k=0):
    if part == "proj":
        b, at = PROJ[which]
        done = 0 if isinstance(k, int) and k == 0 else k - 1
        n = k * N_PROJ[b] + done * N_WO[b] + at + N_LORA[b]
    elif part == "wo":
        b, at = WOUT[which]
        n = (KVH if isinstance(k, int) and k == KVH else k + 1) * N_PROJ[b] + (k - 1) * N_WO[b] + at + N_LORA[b]
    elif part == "lora":
        b, n = which, 0
    else:
        b = which
        n = N_LORA[b] + KVH * (N_PROJ[b] + N_WO[b])
        if part == "b":
            n = n + k
        else:
            n = n + KC
            if part == "route":
                n = n + 1 + k * N_ROUTE[b]
    return b, n + c * RING_CHUNK[b]


C_FREQ, C_SIGN, C_EID, C_EVEN, C_ODD = range(5)
C_HM = 5
C_TIE = 13
C_E = 21
C_CAUSAL = 29
C_IDENT = 61
C_COLS = C_IDENT + P


def constants():
    p = np.arange(P)
    half = HD // 2
    c = np.zeros((P, C_COLS), np.float32)
    freq = np.float32(THETA) ** (-np.arange(half, dtype=np.float32) / np.float32(half))
    c[:, C_FREQ] = freq[p % half]
    c[:, C_SIGN] = np.where(p < half, -1.0, 1.0)
    c[:, C_EID] = p // R
    c[:, C_EVEN] = (p // HD2) % 2 == 0
    c[:, C_ODD] = (p // HD2) % 2 == 1
    c[:, C_HM:C_HM + 8] = (p // HD2)[:, None] == np.arange(8)
    c[:, C_TIE:C_TIE + 8] = 8 - np.arange(8)
    c[:, C_E:C_E + 8] = np.arange(8)
    c[:, C_CAUSAL:C_CAUSAL + T] = (p % T)[:, None] >= np.arange(T)
    c[:, C_IDENT:] = np.eye(P)
    return c


TWO_PI = 2 * np.pi
ROUND = 1.5 * 2.0 ** 23
PI_A = 6.28125
PI_B = float(np.float32(np.float32((TWO_PI - PI_A) * 2 ** 20).astype(np.int64) / 2 ** 20))
PI_C = float(np.float32(TWO_PI - PI_A - PI_B))
PI_IN = 3.1415925

N_TABLE = 15
N_ROUTING = 17


class Chain:

    def __init__(self, eng, sem, base):
        self.eng, self.sem, self.base, self.n = eng, sem, base, 0

    def then(self, ins):
        ins.then_inc(self.sem, 1)
        self.n += 1
        self.eng.wait_ge(self.sem, self.base + self.n)


def build(nc, xT, pos, idx, idx_tile, mask, bias, consts, stream, outT):
    with ExitStack() as ctx:
        def sb(name, shape, dt=F32):
            return ctx.enter_context(nc.sbuf_tensor(name, shape, dt))

        def sem(name):
            return ctx.enter_context(nc.semaphore(name))

        w_hi_t = [sb(f"w_hi{s}", [P, PIECE], F32R) for s in range(SLOTS)]
        w_lo_t = [sb(f"w_lo{s}", [P, PIECE], F32R) for s in range(SLOTS)]
        raw = [sb(f"raw{r}", [P, PIECE]) for r in range(RAWS)]
        act_hi = [sb(f"act_hi{i}", [P, KC, CT], F32R) for i in range(2)]
        act_lo = [sb(f"act_lo{i}", [P, KC, CT], F32R) for i in range(2)]
        q_hi, q_lo = sb("q_hi", [P, GROUP, CT], F32R), sb("q_lo", [P, GROUP, CT], F32R)
        k_hi, k_lo = sb("k_hi", [P, CT], F32R), sb("k_lo", [P, CT], F32R)
        v_hi, v_lo = sb("v_hi", [P, TILES, P], F32R), sb("v_lo", [P, TILES, P], F32R)
        p_hi, p_lo = sb("p_hi", [P, TILES * GROUP, 4, T], F32R), sb("p_lo", [P, TILES * GROUP, 4, T], F32R)
        o_hi, o_lo = sb("o_hi", [P, GROUP, CT], F32R), sb("o_lo", [P, GROUP, CT], F32R)
        h_hi, h_lo = sb("h_hi", [P, 3, CT], F32R), sb("h_lo", [P, 3, CT], F32R)
        x_res = sb("x_res", [P, KC, CT])
        y_acc = sb("y_acc", [P, KC + 1, CT])
        cos_t, sin_t = sb("cos_t", [P, CT]), sb("sin_t", [P, CT])
        own = sb("own", [P, CT])
        r_cos, r_sin = sb("r_cos", [P, 2, CT]), sb("r_sin", [P, 2, CT])
        roped = r_cos
        q2_f = r_cos[:, 0, :]
        odd_f, o2_f = r_sin[:, 0, :], r_sin[:, 1, :]
        x_next = [r_cos[:, 0, :], r_cos[:, 1, :], r_sin[:, 0, :], r_sin[:, 1, :]]
        h_f = sb("h_f", [P, 2, CT])
        v_f = h_f[:, 0, :]
        sT = sb("sT", [P, TILES * GROUP, T])
        sc = sb("sc", [P, TILES * GROUP, T])
        pT = sb("pT", [P, TILES * GROUP, T])
        pos_i = pT[:, :, :].rearrange("p a b -> p (a b)").bitcast(I32)
        idx_i = sc[:, :, :].rearrange("p a b -> p (a b)").bitcast(I32)
        s_max, s_sum, s_inv = (sb(n, [P, TILES * GROUP]) for n in ("s_max", "s_sum", "s_inv"))
        mask_u = sb("mask_u", [P, TILES, T], U8)
        mask_f = sb("mask_f", [P, TILES, T])
        cst = sb("cst", [P, C_COLS])
        ffn_b = sb("ffn_b", [P, KC])
        idx_ti = sb("idx_ti", [P, TILES], I32)
        idx_tf = sb("idx_tf", [P, TILES])
        lang = sb("lang", [P, TILES, E])
        rt = {n: sb("rt_" + n, [P, TILES, E]) for n in ("l", "eq", "one", "l2", "two", "gate")}
        rs = {n: sb("rs_" + n, [P, TILES]) for n in ("m1", "m2", "c", "d", "e", "s", "w1", "w2")}
        gate_x, gate_t = sT[:, :, :].rearrange("p a (e r) -> p (a e) r", e=2)\
            .rearrange("p (a e) r -> p a e r", a=TILES), pT[:, :, :].rearrange("p a b -> p (a b)")

        ring = [ctx.enter_context(nc.psum_tensor(f"ring{b}", [P, CT], F32)) for b in range(4)]
        att = ctx.enter_context(nc.psum_tensor("att", [P, TILES, CT], F32))

        ring_full = [sem(f"ring_full{b}") for b in range(4)]
        ring_free = [sem(f"ring_free{b}") for b in range(4)]
        raw_full = [sem(f"raw_full{r}") for r in range(RAWS)]
        raw_free = [sem(f"raw_free{r}") for r in range(RAWS)]
        w_hi_ok = [sem(f"w_hi_ok{s}") for s in range(SLOTS)]
        w_ok = [sem(f"w_ok{s}") for s in range(SLOTS)]
        ld_const, ld_x, ld_pos, ld_idx = (sem(n) for n in ("ld_const", "ld_x", "ld_pos", "ld_idx"))
        ld_mask, ld_tile, ld_res, stored = (sem(n) for n in ("ld_mask", "ld_tile", "ld_res", "stored"))
        act_hi_ok = [sem(f"act_hi_ok{i}") for i in range(2)]
        act_ok = [[sem(f"act_ok{i}{a}") for a in range(KC)] for i in range(2)]
        own_ok, y_zero, table, zeroed, trig_ok = (sem(n) for n in ("own_ok", "y_zero", "table", "zeroed", "trig_ok"))
        h_f_ok, h_hi_ok, h_ok = (sem(n) for n in ("h_f_ok", "h_hi_ok", "h_ok"))
        rope_part, rope_sum, qk_hi_ok, qk_ok = (sem(n) for n in ("rope_part", "rope_sum", "qk_hi_ok", "qk_ok"))
        v_hi_ok, s_full, s_evac, smax, exp_ok = (sem(n) for n in ("v_hi_ok", "s_full", "s_evac", "smax", "exp_ok"))
        p_hi_ok, p_ok, pv_full, o_hi_ok, o_ok = (sem(n) for n in ("p_hi_ok", "p_ok", "pv_full", "o_hi_ok", "o_ok"))
        q2_ok, k2_hi_ok, qx_hi_ok, qx_ok = (sem(n) for n in ("q2_ok", "k2_hi_ok", "qx_hi_ok", "qx_ok"))
        pv2_full, odd_ok, o2_ok, o2_hi_ok, o2_lo_ok = (sem(n) for n in ("pv2_full", "odd_ok", "o2_ok", "o2_hi_ok", "o2_lo_ok"))
        routing, gating, route_exp, gate_ok, base_full, f_sum = (sem(n) for n in ("routing", "gating", "route_exp", "gate_ok", "base_full", "f_sum"))

        ident = cst[:, C_IDENT:C_IDENT + P]
        QK = {"k": 0, "q0": 1, "q1": 2, "q2": 3, "q3": 4}

        def f(ap):
            return ap.bitcast(F32)

        def w_count(c, s, content):
            return c * CONTENTS[s] + (content + 1)

        def step_of(c, k):
            return c * KVH + k

        def soft(c, group):
            return c * 16 + group

        block = ctx.enter_context(nc.Block())

        @block.sync
        def _(sp):
            def load(c, part, j, slot, content, k=0):
                r, n = raw_use(c, part, j, k)
                sp.wait_ge(raw_free[r], n + PRIMED)
                src = stream[bass.ds(content + SLOT_BASE[slot], 1)].rearrange("o p n -> (o p) n")
                sp.dma_start(raw[r][:, :], src).then_inc(raw_full[r], 16)

            def load_head(c, part):
                for j, s in enumerate(HEAD_ORDER):
                    load(c, part, j, s, 0)

            sp.dma_start(cst[:, :], consts).then_inc(ld_const, 16)
            sp.dma_start(ffn_b[:, :], bias).then_inc(ld_const, 16)

            def chunk_of(dram, c):
                return dram[bass.ds(c, 1)].rearrange("o p n -> (o p) n")

            def load_next(c):
                for a in range(KC):
                    sp.dma_start(x_next[a], chunk_of(xT, c)[:, a * CT:(a + 1) * CT]).then_inc(ld_x, 16)
                sp.dma_start(idx_i, chunk_of(idx, c)).then_inc(ld_idx, 16)
                sp.dma_start(mask_u[:, :, :].rearrange("p a t -> p (a t)"), chunk_of(mask, c)).then_inc(ld_mask, 16)
                sp.dma_start(idx_ti[:, :], chunk_of(idx_tile, c)).then_inc(ld_tile, 16)

            sp.sem_inc(stored, 16 * PRIMED)
            load_next(0)
            sp.dma_start(pos_i, chunk_of(pos, 0)).then_inc(ld_pos, 16)
            load_head(0, "prologue")
            with sp.Fori(0, CHUNKS) as c:
                sp.wait_ge(f_sum, c * KC + PRIMED)
                sp.dma_start(x_res[:, :, :].rearrange("p a t -> p (a t)"), chunk_of(xT, c)).then_inc(ld_res, 16)

                def step(k):
                    for j, s in enumerate(STEP_ORDER):
                        load(c, "step", j, s, k + WO_FIRST[s] if s in WO_FIRST else k + 1, k)

                step(0)
                with sp.Fori(1, KVH) as k:
                    step(k)
                for j, s in enumerate(EPI_ORDER):
                    load(c, "epi", j, s, KVH + WO_FIRST[s])
                with sp.Fori(0, KC) as hb:
                    for s in range(3):
                        load(c, "b", s, s, hb + QKV2_FIRST + 1, hb)
                for j, (s, content) in enumerate(MID_PIECES):
                    load(c, "mid", j, s, content)
                for a in range(KC):
                    sp.wait_ge(act_ok[0][a], c * 2 + 2)
                load_next(c + 1)
                load_head(c, "head")
                sp.wait_ge(h_f_ok, c * 6 + 6)
                sp.dma_start(pos_i, chunk_of(pos, c + 1)).then_inc(ld_pos, 16)
                sp.wait_ge(f_sum, c * KC + KC + PRIMED)
                sp.dma_start(outT[bass.ds(c, 1)].rearrange("o p n -> (o p) n"),
                             y_acc[:, 0:KC, :].rearrange("p a t -> p (a t)")).then_inc(stored, 16)
            sp.wait_ge(stored, 16 * (CHUNKS + PRIMED))

        @block.tensor
        def _(pe):
            def three(out, w, x, start, stop):
                nc.tensor.matmul(out, w[0], x[0], start=start, stop=False)
                nc.tensor.matmul(out, w[1], x[0], start=False, stop=False)
                return nc.tensor.matmul(out, w[0], x[1], start=False, stop=stop)

            def w(s, a, n=P):
                return w_hi_t[s][:, a:a + n], w_lo_t[s][:, a:a + n]

            def open_bank(use):
                b, n = use
                pe.wait_ge(ring_free[b], n + PRIMED)
                return ring[b]

            def weights(c, s, content):
                pe.wait_ge(w_ok[s], w_count(c, s, content))

            def block_of(out, s, x, start=True, stop=True, part=range(KC), ready=None):
                for a in part:
                    if ready:
                        pe.wait_ge(ready[0][a], ready[1])
                    last = three(out, w(s, a * P), (x[0][:, a, :], x[1][:, a, :]),
                                 start and a == 0, stop and a == KC - 1)
                return last

            def scores_and(kh, kl, count):
                for t in range(TILES):
                    cols = slice(t * P, (t + 1) * P)
                    last = three(att[:, t, :], (kh[:, cols], kl[:, cols]),
                                 (q_hi[:, :, cols], q_lo[:, :, cols]), True, True)
                last.then_inc(s_full, 1)

            def values(t):
                cols = slice(t * GROUP, (t + 1) * GROUP)
                return three(att[:, t, :], (v_hi[:, t, :], v_lo[:, t, :]),
                             (p_hi[:, cols, :, :], p_lo[:, cols, :, :]), True, True)

            def turn_v(use):
                out = open_bank(use)
                for t in range(TILES):
                    last = nc.tensor.transpose(out[:, t * P:(t + 1) * P], v_f[:, t * P:(t + 1) * P], ident)
                last.then_inc(ring_full[use[0]], 1)

            def wo_block(c, k, name):
                j = int(name[1]) if name != "ho" else 4
                s = 6 + j
                use = ring_use(c, "wo", name, k)
                out = open_bank(use)
                weights(c, s, k - 1 + WO_FIRST[s])
                block_of(out[:, :], s, (o_hi, o_lo)).then_inc(ring_full[use[0]], 1)

            def pv(c, k):
                pe.wait_ge(p_ok, soft(c, k) * 4)
                pe.wait_ge(s_evac, soft(c, k))
                b, n = ring_use(c, "proj", "vT", k - 1)
                pe.wait_ge(ring_free[b], n + 1 + PRIMED)
                for t in range(TILES):
                    values(t).then_inc(pv_full, 1)

            pe.wait_ge(ld_const, 32)
            pe.wait_ge(zeroed, 2)
            with pe.Fori(0, CHUNKS) as c:
                for j, s in enumerate(LORA_A_SLOTS):
                    use = ring_use(c, "lora", j)
                    out = open_bank(use)
                    weights(c, s, 0)
                    block_of(out[:, :], s, (act_hi[0], act_lo[0]), ready=j == 0 and (act_ok[0], c * 2 + 1))\
                        .then_inc(ring_full[use[0]], 1)

                def proj(k, name, slot, lora):
                    use = ring_use(c, "proj", name, k)
                    out = open_bank(use)
                    weights(c, slot, k)
                    block_of(out[:, :], slot, (act_hi[0], act_lo[0]), stop=False)
                    pe.wait_ge(h_ok, c * 6 + lora + 1)
                    three(out[:, :], w(slot, KC * P), (h_hi[:, lora, :], h_lo[:, lora, :]),
                          False, True).then_inc(ring_full[use[0]], 1)

                def step(k, first=False):
                    proj(k, "k", 0, 0)
                    proj(k, "v", 1, 1)
                    proj(k, "q0", 2, 2)
                    proj(k, "q1", 3, 2)
                    if not first:
                        pv(c, k)
                    proj(k, "q2", 4, 2)
                    proj(k, "q3", 5, 2)
                    b, n = ring_use(c, "proj", "v", k)
                    pe.wait_ge(ring_free[b], n + 1 + PRIMED)
                    turn_v(ring_use(c, "proj", "vT", k))
                    if not first:
                        pe.wait_ge(o_ok, (step_of(c, k)) * TILES)
                        wo_block(c, k, "ho")
                        wo_block(c, k, "y0")
                    pe.wait_ge(qk_ok, step_of(c, k) * 5 + 5)
                    scores_and(k_hi, k_lo, None)
                    if not first:
                        wo_block(c, k, "y1")
                        wo_block(c, k, "y2")
                        wo_block(c, k, "y3")

                step(0, True)
                with pe.Fori(1, KVH) as k:
                    step(k)
                pv(c, KVH)
                pe.wait_ge(o_ok, (step_of(c, KVH)) * TILES)
                wo_block(c, KVH, "ho")

                def up(j):
                    b, _ = ring_use(c, "wo", f"y{j}", KVH)
                    three(ring[b][:, :], w(BO_PIECE[0], j * P), (h_hi[:, 0, :], h_lo[:, 0, :]), False, True)\
                        .then_inc(ring_full[b], 1)

                for j in range(KC):
                    out = open_bank(ring_use(c, "wo", f"y{j}", KVH))
                    weights(c, 6 + j, KVH - 1 + WO_FIRST[6 + j])
                    block_of(out[:, :], 6 + j, (o_hi, o_lo), stop=False)
                    if j == 1:
                        weights(c, *BO_PIECE)
                        pe.wait_ge(h_ok, c * 6 + 4)
                    if j:
                        up(j - 1)
                up(KC - 1)

                def proj2(s, hb, ready=None):
                    use = ring_use(c, "b", s, hb)
                    out = open_bank(use)
                    weights(c, s, hb + QKV2_FIRST)
                    block_of(out[:, :], s, (act_hi[1], act_lo[1]), ready=ready).then_inc(ring_full[use[0]], 1)

                def scores2(hb, q, first=False):
                    quad = (c * KC + hb) * 2 + q
                    b, n = ring_use(c, "b", 1, hb)
                    pe.wait_ge(ring_free[b], n + 1 + PRIMED)
                    pe.wait_ge(qx_ok, quad + 1)
                    pe.wait_ge(s_evac, soft(c, hb * 2 + 8 + q))
                    if not first:
                        pe.wait_ge(o2_ok, (quad - 1) * 2 + PRIMED)
                    scores_and(k_hi, k_lo, None)

                def values2(hb, q, last=False):
                    if q == 0:
                        b, n = ring_use(c, "b", 3, hb)
                        pe.wait_ge(ring_free[b], n + 1 + PRIMED)
                    pe.wait_ge(p_ok, soft(c, hb * 2 + 9 + q) * 4)
                    pe.wait_ge(s_evac, soft(c, hb * 2 + (9 if last else 10) + q))
                    if last:
                        pe.wait_ge(o2_ok, ((c * KC + hb) * 2 + q) * 2 + PRIMED)
                    for t in range(TILES):
                        ins = values(t)
                    ins.then_inc(pv2_full, 1)

                def head_block(hb, last=False):
                    b, n = ring_use(c, "b", 2, hb)
                    pe.wait_ge(ring_free[b], n + 1 + PRIMED)
                    turn_v(ring_use(c, "b", 3, hb))
                    if not last:
                        proj2(0, hb + 1)
                    scores2(hb, 1)
                    if not last:
                        proj2(1, hb + 1)
                    values2(hb, 0)
                    if not last:
                        proj2(2, hb + 1)
                        scores2(hb + 1, 0)
                    values2(hb, 1, last)

                proj2(0, 0, (act_ok[1], c * 2 + 1))
                proj2(1, 0)
                proj2(2, 0)
                scores2(0, 0, True)
                with pe.Fori(0, KC - 1) as hb:
                    head_block(hb)
                head_block(KC - 1, True)

                for part in (range(KC - 1), range(KC - 1, KC)):
                    pe.wait_ge(o2_lo_ok, c * KC + part[-1] + 1 + PRIMED)
                    for j, (s, content) in enumerate(OUT2_PIECES):
                        use = ring_use(c, "out2", j)
                        if part[0] == 0:
                            open_bank(use)
                            weights(c, s, content)
                        ins = block_of(ring[use[0]][:, :], s, (o_hi, o_lo), part=part)
                        if part[0]:
                            ins.then_inc(ring_full[use[0]], 1)

                for layer, ((sa, ca), pieces) in enumerate(ROUTED):
                    x = act_hi[layer], act_lo[layer]
                    weights(c, sa, ca)
                    use = ring_use(c, "route", 0, layer)
                    out = open_bank(use)
                    for a in range(KC):
                        pe.wait_ge(act_ok[layer][a], c * 2 + 2)
                        last = three(out[:, :], w(sa, KC * P + (a + 1) * E - P),
                                     (x[0][:, a, :], x[1][:, a, :]), a == 0, a == KC - 1)
                    last.then_inc(ring_full[use[0]], 1)
                    logits_sb = use
                    use = ring_use(c, "route", 1, layer)
                    out = open_bank(use)
                    block_of(out[:, :], sa, x).then_inc(ring_full[use[0]], 1)

                    def turn(which, src):
                        use = ring_use(c, "route", which, layer)
                        out = open_bank(use)
                        for t in range(TILES):
                            last = nc.tensor.transpose(out[:, t * P:(t + 1) * P], src(t), ident)
                        last.then_inc(ring_full[use[0]], 1)

                    for j, (s, content) in enumerate(pieces):
                        weights(c, s, content)
                        block_of(att[:, j, :], s, x, stop=False)
                        if j == 0:
                            pe.wait_ge(ring_free[logits_sb[0]], logits_sb[1] + 1 + PRIMED)
                            turn(2, lambda t: h_f[:, 1 - layer, t * P:(t + 1) * P])
                    pe.wait_ge(gate_ok, c * 2 + layer + 1)
                    turn(3, lambda t: gate_x[:, t, :, :].rearrange("p e r -> p (e r)"))
                    pe.wait_ge(h_ok, c * 6 + 5 + layer)
                    for j, (s, content) in enumerate(pieces):
                        three(att[:, j, :], w(s, KC * P), (h_hi[:, 1 + layer, :], h_lo[:, 1 + layer, :]),
                              False, True).then_inc(base_full, 1)

        @block.scalar
        def _(act):
            def copy(out, in_, scale=1.0):
                return nc.scalar.activation(out, in_, ACT.Copy, scale=scale)

            def split(c, part, j, slot, content, k=0):
                r, n = raw_use(c, part, j, k)
                act.wait_ge(raw_full[r], (n + 1) * 16)
                copy(w_hi_t[slot][:, :], raw[r][:, :]).then_inc(w_hi_ok[slot], 1)

            def split_head(c, part, which):
                for j, s in enumerate(HEAD_ORDER):
                    if s in which:
                        split(c, part, j, s, 0)

            def full(use):
                act.wait_ge(ring_full[use[0]], use[1] + 1)
                return ring[use[0]]

            def hidden(c, fill, at):
                act.wait_ge(h_f_ok, c * 6 + fill + 1)
                copy(h_hi[:, at, :], h_f[:, fill % 2, :]).then_inc(h_hi_ok, 1)

            def turned_v(use):
                out = full(use)
                copy(v_hi[:, :, :], out[:, :].rearrange("p (t d) -> p t d", t=TILES)).then_inc(v_hi_ok, 1)

            def scores_out(group, scale):
                act.wait_ge(s_full, group + 1)
                for b in range(4):
                    rows = slice(T * b, T * b + T)
                    src = att[rows, :, :].rearrange("p a (g t) -> p (a g) t", g=GROUP)[:, :, T * b:T * b + T]
                    last = copy(sT[rows, :, :], src, scale)
                last.then_inc(s_evac, 1)

            def exponent(group):
                act.wait_ge(smax, group * 8 + 4)
                nc.scalar.activation(sc[:, :, :], sc[:, :, :], ACT.Exp).then_inc(exp_ok, 1)

            def probs_hi(group):
                act.wait_ge(smax, group * 8 + 8)
                for b in range(4):
                    rows = slice(T * b, T * b + T)
                    last = copy(p_hi[rows, :, b, :], pT[rows, :, :])
                last.then_inc(p_hi_ok, 1)

            def take_next(c):
                for a in range(KC):
                    act.wait_ge(ld_x, (c * KC + KC) * 16)
                    copy(act_hi[0][:, a, :], x_next[a]).then_inc(act_hi_ok[0], 1)

            take_next(0)
            split_head(0, "prologue", HEAD_ORDER)
            act.wait_ge(ld_const, 32)
            act.wait_ge(zeroed, 2)
            with act.Fori(0, CHUNKS) as c:
                for j in range(3):
                    hidden(c, j, j)
                act.wait_ge(table, c * N_TABLE + N_TABLE)
                nc.scalar.activation(sin_t[:, :], r_sin[:, 0, :], ACT.Sin, scale=cst[:, C_SIGN:C_SIGN + 1])\
                    .then_inc(trig_ok, 1)
                nc.scalar.activation(cos_t[:, :], r_sin[:, 1, :], ACT.Sin).then_inc(trig_ok, 1)

                def attention_out(k):
                    for t in range(TILES):
                        act.wait_ge(pv_full, step_of(c, k - 1) * TILES + t + 1)
                        copy(o_hi[:, :, t * P:(t + 1) * P],
                             att[:, t, :].rearrange("p (g n) -> p g n", g=GROUP)).then_inc(o_hi_ok, 1)

                def qk_out(k, name, dst):
                    act.wait_ge(rope_sum, step_of(c, k) * 5 + QK[name] + 1)
                    copy(dst, roped[:, QK[name] % 2, :]).then_inc(qk_hi_ok, 1)

                def step(k, first=False):
                    qk_out(k, "k", k_hi[:, :])
                    split(c, "step", 0, 0, k + 1, k)
                    use = ring_use(c, "proj", "v", k)
                    if first:
                        act.wait_ge(h_ok, c * 6 + 3)
                    copy(v_f, full(use)[:, :]).then_inc(ring_free[use[0]], 1)
                    split(c, "step", 1, 1, k + 1, k)
                    qk_out(k, "q0", q_hi[:, 0, :])
                    split(c, "step", 2, 2, k + 1, k)
                    qk_out(k, "q1", q_hi[:, 1, :])
                    if not first:
                        attention_out(k)
                    split(c, "step", 3, 3, k + 1, k)
                    qk_out(k, "q2", q_hi[:, 2, :])
                    split(c, "step", 4, 4, k + 1, k)
                    qk_out(k, "q3", q_hi[:, 3, :])
                    turned_v(ring_use(c, "proj", "vT", k))
                    split(c, "step", 5, 5, k + 1, k)
                    def next_wo(j, name):
                        if not first:
                            full(ring_use(c, "wo", name, k))
                        split(c, "step", j, STEP_ORDER[j], None, k)

                    next_wo(6, "ho")
                    next_wo(7, "y0")
                    group = soft(c, k)
                    scores_out(group, HD ** -0.5)
                    exponent(group)
                    next_wo(8, "y1")
                    next_wo(9, "y2")
                    probs_hi(group)
                    next_wo(10, "y3")

                step(0, True)
                with act.Fori(1, KVH) as k:
                    step(k)
                attention_out(KVH)
                full(ring_use(c, "wo", "ho", KVH))
                split(c, "epi", 0, EPI_ORDER[0], None)
                hidden(c, 3, 0)
                for j in range(KC):
                    b, n = ring_use(c, "wo", f"y{j}", KVH)
                    act.wait_ge(ring_free[b], n + 1 + PRIMED)
                    copy(act_hi[1][:, j, :], y_acc[:, j, :]).then_inc(act_hi_ok[1], 1)
                    split(c, "epi", 1 + j, EPI_ORDER[1 + j], None)

                def spread(q):
                    for h in range(GROUP):
                        col = C_HM + GROUP * q + h
                        last = copy(q_hi[:, h, :], q2_f, cst[:, col:col + 1])
                    last.then_inc(qx_hi_ok, 1)

                def take_q(hb):
                    use = ring_use(c, "b", 0, hb)
                    copy(q2_f, full(use)[:, :]).then_inc(ring_free[use[0]], 1)
                    split(c, "b", 0, 0, None, hb)

                def take_k(hb):
                    use = ring_use(c, "b", 1, hb)
                    copy(k_hi[:, :], full(use)[:, :]).then_inc(k2_hi_ok, 1)
                    split(c, "b", 1, 1, None, hb)
                    b, n = ring_use(c, "b", 0, hb)
                    act.wait_ge(ring_free[b], n + 1 + PRIMED)
                    spread(0)

                def take_v(hb):
                    use = ring_use(c, "b", 2, hb)
                    copy(v_f, full(use)[:, :]).then_inc(ring_free[use[0]], 1)
                    split(c, "b", 2, 2, None, hb)

                def odd_heads(hb, q):
                    act.wait_ge(pv2_full, (c * KC + hb) * 2 + q + 1)
                    for j in range(2):
                        rows = slice(64 * q + 32 * j, 64 * q + 32 * j + 32)
                        copy(odd_f[rows, :].rearrange("p (a n) -> p a n", a=TILES),
                             att[rows, :, (2 * j + 1) * P:(2 * j + 2) * P],
                             cst[rows, C_ODD:C_ODD + 1]).then_inc(odd_ok, 1)

                def head_block(hb, last=False):
                    quad = (c * KC + hb) * 2
                    group = soft(c, hb * 2 + 8)
                    spread(1)
                    exponent(group)
                    turned_v(ring_use(c, "b", 3, hb))
                    probs_hi(group)
                    if not last:
                        act.wait_ge(qx_ok, quad + 2)
                        take_q(hb + 1)
                    scores_out(group + 1, HD2 ** -0.5)
                    if not last:
                        take_k(hb + 1)
                    exponent(group + 1)
                    odd_heads(hb, 0)
                    if not last:
                        take_v(hb + 1)
                    probs_hi(group + 1)
                    if not last:
                        scores_out(group + 2, HD2 ** -0.5)
                    odd_heads(hb, 1)
                    act.wait_ge(o2_ok, (quad + 2) * 2 + PRIMED)
                    copy(o_hi[:, hb:hb + 1, :] if last else o_hi[:, bass.ds(hb, 1), :],
                         o2_f.unsqueeze(1)).then_inc(o2_hi_ok, 1)

                take_q(0)
                take_k(0)
                take_v(0)
                scores_out(soft(c, 8), HD2 ** -0.5)
                with act.Fori(0, KC - 1) as hb:
                    head_block(hb)
                head_block(KC - 1, True)

                for j in range(KC):
                    b, n = ring_use(c, "out2", j)
                    act.wait_ge(ring_free[b], n + 1 + PRIMED)
                    copy(act_hi[0][:, j, :], x_res[:, j, :]).then_inc(act_hi_ok[0], 1)
                for j, (s, content) in enumerate(MID_PIECES):
                    split(c, "mid", j, s, content)

                def routed(layer):
                    use = ring_use(c, "route", 0, layer)
                    copy(h_f[:, 1 - layer, :], full(use)[:, :]).then_inc(ring_free[use[0]], 1)
                    act.wait_ge(routing, (c * 2 + layer) * N_ROUTING + 12)
                    nc.scalar.activation(rs["e"][:, :], rs["d"][:, :], ACT.Exp).then_inc(route_exp, 1)
                    use = ring_use(c, "route", 3, layer)
                    copy(gate_t, full(use)[:, :]).then_inc(ring_free[use[0]], 1)
                    hidden(c, 4 + layer, 1 + layer)

                routed(0)
                for j in range(KC):
                    act.wait_ge(base_full, c * 8 + j + 1)
                    copy(act_hi[1][:, j, :], att[:, j, :]).then_inc(act_hi_ok[1], 1)
                take_next(c + 1)
                split_head(c, "head", HEAD_ORDER[:4])
                routed(1)
                act.wait_ge(base_full, c * 8 + 8)
                split_head(c, "head", HEAD_ORDER[4:])

        @block.vector
        def _(dve):
            tt, ts, stt = nc.vector.tensor_tensor, nc.vector.tensor_scalar, nc.vector.scalar_tensor_tensor

            def full(use):
                dve.wait_ge(ring_full[use[0]], use[1] + 1)
                return ring[use[0]]

            def softmax_first(group, masked):
                chain = Chain(dve, smax, group * 8)
                dve.wait_ge(s_evac, group + 1)
                nc.vector.transpose(sc[:, :, :], sT[:, :, :]).then_inc(smax, 1 if masked else 2)
                dve.wait_ge(smax, group * 8 + (1 if masked else 2))
                chain.n = 1 if masked else 2
                if masked:
                    s4 = sc[:, :, :].rearrange("p (a g) s -> p a g s", a=TILES)
                    chain.then(tt(s4, s4, mask_f[:, :, :].unsqueeze(2).to_broadcast([P, TILES, GROUP, T]), ALU.add))
                chain.then(nc.vector.tensor_reduce(s_max[:, :], sc[:, :, :], AX.X, ALU.max))
                tt(sc[:, :, :], sc[:, :, :], s_max[:, :].unsqueeze(2).to_broadcast([P, TILES * GROUP, T]),
                   ALU.subtract).then_inc(smax, 1)

            def softmax_second(group):
                chain = Chain(dve, smax, group * 8 + 4)
                dve.wait_ge(exp_ok, group + 1)
                chain.then(nc.vector.tensor_reduce(s_sum[:, :], sc[:, :, :], AX.X, ALU.add))
                chain.then(nc.vector.reciprocal(s_inv[:, :], s_sum[:, :]))
                chain.then(tt(sc[:, :, :], sc[:, :, :], s_inv[:, :].unsqueeze(2).to_broadcast([P, TILES * GROUP, T]),
                              ALU.mult))
                nc.vector.transpose(pT[:, :, :], sc[:, :, :]).then_inc(smax, 1)

            def own_hidden(c, fill, src, gate, freed):
                if fill >= 2:
                    dve.wait_ge(h_ok, c * 6 + fill - 1)
                ins = tt(h_f[:, fill % 2, :], src, gate, ALU.mult)
                ins.then_inc(h_f_ok, 1)
                if freed is not None:
                    dve.wait_ge(h_f_ok, c * 6 + fill + 1)
                    dve.sem_inc(ring_free[freed], 1)

            for primed in ring_free + [f_sum, o2_ok]:
                dve.sem_inc(primed, PRIMED)
            for part in (p_hi, p_lo):
                nc.vector.memset(f(part[:, :, :, :]), 0.0).then_inc(zeroed, 1)
            dve.wait_ge(ld_const, 32)

            def lo_block(i, a, src, count):
                dve.wait_ge(act_hi_ok[i], count + a + 1)
                tt(act_lo[i][:, a, :], src, f(act_hi[i][:, a, :]), ALU.subtract).then_inc(act_ok[i][a], 1)

            def take_next(c):
                for a in (1, 3):
                    lo_block(0, a, x_next[a], c * 8)
                dve.wait_ge(ld_idx, (c + 1) * 16)
                ts(own[:, :], idx_i, cst[:, C_EID:C_EID + 1], None, ALU.is_equal).then_inc(own_ok, 1)

            take_next(0)
            with dve.Fori(0, CHUNKS) as c:
                dve.wait_ge(own_ok, c + 1)
                for j in range(3):
                    b, _ = use = ring_use(c, "lora", j)
                    own_hidden(c, j, full(use)[:, :], own[:, :], b)
                for a in (0, 2):
                    dve.wait_ge(act_ok[0][a], c * 2 + 1)
                chain = Chain(dve, table, c * N_TABLE)
                dve.wait_ge(ld_pos, (c + 1) * 16)
                ang, turns, cosa = r_cos[:, 0, :], r_cos[:, 1, :], r_sin[:, 1, :]
                chain.then(ts(ang, pos_i, cst[:, C_FREQ:C_FREQ + 1], None, ALU.mult))
                chain.then(ts(turns, ang, 1 / TWO_PI, ROUND, ALU.mult, ALU.add))
                chain.then(ts(turns, turns, -ROUND, None, ALU.add))
                for part in (PI_A, PI_B, PI_C):
                    chain.then(stt(out=ang, in0=turns, scalar=-part, in1=ang, op0=ALU.mult, op1=ALU.add))
                chain.then(ts(r_sin[:, 0, :], ang, PI_IN, -PI_IN, ALU.min, ALU.max))
                chain.then(ts(ang, ang, float(np.pi / 2), None, ALU.add))
                chain.then(ts(turns, ang, float(np.pi), -TWO_PI, ALU.is_gt, ALU.mult))
                chain.then(tt(ang, ang, turns, ALU.add))
                dve.wait_ge(ld_mask, (c + 1) * 16)
                causal = cst[:, C_CAUSAL:C_CAUSAL + T].unsqueeze(1).to_broadcast([P, TILES, T])
                chain.then(tt(mask_f[:, :, :], mask_u[:, :, :], causal, ALU.mult))
                chain.then(ts(mask_f[:, :, :], mask_f[:, :, :], -1.0, FLT_MAX, ALU.add, ALU.mult))
                dve.wait_ge(ld_tile, (c + 1) * 16)
                chain.then(nc.vector.tensor_copy(idx_tf[:, :], idx_ti[:, :]))
                chain.then(tt(lang[:, :, :], cst[:, C_E:C_E + E].unsqueeze(1).to_broadcast([P, TILES, E]),
                              idx_tf[:, :].unsqueeze(2).to_broadcast([P, TILES, E]), ALU.is_equal))
                chain.then(ts(cosa, ang, PI_IN, -PI_IN, ALU.min, ALU.max))
                assert chain.n == N_TABLE
                dve.wait_ge(stored, (c + PRIMED) * 16)
                nc.vector.memset(y_acc[:, :, :], 0.0).then_inc(y_zero, 1)
                dve.wait_ge(trig_ok, c * 2 + 2)

                def rope(k, name):
                    at = step_of(c, k) * 5 + QK[name]
                    half = QK[name] % 2
                    use = ring_use(c, "proj", name, k)
                    src = full(use)
                    if QK[name] >= 2:
                        dve.wait_ge(qk_ok, at - 1)
                    elif QK[name] == 1:
                        if not (isinstance(k, int) and k == 0):
                            dve.wait_ge(qk_ok, at - 1)
                    elif not (isinstance(k, int) and k == 0):
                        dve.wait_ge(qk_ok, at)
                    tt(r_cos[:, half, :], src[:, :], cos_t[:, :], ALU.mult).then_inc(rope_part, 1)
                    tt(r_sin[0:64, half, :], src[64:128, :], sin_t[0:64, :], ALU.mult).then_inc(rope_part, 1)
                    tt(r_sin[64:128, half, :], src[0:64, :], sin_t[64:128, :], ALU.mult).then_inc(ring_free[use[0]], 1)
                    dve.wait_ge(rope_part, at * 2 + 2)
                    dve.wait_ge(ring_free[use[0]], use[1] + 1 + PRIMED)
                    tt(roped[:, half, :], r_cos[:, half, :], r_sin[:, half, :], ALU.add).then_inc(rope_sum, 1)

                def attention_lo(k):
                    for t in range(TILES):
                        dve.wait_ge(o_hi_ok, step_of(c, k - 1) * TILES + t + 1)
                        cols = slice(t * P, (t + 1) * P)
                        tt(o_lo[:, :, cols], att[:, t, :].rearrange("p (g n) -> p g n", g=GROUP),
                           f(o_hi[:, :, cols]), ALU.subtract).then_inc(o_ok, 1)

                def add_y(k, name):
                    j = 4 if name == "ho" else int(name[1])
                    use = ring_use(c, "wo", name, k)
                    src = full(use)
                    tt(y_acc[:, j, :], src[:, :], y_acc[:, j, :], ALU.add).then_inc(ring_free[use[0]], 1)

                def turned_v_lo(use, count):
                    dve.wait_ge(v_hi_ok, count)
                    src = ring[use[0]][:, :].rearrange("p (t d) -> p t d", t=TILES)
                    tt(v_lo[:, :, :], src, f(v_hi[:, :, :]), ALU.subtract).then_inc(ring_free[use[0]], 1)

                def step(k, first=False):
                    group = soft(c, k)
                    rope(k, "k")
                    rope(k, "q0")
                    rope(k, "q1")
                    if not first:
                        attention_lo(k)
                    rope(k, "q2")
                    rope(k, "q3")
                    turned_v_lo(ring_use(c, "proj", "vT", k), c * (KVH + KC) + k + 1)
                    if not first:
                        add_y(k, "ho")
                        add_y(k, "y0")
                    softmax_first(group, True)
                    if not first:
                        add_y(k, "y1")
                    softmax_second(group)
                    if not first:
                        add_y(k, "y2")
                        add_y(k, "y3")

                dve.wait_ge(y_zero, c + 1)
                step(0, True)
                with dve.Fori(1, KVH) as k:
                    step(k)
                attention_lo(KVH)
                add_y(KVH, "ho")
                b, n = ring_use(c, "wo", "ho", KVH)
                dve.wait_ge(ring_free[b], n + 1 + PRIMED)
                own_hidden(c, 3, y_acc[:, KC, :], own[:, :], None)
                for j in range(KC):
                    add_y(KVH, f"y{j}")
                    if j % 2:
                        lo_block(1, j, y_acc[:, j, :], c * 8)

                def spread_lo(hb, q):
                    dve.wait_ge(qx_hi_ok, (c * KC + hb) * 2 + q + 1)
                    for h in range(GROUP):
                        col = C_HM + GROUP * q + h
                        last = stt(out=q_lo[:, h, :], in0=q2_f, scalar=cst[:, col:col + 1],
                                   in1=f(q_hi[:, h, :]), op0=ALU.mult, op1=ALU.subtract)
                    last.then_inc(qx_ok, 1)

                def take_k(hb):
                    use = ring_use(c, "b", 1, hb)
                    dve.wait_ge(k2_hi_ok, c * KC + hb + 1)
                    tt(k_lo[:, :], ring[use[0]][:, :], f(k_hi[:, :]), ALU.subtract).then_inc(ring_free[use[0]], 1)
                    spread_lo(hb, 0)

                def extract(hb, q):
                    for j in range(2):
                        rows = slice(64 * q + 32 * j, 64 * q + 32 * j + 32)
                        dve.wait_ge(odd_ok, ((c * KC + hb) * 2 + q) * 2 + j + 1)
                        stt(out=o2_f[rows, :].rearrange("p (a n) -> p a n", a=TILES),
                            in0=att[rows, :, 2 * j * P:(2 * j + 1) * P], scalar=cst[rows, C_EVEN:C_EVEN + 1],
                            in1=odd_f[rows, :].rearrange("p (a n) -> p a n", a=TILES),
                            op0=ALU.mult, op1=ALU.add).then_inc(o2_ok, 1)

                def head_block(hb, last=False):
                    group = soft(c, hb * 2 + 8)
                    spread_lo(hb, 1)
                    softmax_second(group)
                    turned_v_lo(ring_use(c, "b", 3, hb), c * (KVH + KC) + hb + KVH + 1)
                    softmax_first(group + 1, False)
                    if not last:
                        take_k(hb + 1)
                    dve.wait_ge(p_ok, group * 4 + 4)
                    softmax_second(group + 1)
                    dve.wait_ge(o2_lo_ok, c * KC + hb + PRIMED)
                    extract(hb, 0)
                    if not last:
                        softmax_first(group + 2, False)
                    extract(hb, 1)

                take_k(0)
                softmax_first(soft(c, 8), False)
                with dve.Fori(0, KC - 1) as hb:
                    head_block(hb)
                head_block(KC - 1, True)

                dve.wait_ge(ld_res, (c + 1) * 16)
                for j in range(KC):
                    use = ring_use(c, "out2", j)
                    tt(x_res[:, j, :], full(use)[:, :], x_res[:, j, :], ALU.add).then_inc(ring_free[use[0]], 1)
                for j in (1, 3):
                    lo_block(0, j, x_res[:, j, :], c * 8 + KC)

                def routed(layer):
                    chain = Chain(dve, routing, (c * 2 + layer) * N_ROUTING)
                    use = ring_use(c, "route", 2, layer)
                    src = full(use)[:, :].rearrange("p (a n) -> p a n", a=TILES)[:, :, P - E:P]

                    def wide(ap):
                        return ap[:, :].unsqueeze(2).to_broadcast([P, TILES, E])

                    tie = cst[:, C_TIE:C_TIE + E].unsqueeze(1).to_broadcast([P, TILES, E])
                    if layer == 0:
                        ins = stt(out=rt["l"][:, :, :], in0=lang[:, :, :], scalar=LANG_BIAS, in1=src,
                                  op0=ALU.mult, op1=ALU.add)
                    else:
                        ins = nc.vector.tensor_copy(rt["l"][:, :, :], src)
                    chain.then(ins)
                    dve.sem_inc(ring_free[use[0]], 1)

                    def largest(logits, m, chosen):
                        chain.then(nc.vector.tensor_reduce(rs[m][:, :], logits[:, :, :], AX.X, ALU.max))
                        chain.then(tt(rt["eq"][:, :, :], logits[:, :, :], wide(rs[m]), ALU.is_equal))
                        chain.then(tt(rt["eq"][:, :, :], rt["eq"][:, :, :], tie, ALU.mult))
                        chain.then(nc.vector.tensor_reduce(rs["c"][:, :], rt["eq"][:, :, :], AX.X, ALU.max))
                        chain.then(tt(rt[chosen][:, :, :], tie, wide(rs["c"]), ALU.is_equal))

                    largest(rt["l"], "m1", "one")
                    chain.then(stt(out=rt["l2"][:, :, :], in0=rt["one"][:, :, :], scalar=-3e38,
                                   in1=rt["l"][:, :, :], op0=ALU.mult, op1=ALU.add))
                    chain.then(nc.vector.tensor_reduce(rs["m2"][:, :], rt["l2"][:, :, :], AX.X, ALU.max))
                    chain.then(tt(rt["eq"][:, :, :], rt["l2"][:, :, :], wide(rs["m2"]), ALU.is_equal))
                    chain.then(tt(rt["eq"][:, :, :], rt["eq"][:, :, :], tie, ALU.mult))
                    chain.then(nc.vector.tensor_reduce(rs["c"][:, :], rt["eq"][:, :, :], AX.X, ALU.max))
                    chain.then(tt(rs["d"][:, :], rs["m2"][:, :], rs["m1"][:, :], ALU.subtract))
                    assert chain.n == 12
                    chain.then(tt(rt["two"][:, :, :], tie, wide(rs["c"]), ALU.is_equal))
                    dve.wait_ge(route_exp, c * 2 + layer + 1)
                    chain.then(ts(rs["s"][:, :], rs["e"][:, :], 1.0, None, ALU.add))
                    chain.then(nc.vector.reciprocal(rs["w1"][:, :], rs["s"][:, :]))
                    chain.then(stt(out=rs["w2"][:, :], in0=rs["e"][:, :], scalar=SCALING, in1=rs["w1"][:, :],
                                   op0=ALU.mult, op1=ALU.mult))
                    chain.then(ts(rs["w1"][:, :], rs["w1"][:, :], SCALING, None, ALU.mult))
                    assert chain.n == N_ROUTING
                    gate_chain = Chain(dve, gating, (c * 2 + layer) * 3)
                    gate_chain.then(tt(rt["one"][:, :, :], rt["one"][:, :, :], wide(rs["w1"]), ALU.mult))
                    gate_chain.then(tt(rt["two"][:, :, :], rt["two"][:, :, :], wide(rs["w2"]), ALU.mult))
                    gate_chain.then(tt(rt["gate"][:, :, :], rt["one"][:, :, :], rt["two"][:, :, :], ALU.add))
                    nc.vector.tensor_copy(gate_x[:, :, :, :], rt["gate"][:, :, :].unsqueeze(3)
                                          .to_broadcast([P, TILES, E, R])).then_inc(gate_ok, 1)
                    b, n = ring_use(c, "route", 3, layer)
                    dve.wait_ge(ring_free[b], n + 1 + PRIMED)
                    use = ring_use(c, "route", 1, layer)
                    own_hidden(c, 4 + layer, full(use)[:, :], gate_t, use[0])

                routed(0)
                for j in range(KC):
                    dve.wait_ge(act_hi_ok[1], c * 8 + KC + j + 1)
                    tt(act_lo[1][:, j, :], att[:, j, :], f(act_hi[1][:, j, :]), ALU.subtract)\
                        .then_inc(act_ok[1][j], 1)
                take_next(c + 1)
                routed(1)
                for j in range(KC):
                    dve.wait_ge(base_full, c * 8 + KC + j + 1)
                    stt(out=y_acc[:, j, :], in0=att[:, j, :], scalar=ffn_b[:, j:j + 1], in1=x_res[:, j, :],
                        op0=ALU.add, op1=ALU.add).then_inc(f_sum, 1)

        @block.gpsimd
        def _(pool):
            def lo(out, whole, hi):
                return nc.gpsimd.tensor_tensor(out, whole, f(hi), ALU.subtract)

            def split(c, part, j, slot, content, k=0):
                r, n = raw_use(c, part, j, k)
                pool.wait_ge(w_hi_ok[slot], w_count(c, slot, content))
                lo(w_lo_t[slot][:, :], raw[r][:, :], w_hi_t[slot][:, :]).then_inc(w_ok[slot], 1)
                pool.wait_ge(w_ok[slot], w_count(c, slot, content))
                pool.sem_inc(raw_free[r], 1)

            def split_head(c, part, which, of):
                for j, s in enumerate(HEAD_ORDER):
                    if s in which:
                        split(c, part, j, s, CONTENTS[s] * of)

            def hidden(c, fill, at):
                pool.wait_ge(h_hi_ok, c * 6 + fill + 1)
                lo(h_lo[:, at, :], h_f[:, fill % 2, :], h_hi[:, at, :]).then_inc(h_ok, 1)

            def probs_lo(group):
                pool.wait_ge(p_hi_ok, group + 1)
                for b in range(4):
                    rows = slice(T * b, T * b + T)
                    lo(p_lo[rows, :, b, :], pT[rows, :, :], p_hi[rows, :, b, :]).then_inc(p_ok, 1)
                pool.wait_ge(p_ok, group * 4 + 4)

            for primed in raw_free + [o2_lo_ok]:
                pool.sem_inc(primed, PRIMED)
            def lo_block(i, a, src, count):
                pool.wait_ge(act_hi_ok[i], count + a + 1)
                lo(act_lo[i][:, a, :], src, act_hi[i][:, a, :]).then_inc(act_ok[i][a], 1)

            def take_next(c):
                for a in (0, 2):
                    lo_block(0, a, x_next[a], c * 8)

            take_next(0)
            split_head(0, "prologue", HEAD_ORDER, 0)
            pool.wait_ge(zeroed, 2)
            with pool.Fori(0, CHUNKS) as c:
                for j in range(3):
                    hidden(c, j, j)

                def step(k):
                    def qk_lo(name, dst, hi):
                        pool.wait_ge(qk_hi_ok, step_of(c, k) * 5 + QK[name] + 1)
                        lo(dst, roped[:, QK[name] % 2, :], hi).then_inc(qk_ok, 1)

                    qk_lo("k", k_lo[:, :], k_hi[:, :])
                    split(c, "step", 0, 0, k + 1, k)
                    split(c, "step", 1, 1, k + 1, k)
                    for g in range(GROUP):
                        qk_lo(f"q{g}", q_lo[:, g, :], q_hi[:, g, :])
                        split(c, "step", 2 + g, 2 + g, k + 1, k)
                    for j in range(6, SLOTS):
                        s = STEP_ORDER[j]
                        if j == SLOTS - 1:
                            probs_lo(soft(c, k))
                        split(c, "step", j, s, k + WO_FIRST[s], k)

                step(0)
                with pool.Fori(1, KVH) as k:
                    step(k)
                def split_epi(j):
                    split(c, "epi", j, EPI_ORDER[j], KVH + WO_FIRST[EPI_ORDER[j]])

                split_epi(0)
                hidden(c, 3, 0)
                for j in range(KC):
                    if j % 2 == 0:
                        lo_block(1, j, y_acc[:, j, :], c * 8)
                    split_epi(1 + j)

                def split_b(s, hb):
                    split(c, "b", s, s, hb + QKV2_FIRST + 1, hb)

                def head_block(hb, last=False):
                    probs_lo(soft(c, hb * 2 + 8))
                    if not last:
                        split_b(0, hb + 1)
                        split_b(1, hb + 1)
                    probs_lo(soft(c, hb * 2 + 9))
                    if not last:
                        split_b(2, hb + 1)
                    pool.wait_ge(o2_hi_ok, c * KC + hb + 1)
                    at = slice(hb, hb + 1) if last else bass.ds(hb, 1)
                    lo(o_lo[:, at, :], o2_f.unsqueeze(1), o_hi[:, at, :]).then_inc(o2_lo_ok, 1)
                    pool.wait_ge(o2_lo_ok, c * KC + hb + 1 + PRIMED)

                for s in range(3):
                    split_b(s, 0)
                with pool.Fori(0, KC - 1) as hb:
                    head_block(hb)
                head_block(KC - 1, True)
                for j in (0, 2):
                    lo_block(0, j, x_res[:, j, :], c * 8 + KC)
                for j, (s, content) in enumerate(MID_PIECES):
                    split(c, "mid", j, s, content)
                hidden(c, 4, 1)
                take_next(c + 1)
                split_head(c, "head", HEAD_ORDER[:4], 1)
                hidden(c, 5, 2)
                split_head(c, "head", HEAD_ORDER[4:], 1)


def weight_stream(a):
    out = np.zeros((sum(CONTENTS), P, 5, P), np.float32)

    def put(slot, content, blocks, at=0):
        out[SLOT_BASE[slot] + content, :, at:at + len(blocks)] = np.transpose(blocks, (1, 0, 2))

    def rows(w, cols):
        return w[:, cols].reshape(-1, P, P)

    up = {n: a["L0_cond_b" + n].reshape(E * R, -1) for n in "qkvo"}
    down = {n: np.transpose(a["L0_cond_a" + n], (1, 0, 2)).reshape(-1, E * R) for n in "qkvo"}
    for s, n in zip(LORA_A_SLOTS, "kvq"):
        put(s, 0, rows(down[n], slice(None)))
    for k in range(KVH):
        for slot, n, h in [(0, "k", k), (1, "v", k)] + [(2 + g, "q", k * GROUP + g) for g in range(GROUP)]:
            cols = slice(h * HD, (h + 1) * HD)
            put(slot, k, rows(a["L0_cond_w" + n], cols))
            put(slot, k, up[n][None, :, cols], KC)
        mine = slice(k * GROUP * HD, (k + 1) * GROUP * HD)
        for j in range(KC):
            put(6 + j, k + WO_FIRST[6 + j], rows(a["L0_cond_wo"][mine], slice(j * P, (j + 1) * P)))
        put(10, k + WO_FIRST[10], rows(down["o"][mine], slice(None)))
    put(*BO_PIECE, up["o"].reshape(P, KC, P).transpose(1, 0, 2))
    for hb in range(KC):
        for s, n in enumerate("qkv"):
            put(s, QKV2_FIRST + hb, rows(a["L0_attn_w_" + n].T, slice(hb * P, (hb + 1) * P)))
    for j, (s, content) in enumerate(OUT2_PIECES):
        put(s, content, rows(a["L0_attn_w_o"].T, slice(j * P, (j + 1) * P)))
    layers = [("L0_cond2_W", "L0_cond2_Wr", "L0_cond2_A", "L0_cond2_B"),
              ("L0_ffn_W_base", "L0_ffn_W_router", "L0_ffn_A_stack", "L0_ffn_B_stack")]
    for (wb, wr, wa, wu), ((sa, ca), pieces) in zip(layers, ROUTED):
        put(sa, ca, rows(a[wa].reshape(E * R, DM).T, slice(None)))
        router = a[wr].T.reshape(KC, P, E).transpose(1, 0, 2)
        out[SLOT_BASE[sa] + ca, :, KC, 0:KC * E] = router.reshape(P, KC * E)
        up2 = np.transpose(a[wu], (0, 2, 1)).reshape(E * R, DM)
        for j, (s, content) in enumerate(pieces):
            cols = slice(j * P, (j + 1) * P)
            put(s, content, rows(a[wb].T, cols))
            put(s, content, up2[None, :, cols], KC)
    return out.reshape(-1, P, PIECE)


def layouts(a):
    x = a["x"].reshape(CHUNKS, CT, KC, P).transpose(0, 3, 2, 1).reshape(CHUNKS, P, KC * CT)

    def over_partitions(v):
        return np.broadcast_to(v.reshape(CHUNKS, 1, CT), (CHUNKS, P, CT))

    def one_more(v):
        return np.concatenate([v, v[:1]])

    idx = a["itok_B_0_7"]
    idx_tok = np.repeat(idx, T)
    m = a["mask_BxS_bf1"].view(np.uint8).reshape(CHUNKS, TILES, 4, 1, T)
    m = np.broadcast_to(m, (CHUNKS, TILES, 4, T, T)).transpose(0, 2, 3, 1, 4).reshape(CHUNKS, P, TILES * T)
    return {
        "xT": one_more(x),
        "pos": one_more(over_partitions(a["pos_BxS"])),
        "idx": one_more(over_partitions(idx_tok)),
        "idx_tile": one_more(idx_tok.reshape(CHUNKS, TILES, P).transpose(0, 2, 1)),
        "mask": one_more(m),
        "bias": a["L0_ffn_b_base"].reshape(KC, P).T,
        "consts": constants(),
        "stream": weight_stream(a),
    }


def kernel(**inputs):
    from concourse import bacc
    from concourse.bass_utils import run_bass_kernel_spmd

    a = {n: np.asarray(v) for n, v in inputs.items()}
    nc = bacc.Bacc("TRN2", target_bir_lowering=False, num_devices=1)
    arrays, args = {}, {}
    for name, v in layouts(a).items():
        v = np.ascontiguousarray(v)
        arrays[f"in_{name}"] = v
        args[name] = nc.dram_tensor(f"in_{name}", v.shape, mybir.dt.from_np(v.dtype), kind="ExternalInput").ap()
    args["outT"] = nc.dram_tensor("out_T", (CHUNKS, P, KC * CT), F32, kind="ExternalOutput").ap()
    build(nc, **args)
    r = run_bass_kernel_spmd(nc, [arrays], core_ids=[0])
    got = r.results[0]["out_T"].reshape(CHUNKS, P, KC, CT).transpose(0, 3, 2, 1)
    return np.ascontiguousarray(got.reshape(B, T, DM))
```

```python
from contextlib import ExitStack

import numpy as np
import concourse.bass as bass
from concourse import mybir

ALU = mybir.AluOpType
ACT = mybir.ActivationFunctionType
AX = mybir.AxisListType
F32 = mybir.dt.float32
F32R = mybir.dt.float32r
I32 = mybir.dt.int32
U8 = mybir.dt.uint8

B, T, DM = 64, 32, 512
TOKENS = B * T
P = 128
CT = 512
CHUNKS = TOKENS // CT
TILES = CT // P
KC = DM // P
KVH, GROUP, HD = 8, 4, 128
E, R = 8, 16
HEADS2, HD2 = 32, 16
THETA = 500000.0
LANG_BIAS, SCALING = 5.0, 2.0
FLT_MAX = 3.4028234663852886e38
PIECE = 5 * P

SLOTS = 11
RAWS = 3
PRIMED = 1
CONTENTS = [13, 13, 13, 10, 10, 10, 9, 9, 10, 10, 11]
SLOT_BASE = [sum(CONTENTS[:s]) for s in range(SLOTS)]
LORA_A_SLOTS = [8, 9, 10]
WO_FIRST = {6: 0, 7: 0, 8: 1, 9: 1, 10: 1}
QKV2_FIRST = 8
OUT2_PIECES = [(3, 8), (4, 8), (5, 8), (7, 8)]
BO_PIECE = (10, 9)
ROUTED = [
    ((8, 9), [(9, 9), (6, 8), (0, 12), (1, 12)]),
    ((2, 12), [(3, 9), (4, 9), (5, 9), (10, 10)]),
]
HEAD_ORDER = [8, 9, 0, 1, 10, 2, 3, 4, 5]
LATE = 7
STEP_ORDER = [0, 1, 2, 3, 4, 5, 10, 6, 7, 8, 9]
EPI_ORDER = [10, 6, 7, 8, 9]
MID_PIECES = [(3, 9), (4, 9), (5, 9), (10, 10)]

def _per_raw(n):
    return [len(range(r, n, RAWS)) for r in range(RAWS)]


RAW_HEAD, RAW_STEP, RAW_EPI, RAW_B, RAW_MID = map(_per_raw, (9, SLOTS, 5, 3, 4))
RAW_CHUNK = [8 * s + e + 4 * b + m + h
             for s, e, b, m, h in zip(RAW_STEP, RAW_EPI, RAW_B, RAW_MID, RAW_HEAD)]


def raw_use(c, part, j, k=0):
    r = j % RAWS
    before = j // RAWS
    if part == "prologue":
        return r, before
    if part == "late":
        return r, before + c * RAW_CHUNK[r]
    n = before + RAW_HEAD[r] + c * RAW_CHUNK[r]
    if part == "step":
        return r, n + k * RAW_STEP[r]
    n = n + KVH * RAW_STEP[r]
    if part == "epi":
        return r, n
    n = n + RAW_EPI[r]
    if part == "b":
        return r, n + k * RAW_B[r]
    n = n + KC * RAW_B[r]
    if part == "mid":
        return r, n
    return r, n + RAW_MID[r]


PROJ = {"k": (0, 0), "v": (1, 0), "q0": (2, 0), "q1": (3, 0), "q2": (0, 1), "q3": (1, 1), "vT": (2, 1)}
WOUT = {"ho": (3, 0), "y0": (0, 0), "y1": (1, 0), "y2": (2, 0), "y3": (3, 1)}
N_LORA, N_PROJ, N_WO, N_ROUTE = [1, 1, 1, 0], [2, 2, 2, 1], [1, 1, 1, 2], [1, 1, 1, 1]
RING_CHUNK = [a + KVH * (b + w) + KC + 1 + 2 * r
              for a, b, w, r in zip(N_LORA, N_PROJ, N_WO, N_ROUTE)]


def ring_use(c, part, which, k=0):
    if part == "proj":
        b, at = PROJ[which]
        done = 0 if isinstance(k, int) and k == 0 else k - 1
        n = k * N_PROJ[b] + done * N_WO[b] + at + N_LORA[b]
    elif part == "wo":
        b, at = WOUT[which]
        n = (KVH if isinstance(k, int) and k == KVH else k + 1) * N_PROJ[b] + (k - 1) * N_WO[b] + at + N_LORA[b]
    elif part == "lora":
        b, n = which, 0
    else:
        b = which
        n = N_LORA[b] + KVH * (N_PROJ[b] + N_WO[b])
        if part == "b":
            n = n + k
        else:
            n = n + KC
            if part == "route":
                n = n + 1 + k * N_ROUTE[b]
    return b, n + c * RING_CHUNK[b]


C_FREQ, C_SIGN, C_EID, C_EVEN, C_ODD = range(5)
C_HM = 5
C_TIE = 13
C_E = 21
C_CAUSAL = 29
C_IDENT = 61
C_COLS = C_IDENT + P


def constants():
    p = np.arange(P)
    half = HD // 2
    c = np.zeros((P, C_COLS), np.float32)
    freq = np.float32(THETA) ** (-np.arange(half, dtype=np.float32) / np.float32(half))
    c[:, C_FREQ] = freq[p % half]
    c[:, C_SIGN] = np.where(p < half, -1.0, 1.0)
    c[:, C_EID] = p // R
    c[:, C_EVEN] = (p // HD2) % 2 == 0
    c[:, C_ODD] = (p // HD2) % 2 == 1
    c[:, C_HM:C_HM + 8] = ((p // HD2) % 2 * GROUP + p // T)[:, None] == np.arange(8)
    c[:, C_TIE:C_TIE + 8] = 8 - np.arange(8)
    c[:, C_E:C_E + 8] = np.arange(8)
    c[:, C_CAUSAL:C_CAUSAL + T] = (p % T)[:, None] >= np.arange(T)
    c[:, C_IDENT:] = np.eye(P)
    return c


TWO_PI = 2 * np.pi
ROUND = 1.5 * 2.0 ** 23
PI_A = 6.28125
PI_B = float(np.float32(np.float32((TWO_PI - PI_A) * 2 ** 20).astype(np.int64) / 2 ** 20))
PI_C = float(np.float32(TWO_PI - PI_A - PI_B))
PI_IN = 3.1415925

N_TABLE = 11
N_ROUTING = 17


class Chain:

    def __init__(self, eng, sem, base):
        self.eng, self.sem, self.base, self.n = eng, sem, base, 0

    def then(self, ins):
        ins.then_inc(self.sem, 1)
        self.n += 1
        self.eng.wait_ge(self.sem, self.base + self.n)


def build(nc, xT, pos, idx, idx_tile, mask, bias, consts, stream, outT):
    with ExitStack() as ctx:
        def sb(name, shape, dt=F32):
            return ctx.enter_context(nc.sbuf_tensor(name, shape, dt))

        def sem(name):
            return ctx.enter_context(nc.semaphore(name))

        w_hi_t = [sb(f"w_hi{s}", [P, PIECE], F32R) for s in range(SLOTS)]
        w_lo_t = [sb(f"w_lo{s}", [P, PIECE], F32R) for s in range(SLOTS)]
        raw = [sb(f"raw{r}", [P, PIECE]) for r in range(RAWS)]
        act_hi = [sb(f"act_hi{i}", [P, KC, CT], F32R) for i in range(2)]
        act_lo = [sb(f"act_lo{i}", [P, KC, CT], F32R) for i in range(2)]
        q_hi, q_lo = sb("q_hi", [P, GROUP, CT], F32R), sb("q_lo", [P, GROUP, CT], F32R)
        k_hi, k_lo = sb("k_hi", [P, CT], F32R), sb("k_lo", [P, CT], F32R)
        v_hi, v_lo = sb("v_hi", [P, TILES, P], F32R), sb("v_lo", [P, TILES, P], F32R)
        p_hi, p_lo = sb("p_hi", [P, TILES * GROUP, 4, T], F32R), sb("p_lo", [P, TILES * GROUP, 4, T], F32R)
        o_hi, o_lo = sb("o_hi", [P, GROUP, CT], F32R), sb("o_lo", [P, GROUP, CT], F32R)
        h_hi, h_lo = sb("h_hi", [P, 3, CT], F32R), sb("h_lo", [P, 3, CT], F32R)
        x_res = sb("x_res", [P, KC, CT])
        y_acc = sb("y_acc", [P, KC + 1, CT])
        cos_t, sin_t = sb("cos_t", [P, CT]), sb("sin_t", [P, CT])
        own = sb("own", [P, CT])
        r_cos, r_sin = sb("r_cos", [P, 2, CT]), sb("r_sin", [P, 2, CT])
        roped = r_cos
        q2_hi, q2_lo = r_cos[:, 0, :], r_cos[:, 1, :]
        quad_out = r_sin
        x_next = [r_cos[:, 0, :], r_cos[:, 1, :], r_sin[:, 0, :], r_sin[:, 1, :]]
        h_f = sb("h_f", [P, 2, CT])
        v_f = h_f[:, 0, :]
        o2_f = h_f[:, 1, :]
        table_in = sb("table_in", [P, 1])
        sT = sb("sT", [P, TILES * GROUP, T])
        sc = sb("sc", [P, TILES * GROUP, T])
        pT = sb("pT", [P, TILES * GROUP, T])
        pos_i = pT[:, :, :].rearrange("p a b -> p (a b)").bitcast(I32)
        idx_i = sc[:, :, :].rearrange("p a b -> p (a b)").bitcast(I32)
        s_max, s_sum, s_inv = (sb(n, [P, TILES * GROUP]) for n in ("s_max", "s_sum", "s_inv"))
        mask_u = sb("mask_u", [P, TILES, T], U8)
        mask_f = sb("mask_f", [P, TILES, T])
        cst = sb("cst", [P, C_COLS])
        ffn_b = sb("ffn_b", [P, KC])
        idx_ti = sb("idx_ti", [P, TILES], I32)
        idx_tf = sb("idx_tf", [P, TILES])
        lang = sb("lang", [P, TILES, E])
        rt = {n: sb("rt_" + n, [P, TILES, E]) for n in ("l", "eq", "one", "l2", "two", "gate")}
        rs = {n: sb("rs_" + n, [P, TILES]) for n in ("m1", "m2", "c", "d", "e", "s", "w1", "w2")}
        gate_x, gate_t = sT[:, :, :].rearrange("p a (e r) -> p (a e) r", e=2)\
            .rearrange("p (a e) r -> p a e r", a=TILES), pT[:, :, :].rearrange("p a b -> p (a b)")

        ring = [ctx.enter_context(nc.psum_tensor(f"ring{b}", [P, CT], F32)) for b in range(4)]
        att = ctx.enter_context(nc.psum_tensor("att", [P, TILES, CT], F32))

        ring_full = [sem(f"ring_full{b}") for b in range(4)]
        ring_free = [sem(f"ring_free{b}") for b in range(4)]
        raw_full = [sem(f"raw_full{r}") for r in range(RAWS)]
        raw_free = [sem(f"raw_free{r}") for r in range(RAWS)]
        w_hi_ok = [sem(f"w_hi_ok{s}") for s in range(SLOTS)]
        w_ok = [sem(f"w_ok{s}") for s in range(SLOTS)]
        ld_const, ld_x, ld_pos, ld_idx = (sem(n) for n in ("ld_const", "ld_x", "ld_pos", "ld_idx"))
        ld_mask, ld_tile, ld_res, stored = (sem(n) for n in ("ld_mask", "ld_tile", "ld_res", "stored"))
        act_hi_ok = [sem(f"act_hi_ok{i}") for i in range(2)]
        act_ok = [[sem(f"act_ok{i}{a}") for a in range(KC)] for i in range(2)]
        own_ok, y_zero, table, masking, zeroed, trig_ok, table_loaded = (
            sem(n) for n in ("own_ok", "y_zero", "table", "masking", "zeroed", "trig_ok", "table_loaded"))
        h_f_ok, h_hi_ok, h_ok = (sem(n) for n in ("h_f_ok", "h_hi_ok", "h_ok"))
        rope_part, rope_sum, qk_hi_ok, qk_ok = (sem(n) for n in ("rope_part", "rope_sum", "qk_hi_ok", "qk_ok"))
        v_hi_ok, s_full, s_evac, smax, exp_ok = (sem(n) for n in ("v_hi_ok", "s_full", "s_evac", "smax", "exp_ok"))
        p_hi_ok, p_ok, pv_full, o_hi_ok, o_ok = (sem(n) for n in ("p_hi_ok", "p_ok", "pv_full", "o_hi_ok", "o_ok"))
        q2_hi_ok, k2_hi_ok, qx_ok = (sem(n) for n in ("q2_hi_ok", "k2_hi_ok", "qx_ok"))
        pv2_full, o2_sum, o2_ok, o2_hi_ok, o2_lo_ok = (sem(n) for n in ("pv2_full", "o2_sum", "o2_ok", "o2_hi_ok", "o2_lo_ok"))
        routing, gating, route_exp, gate_ok, base_full, f_sum = (sem(n) for n in ("routing", "gating", "route_exp", "gate_ok", "base_full", "f_sum"))

        ident = cst[:, C_IDENT:C_IDENT + P]
        QK = {"k": 0, "q0": 1, "q1": 2, "q2": 3, "q3": 4}

        def f(ap):
            return ap.bitcast(F32)

        def w_count(c, s, content):
            return c * CONTENTS[s] + (content + 1)

        def step_of(c, k):
            return c * KVH + k

        def soft(c, group):
            return c * 16 + group

        block = ctx.enter_context(nc.Block())

        @block.sync
        def _(sp):
            def load(c, part, j, slot, content, k=0):
                r, n = raw_use(c, part, j, k)
                sp.wait_ge(raw_free[r], n + PRIMED)
                src = stream[bass.ds(content + SLOT_BASE[slot], 1)].rearrange("o p n -> (o p) n")
                sp.dma_start(raw[r][:, :], src).then_inc(raw_full[r], 16)

            def load_head(c, part, pieces=range(len(HEAD_ORDER))):
                for j in pieces:
                    load(c, part, j, HEAD_ORDER[j], 0)

            sp.dma_start(cst[:, :], consts).then_inc(ld_const, 16)
            sp.dma_start(ffn_b[:, :], bias).then_inc(ld_const, 16)

            def chunk_of(dram, c):
                return dram[bass.ds(c, 1)].rearrange("o p n -> (o p) n")

            def load_next(c):
                for a in range(KC):
                    sp.dma_start(x_next[a], chunk_of(xT, c)[:, a * CT:(a + 1) * CT]).then_inc(ld_x, 16)
                sp.dma_start(idx_i, chunk_of(idx, c)).then_inc(ld_idx, 16)
                sp.dma_start(mask_u[:, :, :].rearrange("p a t -> p (a t)"), chunk_of(mask, c)).then_inc(ld_mask, 16)
                sp.dma_start(idx_ti[:, :], chunk_of(idx_tile, c)).then_inc(ld_tile, 16)

            sp.sem_inc(stored, 16 * PRIMED)
            load_next(0)
            sp.dma_start(pos_i, chunk_of(pos, 0)).then_inc(ld_pos, 16)
            load_head(0, "prologue")
            with sp.Fori(0, CHUNKS) as c:
                sp.wait_ge(f_sum, c * KC + PRIMED)
                sp.dma_start(x_res[:, :, :].rearrange("p a t -> p (a t)"), chunk_of(xT, c)).then_inc(ld_res, 16)

                def step(k):
                    for j, s in enumerate(STEP_ORDER):
                        load(c, "step", j, s, k + WO_FIRST[s] if s in WO_FIRST else k + 1, k)

                step(0)
                with sp.Fori(1, KVH) as k:
                    step(k)
                for j, s in enumerate(EPI_ORDER):
                    load(c, "epi", j, s, KVH + WO_FIRST[s])
                with sp.Fori(0, KC) as hb:
                    for s in range(3):
                        load(c, "b", s, s, hb + QKV2_FIRST + 1, hb)
                for j, (s, content) in enumerate(MID_PIECES):
                    load(c, "mid", j, s, content)
                for a in range(KC):
                    sp.wait_ge(act_ok[0][a], c * 2 + 2)
                load_next(c + 1)
                load_head(c, "head", range(6))
                sp.wait_ge(h_f_ok, c * 6 + 6)
                sp.dma_start(pos_i, chunk_of(pos, c + 1)).then_inc(ld_pos, 16)
                load_head(c, "head", range(6, len(HEAD_ORDER)))
                sp.wait_ge(f_sum, c * KC + KC + PRIMED)
                sp.dma_start(outT[bass.ds(c, 1)].rearrange("o p n -> (o p) n"),
                             y_acc[:, 0:KC, :].rearrange("p a t -> p (a t)")).then_inc(stored, 16)
            sp.wait_ge(stored, 16 * (CHUNKS + PRIMED))

        @block.tensor
        def _(pe):
            def three(out, w, x, start, stop):
                nc.tensor.matmul(out, w[0], x[0], start=start, stop=False)
                nc.tensor.matmul(out, w[1], x[0], start=False, stop=False)
                return nc.tensor.matmul(out, w[0], x[1], start=False, stop=stop)

            def w(s, a, n=P):
                return w_hi_t[s][:, a:a + n], w_lo_t[s][:, a:a + n]

            def open_bank(use):
                b, n = use
                pe.wait_ge(ring_free[b], n + PRIMED)
                return ring[b]

            def weights(c, s, content):
                pe.wait_ge(w_ok[s], w_count(c, s, content))

            def block_of(out, s, x, start=True, stop=True, part=range(KC), ready=None):
                for a in part:
                    if ready:
                        pe.wait_ge(ready[0][a], ready[1])
                    last = three(out, w(s, a * P), (x[0][:, a, :], x[1][:, a, :]),
                                 start and a == 0, stop and a == KC - 1)
                return last

            def scores_and(kh, kl, count):
                for t in range(TILES):
                    cols = slice(t * P, (t + 1) * P)
                    last = three(att[:, t, :], (kh[:, cols], kl[:, cols]),
                                 (q_hi[:, :, cols], q_lo[:, :, cols]), True, True)
                last.then_inc(s_full, 1)

            def values(t):
                cols = slice(t * GROUP, (t + 1) * GROUP)
                return three(att[:, t, :], (v_hi[:, t, :], v_lo[:, t, :]),
                             (p_hi[:, cols, :, :], p_lo[:, cols, :, :]), True, True)

            def turn_v(use):
                out = open_bank(use)
                for t in range(TILES):
                    last = nc.tensor.transpose(out[:, t * P:(t + 1) * P], v_f[:, t * P:(t + 1) * P], ident)
                last.then_inc(ring_full[use[0]], 1)

            def wo_block(c, k, name):
                j = int(name[1]) if name != "ho" else 4
                s = 6 + j
                use = ring_use(c, "wo", name, k)
                out = open_bank(use)
                weights(c, s, k - 1 + WO_FIRST[s])
                block_of(out[:, :], s, (o_hi, o_lo)).then_inc(ring_full[use[0]], 1)

            def pv(c, k):
                pe.wait_ge(p_ok, soft(c, k) * 4)
                pe.wait_ge(s_evac, soft(c, k) * 4)
                b, n = ring_use(c, "proj", "vT", k - 1)
                pe.wait_ge(ring_free[b], n + 1 + PRIMED)
                for t in range(TILES):
                    values(t).then_inc(pv_full, 1)

            pe.wait_ge(ld_const, 32)
            pe.wait_ge(zeroed, 2)
            with pe.Fori(0, CHUNKS) as c:
                for j, s in enumerate(LORA_A_SLOTS):
                    use = ring_use(c, "lora", j)
                    out = open_bank(use)
                    weights(c, s, 0)
                    block_of(out[:, :], s, (act_hi[0], act_lo[0]), ready=j == 0 and (act_ok[0], c * 2 + 1))\
                        .then_inc(ring_full[use[0]], 1)

                def proj(k, name, slot, lora):
                    use = ring_use(c, "proj", name, k)
                    out = open_bank(use)
                    weights(c, slot, k)
                    block_of(out[:, :], slot, (act_hi[0], act_lo[0]), stop=False)
                    pe.wait_ge(h_ok, c * 6 + lora + 1)
                    three(out[:, :], w(slot, KC * P), (h_hi[:, lora, :], h_lo[:, lora, :]),
                          False, True).then_inc(ring_full[use[0]], 1)

                def step(k, first=False, last=False):
                    proj(k, "v", 1, 1)
                    proj(k, "q0", 2, 2)
                    proj(k, "q1", 3, 2)
                    if not first:
                        pv(c, k)
                    proj(k, "q2", 4, 2)
                    proj(k, "q3", 5, 2)
                    b, n = ring_use(c, "proj", "v", k)
                    pe.wait_ge(ring_free[b], n + 1 + PRIMED)
                    turn_v(ring_use(c, "proj", "vT", k))
                    if not first:
                        pe.wait_ge(o_ok, (step_of(c, k)) * TILES)
                        wo_block(c, k, "y0")
                        wo_block(c, k, "ho")
                    if not last:
                        proj(k + 1, "k", 0, 0)
                    pe.wait_ge(qk_ok, step_of(c, k) * 5 + 5)
                    scores_and(k_hi, k_lo, None)
                    if not first:
                        wo_block(c, k, "y1")
                        wo_block(c, k, "y2")
                        wo_block(c, k, "y3")

                proj(0, "k", 0, 0)
                step(0, True)
                with pe.Fori(1, KVH - 1) as k:
                    step(k)
                step(KVH - 1, last=True)
                pv(c, KVH)
                pe.wait_ge(o_ok, (step_of(c, KVH)) * TILES)
                wo_block(c, KVH, "ho")

                def up(j):
                    b, _ = ring_use(c, "wo", f"y{j}", KVH)
                    three(ring[b][:, :], w(BO_PIECE[0], j * P), (h_hi[:, 0, :], h_lo[:, 0, :]), False, True)\
                        .then_inc(ring_full[b], 1)

                for j in range(KC):
                    out = open_bank(ring_use(c, "wo", f"y{j}", KVH))
                    weights(c, 6 + j, KVH - 1 + WO_FIRST[6 + j])
                    block_of(out[:, :], 6 + j, (o_hi, o_lo), stop=False)
                    if j == 1:
                        weights(c, *BO_PIECE)
                        pe.wait_ge(h_ok, c * 6 + 4)
                    if j:
                        up(j - 1)
                up(KC - 1)

                def proj2(s, hb, ready=None):
                    use = ring_use(c, "b", s, hb)
                    out = open_bank(use)
                    weights(c, s, hb + QKV2_FIRST)
                    block_of(out[:, :], s, (act_hi[1], act_lo[1]), ready=ready).then_inc(ring_full[use[0]], 1)

                def scores2(hb, q, first=False):
                    quad = (c * KC + hb) * 2 + q
                    b, n = ring_use(c, "b", 1, hb)
                    pe.wait_ge(ring_free[b], n + 1 + PRIMED)
                    pe.wait_ge(qx_ok, (quad + 1) * 3)
                    pe.wait_ge(s_evac, soft(c, hb * 2 + 8 + q) * 4)
                    if not first:
                        pe.wait_ge(o2_ok, (quad - 1) * 4 + PRIMED)
                    scores_and(k_hi, k_lo, None)

                def values2(hb, q, last=False):
                    if q == 0:
                        b, n = ring_use(c, "b", 3, hb)
                        pe.wait_ge(ring_free[b], n + 1 + PRIMED)
                    pe.wait_ge(p_ok, soft(c, hb * 2 + 9 + q) * 4)
                    pe.wait_ge(s_evac, soft(c, hb * 2 + (9 if last else 10) + q) * 4)
                    if last:
                        pe.wait_ge(o2_ok, ((c * KC + hb) * 2 + q) * 4 + PRIMED)
                    for t in range(TILES):
                        ins = values(t)
                    ins.then_inc(pv2_full, 1)

                def turn_v2(hb):
                    b, n = ring_use(c, "b", 2, hb)
                    pe.wait_ge(ring_free[b], n + 1 + PRIMED)
                    turn_v(ring_use(c, "b", 3, hb))

                def out2(a, blocks=range(KC)):
                    pe.wait_ge(o2_lo_ok, c * KC + a + 1 + PRIMED)
                    for j in blocks:
                        s, content = OUT2_PIECES[j]
                        use = ring_use(c, "out2", j)
                        if a == 0:
                            open_bank(use)
                            weights(c, s, content)
                        ins = block_of(ring[use[0]][:, :], s, (o_hi, o_lo), part=(a,))
                        if a == KC - 1:
                            ins.then_inc(ring_full[use[0]], 1)

                def head_block(hb, last=False):
                    if last:
                        out2(0, range(3))
                    else:
                        proj2(0, hb + 1)
                    scores2(hb, 1)
                    if last:
                        out2(0, (3,))
                        out2(1)
                    else:
                        proj2(1, hb + 1)
                    values2(hb, 0)
                    if last:
                        out2(2)
                    else:
                        proj2(2, hb + 1)
                        scores2(hb + 1, 0)
                        turn_v2(hb + 1)
                    values2(hb, 1, last)

                proj2(0, 0, (act_ok[1], c * 2 + 1))
                proj2(1, 0)
                proj2(2, 0)
                scores2(0, 0, True)
                turn_v2(0)
                with pe.Fori(0, KC - 1) as hb:
                    head_block(hb)
                head_block(KC - 1, True)

                out2(KC - 1)

                for layer, ((sa, ca), pieces) in enumerate(ROUTED):
                    x = act_hi[layer], act_lo[layer]
                    weights(c, sa, ca)
                    use = ring_use(c, "route", 0, layer)
                    out = open_bank(use)
                    for a in range(KC):
                        pe.wait_ge(act_ok[layer][a], c * 2 + 2)
                        last = three(out[:, :], w(sa, KC * P + (a + 1) * E - P),
                                     (x[0][:, a, :], x[1][:, a, :]), a == 0, a == KC - 1)
                    last.then_inc(ring_full[use[0]], 1)
                    logits_sb = use
                    use = ring_use(c, "route", 1, layer)
                    out = open_bank(use)
                    block_of(out[:, :], sa, x).then_inc(ring_full[use[0]], 1)

                    def turn(which, src):
                        use = ring_use(c, "route", which, layer)
                        out = open_bank(use)
                        for t in range(TILES):
                            last = nc.tensor.transpose(out[:, t * P:(t + 1) * P], src(t), ident)
                        last.then_inc(ring_full[use[0]], 1)

                    pe.wait_ge(ring_free[logits_sb[0]], logits_sb[1] + 1 + PRIMED)
                    turn(2, lambda t: h_f[:, 1 - layer, t * P:(t + 1) * P])
                    for j, (s, content) in enumerate(pieces):
                        if j == KC // 2:
                            pe.wait_ge(gate_ok, c * 2 + layer + 1)
                            turn(3, lambda t: gate_x[:, t, :, :].rearrange("p e r -> p (e r)"))
                        weights(c, s, content)
                        block_of(att[:, j, :], s, x, stop=False)
                    pe.wait_ge(h_ok, c * 6 + 5 + layer)
                    for j, (s, content) in enumerate(pieces):
                        three(att[:, j, :], w(s, KC * P), (h_hi[:, 1 + layer, :], h_lo[:, 1 + layer, :]),
                              False, True).then_inc(base_full, 1)

        @block.scalar
        def _(act):
            def copy(out, in_, scale=1.0):
                return nc.scalar.activation(out, in_, ACT.Copy, scale=scale)

            def load_table(function, count):
                nc.scalar.activation(table_in[:, :], cst[:, C_EVEN:C_EVEN + 1], function)\
                    .then_inc(table_loaded, 1)
                act.wait_ge(table_loaded, count)

            def split(c, part, j, slot, content, k=0):
                r, n = raw_use(c, part, j, k)
                act.wait_ge(raw_full[r], (n + 1) * 16)
                copy(w_hi_t[slot][:, :], raw[r][:, :]).then_inc(w_hi_ok[slot], 1)

            def split_head(c, part, which):
                for j, s in enumerate(HEAD_ORDER):
                    if s in which:
                        split(c, part, j, s, 0)

            def full(use):
                act.wait_ge(ring_full[use[0]], use[1] + 1)
                return ring[use[0]]

            def hidden(c, fill, at):
                act.wait_ge(h_f_ok, c * 6 + fill + 1)
                copy(h_hi[:, at, :], h_f[:, fill % 2, :]).then_inc(h_hi_ok, 1)

            def turned_v(use):
                out = full(use)
                copy(v_hi[:, :, :], out[:, :].rearrange("p (t d) -> p t d", t=TILES)).then_inc(v_hi_ok, 1)

            def scores_out(group):
                act.wait_ge(s_full, group + 1)
                for b in range(2):
                    rows = slice(T * b, T * b + T)
                    src = att[rows, :, :].rearrange("p a (g t) -> p (a g) t", g=GROUP)[:, :, T * b:T * b + T]
                    copy(sT[rows, :, :], src).then_inc(s_evac, 1)

            def exponent(group, scale):
                act.wait_ge(smax, group * 8 + 4)
                nc.scalar.activation(sc[:, :, :], sc[:, :, :], ACT.Exp, scale=scale).then_inc(exp_ok, 1)

            def probs_hi(group):
                act.wait_ge(smax, group * 8 + 8)
                for b in range(4):
                    rows = slice(T * b, T * b + T)
                    copy(p_hi[rows, :, b, :], pT[rows, :, :]).then_inc(p_hi_ok, 1)

            def take_next(c):
                for a in range(KC):
                    act.wait_ge(ld_x, (c * KC + KC) * 16)
                    copy(act_hi[0][:, a, :], x_next[a]).then_inc(act_hi_ok[0], 1)

            take_next(0)
            split_head(0, "prologue", HEAD_ORDER[:LATE])
            act.wait_ge(ld_const, 32)
            act.wait_ge(zeroed, 2)
            with act.Fori(0, CHUNKS) as c:
                load_table(ACT.Sin, c * 2 + 1)
                hidden(c, 0, 0)
                act.wait_ge(table, c * N_TABLE + N_TABLE)
                nc.scalar.activation(sin_t[:, :], r_sin[:, 0, :], ACT.Sin, scale=cst[:, C_SIGN:C_SIGN + 1])\
                    .then_inc(trig_ok, 1)
                nc.scalar.activation(cos_t[:, :], r_sin[:, 1, :], ACT.Sin).then_inc(trig_ok, 1)
                load_table(ACT.Exp, c * 2 + 2)
                for j in (1, 2):
                    hidden(c, j, j)
                split_head(c, "late", HEAD_ORDER[LATE:])

                def attention_out(k):
                    for t in range(TILES):
                        act.wait_ge(pv_full, step_of(c, k - 1) * TILES + t + 1)
                        copy(o_hi[:, :, t * P:(t + 1) * P],
                             att[:, t, :].rearrange("p (g n) -> p g n", g=GROUP)).then_inc(o_hi_ok, 1)

                def qk_out(k, name, dst):
                    act.wait_ge(rope_sum, step_of(c, k) * 5 + QK[name] + 1)
                    copy(dst, roped[:, QK[name] % 2, :]).then_inc(qk_hi_ok, 1)

                def step(k, first=False):
                    qk_out(k, "k", k_hi[:, :])
                    split(c, "step", 0, 0, k + 1, k)
                    use = ring_use(c, "proj", "v", k)
                    if first:
                        act.wait_ge(h_ok, c * 6 + 3)
                    copy(v_f, full(use)[:, :]).then_inc(ring_free[use[0]], 1)
                    split(c, "step", 1, 1, k + 1, k)
                    qk_out(k, "q0", q_hi[:, 0, :])
                    split(c, "step", 2, 2, k + 1, k)
                    qk_out(k, "q1", q_hi[:, 1, :])
                    if not first:
                        attention_out(k)
                    split(c, "step", 3, 3, k + 1, k)
                    qk_out(k, "q2", q_hi[:, 2, :])
                    split(c, "step", 4, 4, k + 1, k)
                    qk_out(k, "q3", q_hi[:, 3, :])
                    turned_v(ring_use(c, "proj", "vT", k))
                    split(c, "step", 5, 5, k + 1, k)
                    def next_wo(j, name):
                        if not first:
                            full(ring_use(c, "wo", name, k))
                        split(c, "step", j, STEP_ORDER[j], None, k)

                    next_wo(6, "ho")
                    next_wo(7, "y0")
                    group = soft(c, k)
                    scores_out(group)
                    if first:
                        next_wo(8, "y1")
                    exponent(group, HD ** -0.5)
                    if first:
                        next_wo(9, "y2")
                        next_wo(10, "y3")
                    else:
                        next_wo(8, "y1")
                    probs_hi(group)
                    if not first:
                        next_wo(9, "y2")
                        next_wo(10, "y3")

                step(0, True)
                with act.Fori(1, KVH) as k:
                    step(k)
                attention_out(KVH)
                full(ring_use(c, "wo", "ho", KVH))
                split(c, "epi", 0, EPI_ORDER[0], None)
                hidden(c, 3, 0)
                for j in range(KC):
                    b, n = ring_use(c, "wo", f"y{j}", KVH)
                    act.wait_ge(ring_free[b], n + 1 + PRIMED)
                    copy(act_hi[1][:, j, :], y_acc[:, j, :]).then_inc(act_hi_ok[1], 1)
                    split(c, "epi", 1 + j, EPI_ORDER[1 + j], None)

                def spread(q, heads=range(GROUP)):
                    for h in heads:
                        col = C_HM + GROUP * q + h
                        last = copy(q_hi[:, h, :], q2_hi, cst[:, col:col + 1])
                    if h == GROUP - 1:
                        last.then_inc(qx_ok, 1)

                def split_b(s, hb):
                    split(c, "b", s, s, None, hb)

                def take_q(hb):
                    use = ring_use(c, "b", 0, hb)
                    copy(q2_hi.bitcast(F32R), full(use)[:, :]).then_inc(q2_hi_ok, 1)

                def take_k(hb):
                    use = ring_use(c, "b", 1, hb)
                    copy(k_hi[:, :], full(use)[:, :]).then_inc(k2_hi_ok, 1)

                def spread_first(hb, heads):
                    act.wait_ge(q2_hi_ok, c * KC + hb + 1)
                    spread(0, heads)

                def take_v(hb):
                    use = ring_use(c, "b", 2, hb)
                    copy(v_f, full(use)[:, :]).then_inc(ring_free[use[0]], 1)

                def values_out(hb, q):
                    act.wait_ge(pv2_full, (c * KC + hb) * 2 + q + 1)
                    act.wait_ge(o2_sum, c * KC + hb + PRIMED)
                    for h in range(2):
                        rows = slice(T * h, T * h + T)
                        copy(quad_out[rows, q, :].rearrange("p (a n) -> p a n", a=TILES),
                             att[rows, :, h * P:(h + 1) * P], cst[rows, C_EVEN + q:C_EVEN + q + 1]).then_inc(o2_ok, 1)

                def head_block(hb, last=False):
                    quad = (c * KC + hb) * 2
                    group = soft(c, hb * 2 + 8)
                    turned_v(ring_use(c, "b", 3, hb))
                    if not last:
                        act.wait_ge(qx_ok, (quad + 2) * 3)
                        take_q(hb + 1)
                        split_b(0, hb + 1)
                    probs_hi(group)
                    scores_out(group + 1)
                    if not last:
                        take_k(hb + 1)
                        split_b(1, hb + 1)
                        spread_first(hb + 1, range(2))
                    exponent(group + 1, HD2 ** -0.5)
                    if not last:
                        spread(0, range(2, GROUP))
                    values_out(hb, 0)
                    if not last:
                        take_v(hb + 1)
                        split_b(2, hb + 1)
                    probs_hi(group + 1)
                    if not last:
                        scores_out(group + 2)
                        spread(1)
                        exponent(group + 2, HD2 ** -0.5)
                    values_out(hb, 1)
                    act.wait_ge(o2_sum, c * KC + hb + 1 + PRIMED)
                    copy(o_hi[:, hb:hb + 1, :] if last else o_hi[:, bass.ds(hb, 1), :],
                         o2_f.unsqueeze(1)).then_inc(o2_hi_ok, 1)

                take_q(0)
                spread_first(0, range(GROUP))
                take_k(0)
                split_b(0, 0)
                take_v(0)
                split_b(1, 0)
                split_b(2, 0)
                scores_out(soft(c, 8))
                spread(1)
                exponent(soft(c, 8), HD2 ** -0.5)
                with act.Fori(0, KC - 1) as hb:
                    head_block(hb)
                head_block(KC - 1, True)

                for j in range(KC):
                    b, n = ring_use(c, "out2", j)
                    act.wait_ge(ring_free[b], n + 1 + PRIMED)
                    copy(act_hi[0][:, j, :], x_res[:, j, :]).then_inc(act_hi_ok[0], 1)

                def split_mid(which):
                    for j in which:
                        split(c, "mid", j, *MID_PIECES[j])

                def routed(layer, while_choosing):
                    use = ring_use(c, "route", 0, layer)
                    copy(h_f[:, 1 - layer, :], full(use)[:, :]).then_inc(ring_free[use[0]], 1)
                    while_choosing()
                    act.wait_ge(routing, (c * 2 + layer) * N_ROUTING + 12)
                    nc.scalar.activation(rs["e"][:, :], rs["d"][:, :], ACT.Exp).then_inc(route_exp, 1)
                    use = ring_use(c, "route", 3, layer)
                    copy(gate_t, full(use)[:, :]).then_inc(ring_free[use[0]], 1)
                    hidden(c, 4 + layer, 1 + layer)

                split_mid(range(3))
                routed(0, lambda: split_mid((3,)))
                for j in range(KC):
                    act.wait_ge(base_full, c * 8 + j + 1)
                    copy(act_hi[1][:, j, :], att[:, j, :]).then_inc(act_hi_ok[1], 1)
                take_next(c + 1)
                split_head(c, "head", HEAD_ORDER[:2])
                routed(1, lambda: split_head(c, "head", HEAD_ORDER[2:4]))
                act.wait_ge(base_full, c * 8 + 8)
                split_head(c, "head", HEAD_ORDER[4:LATE])

        @block.vector
        def _(dve):
            tt, ts, stt = nc.vector.tensor_tensor, nc.vector.tensor_scalar, nc.vector.scalar_tensor_tensor

            def full(use):
                dve.wait_ge(ring_full[use[0]], use[1] + 1)
                return ring[use[0]]

            def take_scores(group, again=False):
                if again:
                    dve.wait_ge(smax, group * 8)
                dve.wait_ge(s_full, group + 1)
                for b in (2, 3):
                    rows = slice(T * b, T * b + T)
                    src = att[rows, :, :].rearrange("p a (g t) -> p a g t", g=GROUP)[:, :, :, T * b:T * b + T]
                    nc.vector.transpose(sc[rows, :, :].rearrange("p (a g) s -> p a g s", a=TILES), src)\
                        .then_inc(s_evac, 1)

            def softmax_first(group, masked):
                chain = Chain(dve, smax, group * 8)
                dve.wait_ge(s_evac, group * 4 + 4)
                half = slice(0, 2 * T)
                nc.vector.transpose(sc[half, :, :], sT[half, :, :]).then_inc(smax, 1 if masked else 2)
                dve.wait_ge(smax, group * 8 + (1 if masked else 2))
                chain.n = 1 if masked else 2
                if masked:
                    s4 = sc[:, :, :].rearrange("p (a g) s -> p a g s", a=TILES)
                    chain.then(tt(s4, s4, mask_f[:, :, :].unsqueeze(2).to_broadcast([P, TILES, GROUP, T]), ALU.add))
                chain.then(nc.vector.tensor_reduce(s_max[:, :], sc[:, :, :], AX.X, ALU.max))
                tt(sc[:, :, :], sc[:, :, :], s_max[:, :].unsqueeze(2).to_broadcast([P, TILES * GROUP, T]),
                   ALU.subtract).then_inc(smax, 1)

            def softmax_second(group):
                chain = Chain(dve, smax, group * 8 + 4)
                dve.wait_ge(exp_ok, group + 1)
                chain.then(nc.vector.tensor_reduce(s_sum[:, :], sc[:, :, :], AX.X, ALU.add))
                chain.then(nc.vector.reciprocal(s_inv[:, :], s_sum[:, :]))
                chain.then(tt(sc[:, :, :], sc[:, :, :], s_inv[:, :].unsqueeze(2).to_broadcast([P, TILES * GROUP, T]),
                              ALU.mult))
                nc.vector.transpose(pT[:, :, :], sc[:, :, :]).then_inc(smax, 1)

            def probs_lo(group):
                for b in (2, 3):
                    rows = slice(T * b, T * b + T)
                    dve.wait_ge(p_hi_ok, group * 4 + b + 1)
                    tt(p_lo[rows, :, b, :], pT[rows, :, :], f(p_hi[rows, :, b, :]), ALU.subtract).then_inc(p_ok, 1)

            def own_hidden(c, fill, src, gate, freed):
                if fill >= 2:
                    dve.wait_ge(h_ok, c * 6 + fill - 1)
                ins = tt(h_f[:, fill % 2, :], src, gate, ALU.mult)
                ins.then_inc(h_f_ok, 1)
                if freed is not None:
                    dve.wait_ge(h_f_ok, c * 6 + fill + 1)
                    dve.sem_inc(ring_free[freed], 1)

            for primed in ring_free + [f_sum, o2_ok, o2_sum]:
                dve.sem_inc(primed, PRIMED)
            for part in (p_hi, p_lo):
                nc.vector.memset(f(part[:, :, :, :]), 0.0).then_inc(zeroed, 1)
            dve.wait_ge(ld_const, 32)

            def lo_block(i, a, src, count):
                dve.wait_ge(act_hi_ok[i], count + a + 1)
                tt(act_lo[i][:, a, :], src, f(act_hi[i][:, a, :]), ALU.subtract).then_inc(act_ok[i][a], 1)

            def take_next(c):
                for a in (1, 3):
                    lo_block(0, a, x_next[a], c * 8)
                dve.wait_ge(ld_idx, (c + 1) * 16)
                ts(own[:, :], idx_i, cst[:, C_EID:C_EID + 1], None, ALU.is_equal).then_inc(own_ok, 1)

            take_next(0)
            with dve.Fori(0, CHUNKS) as c:
                def own_lora(j):
                    b, _ = use = ring_use(c, "lora", j)
                    own_hidden(c, j, full(use)[:, :], own[:, :], b)

                for a in (0, 2):
                    dve.wait_ge(act_ok[0][a], c * 2 + 1)
                chain = Chain(dve, table, c * N_TABLE)
                dve.wait_ge(ld_pos, (c + 1) * 16)
                ang, turns, cosa = r_cos[:, 0, :], r_cos[:, 1, :], r_sin[:, 1, :]
                chain.then(ts(ang, pos_i, cst[:, C_FREQ:C_FREQ + 1], None, ALU.mult))
                chain.then(ts(turns, ang, 1 / TWO_PI, ROUND, ALU.mult, ALU.add))
                chain.then(ts(turns, turns, -ROUND, None, ALU.add))
                dve.wait_ge(own_ok, c + 1)
                own_lora(0)
                for part in (PI_A, PI_B, PI_C):
                    chain.then(stt(out=ang, in0=turns, scalar=-part, in1=ang, op0=ALU.mult, op1=ALU.add))
                own_lora(1)
                chain.then(ts(r_sin[:, 0, :], ang, PI_IN, -PI_IN, ALU.min, ALU.max))
                chain.then(ts(ang, ang, float(np.pi / 2), None, ALU.add))
                chain.then(ts(turns, ang, float(np.pi), -TWO_PI, ALU.is_gt, ALU.mult))
                chain.then(tt(ang, ang, turns, ALU.add))
                chain.then(ts(cosa, ang, PI_IN, -PI_IN, ALU.min, ALU.max))
                assert chain.n == N_TABLE
                own_lora(2)
                chain = Chain(dve, masking, c * 4)
                dve.wait_ge(ld_mask, (c + 1) * 16)
                causal = cst[:, C_CAUSAL:C_CAUSAL + T].unsqueeze(1).to_broadcast([P, TILES, T])
                chain.then(tt(mask_f[:, :, :], mask_u[:, :, :], causal, ALU.mult))
                chain.then(ts(mask_f[:, :, :], mask_f[:, :, :], -1.0, FLT_MAX, ALU.add, ALU.mult))
                dve.wait_ge(ld_tile, (c + 1) * 16)
                chain.then(nc.vector.tensor_copy(idx_tf[:, :], idx_ti[:, :]))
                chain.then(tt(lang[:, :, :], cst[:, C_E:C_E + E].unsqueeze(1).to_broadcast([P, TILES, E]),
                              idx_tf[:, :].unsqueeze(2).to_broadcast([P, TILES, E]), ALU.is_equal))
                assert chain.n == 4
                dve.wait_ge(trig_ok, c * 2 + 2)

                def rope(k, name):
                    at = step_of(c, k) * 5 + QK[name]
                    half = QK[name] % 2
                    use = ring_use(c, "proj", name, k)
                    src = full(use)
                    if QK[name] >= 2:
                        dve.wait_ge(qk_ok, at - 1)
                    elif QK[name] == 1:
                        if not (isinstance(k, int) and k == 0):
                            dve.wait_ge(qk_ok, at - 1)
                    elif not (isinstance(k, int) and k == 0):
                        dve.wait_ge(qk_ok, at)
                    tt(r_cos[:, half, :], src[:, :], cos_t[:, :], ALU.mult).then_inc(rope_part, 1)
                    tt(r_sin[0:64, half, :], src[64:128, :], sin_t[0:64, :], ALU.mult).then_inc(rope_part, 1)
                    tt(r_sin[64:128, half, :], src[0:64, :], sin_t[64:128, :], ALU.mult).then_inc(ring_free[use[0]], 1)
                    dve.wait_ge(rope_part, at * 2 + 2)
                    dve.wait_ge(ring_free[use[0]], use[1] + 1 + PRIMED)
                    tt(roped[:, half, :], r_cos[:, half, :], r_sin[:, half, :], ALU.add).then_inc(rope_sum, 1)

                def attention_lo(k):
                    for t in range(TILES):
                        dve.wait_ge(o_hi_ok, step_of(c, k - 1) * TILES + t + 1)
                        cols = slice(t * P, (t + 1) * P)
                        tt(o_lo[:, :, cols], att[:, t, :].rearrange("p (g n) -> p g n", g=GROUP),
                           f(o_hi[:, :, cols]), ALU.subtract).then_inc(o_ok, 1)

                def add_y(k, name):
                    j = 4 if name == "ho" else int(name[1])
                    use = ring_use(c, "wo", name, k)
                    src = full(use)
                    tt(y_acc[:, j, :], src[:, :], y_acc[:, j, :], ALU.add).then_inc(ring_free[use[0]], 1)

                def turned_v_lo(use, count):
                    dve.wait_ge(v_hi_ok, count)
                    src = ring[use[0]][:, :].rearrange("p (t d) -> p t d", t=TILES)
                    tt(v_lo[:, :, :], src, f(v_hi[:, :, :]), ALU.subtract).then_inc(ring_free[use[0]], 1)

                def zero_y(j):
                    nc.vector.memset(y_acc[:, j, :], 0.0).then_inc(y_zero, 1)

                def step(k, first=False, last=False):
                    group = soft(c, k)
                    for name in ("q0", "q1"):
                        rope(k, name)
                        if first:
                            zero_y(QK[name])
                    if not first:
                        attention_lo(k)
                    for name in ("q2", "q3"):
                        rope(k, name)
                        if first:
                            zero_y(QK[name])
                    turned_v_lo(ring_use(c, "proj", "vT", k), c * (KVH + KC) + k + 1)
                    if not first:
                        add_y(k, "y0")
                        add_y(k, "ho")
                    else:
                        dve.wait_ge(y_zero, (c + 1) * (KC + 1))
                    take_scores(group)
                    softmax_first(group, True)
                    if not first and not last:
                        add_y(k, "y1")
                    softmax_second(group)
                    if not last:
                        rope(k + 1, "k")
                    else:
                        add_y(k, "y1")
                    if not first:
                        add_y(k, "y2")
                    probs_lo(group)
                    if not first:
                        add_y(k, "y3")

                rope(0, "k")
                dve.wait_ge(stored, (c + PRIMED) * 16)
                zero_y(0)
                step(0, True)
                with dve.Fori(1, KVH - 1) as k:
                    step(k)
                step(KVH - 1, last=True)
                attention_lo(KVH)
                add_y(KVH, "ho")
                b, n = ring_use(c, "wo", "ho", KVH)
                dve.wait_ge(ring_free[b], n + 1 + PRIMED)
                own_hidden(c, 3, y_acc[:, KC, :], own[:, :], None)
                for j in range(KC):
                    add_y(KVH, f"y{j}")
                    if j % 2:
                        lo_block(1, j, y_acc[:, j, :], c * 8)

                def spread_lo(q):
                    for h in range(1):
                        col = C_HM + GROUP * q + h
                        last = ts(q_lo[:, h, :], q2_lo, cst[:, col:col + 1], None, ALU.mult)
                    last.then_inc(qx_ok, 1)

                def take_q(hb):
                    b, n = ring_use(c, "b", 0, hb)
                    dve.wait_ge(q2_hi_ok, c * KC + hb + 1)
                    tt(q2_lo, ring[b][:, :], q2_hi, ALU.subtract).then_inc(ring_free[b], 1)

                def take_k(hb):
                    b, _ = ring_use(c, "b", 1, hb)
                    dve.wait_ge(k2_hi_ok, c * KC + hb + 1)
                    tt(k_lo[:, :], ring[b][:, :], f(k_hi[:, :]), ALU.subtract).then_inc(ring_free[b], 1)

                def spread_first(hb):
                    b, n = ring_use(c, "b", 0, hb)
                    dve.wait_ge(ring_free[b], n + 1 + PRIMED)
                    spread_lo(0)

                def values_out(hb, q):
                    dve.wait_ge(pv2_full, (c * KC + hb) * 2 + q + 1)
                    dve.wait_ge(o2_sum, c * KC + hb + PRIMED)
                    for h in (2, 3):
                        rows = slice(T * h, T * h + T)
                        ts(quad_out[rows, q, :].rearrange("p (a n) -> p a n", a=TILES), att[rows, :, h * P:(h + 1) * P],
                           cst[rows, C_EVEN + q:C_EVEN + q + 1], None, ALU.mult).then_inc(o2_ok, 1)

                def head_block(hb, last=False):
                    group = soft(c, hb * 2 + 8)
                    softmax_second(group)
                    turned_v_lo(ring_use(c, "b", 3, hb), c * (KVH + KC) + hb + KVH + 1)
                    if not last:
                        take_q(hb + 1)
                    take_scores(group + 1, True)
                    probs_lo(group)
                    softmax_first(group + 1, False)
                    if not last:
                        take_k(hb + 1)
                        spread_first(hb + 1)
                    dve.wait_ge(p_ok, group * 4 + 4)
                    softmax_second(group + 1)
                    values_out(hb, 0)
                    probs_lo(group + 1)
                    if not last:
                        take_scores(group + 2, True)
                        spread_lo(1)
                        softmax_first(group + 2, False)
                    values_out(hb, 1)
                    if last:
                        dve.wait_ge(o2_ok, (c + 1) * KC * 8 + PRIMED)
                        dve.wait_ge(o2_lo_ok, c * KC + hb + PRIMED)
                        tt(o2_f, quad_out[:, 0, :], quad_out[:, 1, :], ALU.add).then_inc(o2_sum, 1)
                        dve.wait_ge(o2_hi_ok, c * KC + KC)
                        tt(o_lo[:, KC - 1, :], o2_f, f(o_hi[:, KC - 1, :]), ALU.subtract).then_inc(o2_lo_ok, 1)

                take_q(0)
                spread_first(0)
                take_k(0)
                take_scores(soft(c, 8))
                spread_lo(1)
                softmax_first(soft(c, 8), False)
                with dve.Fori(0, KC - 1) as hb:
                    head_block(hb)
                head_block(KC - 1, True)

                dve.wait_ge(ld_res, (c + 1) * 16)
                for j in range(KC):
                    use = ring_use(c, "out2", j)
                    tt(x_res[:, j, :], full(use)[:, :], x_res[:, j, :], ALU.add).then_inc(ring_free[use[0]], 1)
                for j in (1, 3):
                    lo_block(0, j, x_res[:, j, :], c * 8 + KC)

                def routed(layer):
                    chain = Chain(dve, routing, (c * 2 + layer) * N_ROUTING)
                    use = ring_use(c, "route", 2, layer)
                    src = full(use)[:, :].rearrange("p (a n) -> p a n", a=TILES)[:, :, P - E:P]

                    def wide(ap):
                        return ap[:, :].unsqueeze(2).to_broadcast([P, TILES, E])

                    tie = cst[:, C_TIE:C_TIE + E].unsqueeze(1).to_broadcast([P, TILES, E])
                    if layer == 0:
                        ins = stt(out=rt["l"][:, :, :], in0=lang[:, :, :], scalar=LANG_BIAS, in1=src,
                                  op0=ALU.mult, op1=ALU.add)
                    else:
                        ins = nc.vector.tensor_copy(rt["l"][:, :, :], src)
                    chain.then(ins)
                    dve.sem_inc(ring_free[use[0]], 1)

                    def largest(logits, m, chosen):
                        chain.then(nc.vector.tensor_reduce(rs[m][:, :], logits[:, :, :], AX.X, ALU.max))
                        chain.then(tt(rt["eq"][:, :, :], logits[:, :, :], wide(rs[m]), ALU.is_equal))
                        chain.then(tt(rt["eq"][:, :, :], rt["eq"][:, :, :], tie, ALU.mult))
                        chain.then(nc.vector.tensor_reduce(rs["c"][:, :], rt["eq"][:, :, :], AX.X, ALU.max))
                        chain.then(tt(rt[chosen][:, :, :], tie, wide(rs["c"]), ALU.is_equal))

                    largest(rt["l"], "m1", "one")
                    chain.then(stt(out=rt["l2"][:, :, :], in0=rt["one"][:, :, :], scalar=-3e38,
                                   in1=rt["l"][:, :, :], op0=ALU.mult, op1=ALU.add))
                    chain.then(nc.vector.tensor_reduce(rs["m2"][:, :], rt["l2"][:, :, :], AX.X, ALU.max))
                    chain.then(tt(rt["eq"][:, :, :], rt["l2"][:, :, :], wide(rs["m2"]), ALU.is_equal))
                    chain.then(tt(rt["eq"][:, :, :], rt["eq"][:, :, :], tie, ALU.mult))
                    chain.then(nc.vector.tensor_reduce(rs["c"][:, :], rt["eq"][:, :, :], AX.X, ALU.max))
                    chain.then(tt(rs["d"][:, :], rs["m2"][:, :], rs["m1"][:, :], ALU.subtract))
                    assert chain.n == 12
                    chain.then(tt(rt["two"][:, :, :], tie, wide(rs["c"]), ALU.is_equal))
                    dve.wait_ge(route_exp, c * 2 + layer + 1)
                    chain.then(ts(rs["s"][:, :], rs["e"][:, :], 1.0, None, ALU.add))
                    chain.then(nc.vector.reciprocal(rs["w1"][:, :], rs["s"][:, :]))
                    chain.then(stt(out=rs["w2"][:, :], in0=rs["e"][:, :], scalar=SCALING, in1=rs["w1"][:, :],
                                   op0=ALU.mult, op1=ALU.mult))
                    chain.then(ts(rs["w1"][:, :], rs["w1"][:, :], SCALING, None, ALU.mult))
                    assert chain.n == N_ROUTING
                    gate_chain = Chain(dve, gating, (c * 2 + layer) * 3)
                    gate_chain.then(tt(rt["one"][:, :, :], rt["one"][:, :, :], wide(rs["w1"]), ALU.mult))
                    gate_chain.then(tt(rt["two"][:, :, :], rt["two"][:, :, :], wide(rs["w2"]), ALU.mult))
                    gate_chain.then(tt(rt["gate"][:, :, :], rt["one"][:, :, :], rt["two"][:, :, :], ALU.add))
                    nc.vector.tensor_copy(gate_x[:, :, :, :], rt["gate"][:, :, :].unsqueeze(3)
                                          .to_broadcast([P, TILES, E, R])).then_inc(gate_ok, 1)
                    b, n = ring_use(c, "route", 3, layer)
                    dve.wait_ge(ring_free[b], n + 1 + PRIMED)
                    use = ring_use(c, "route", 1, layer)
                    own_hidden(c, 4 + layer, full(use)[:, :], gate_t, use[0])
                    dve.wait_ge(h_hi_ok, c * 6 + 5 + layer)
                    tt(h_lo[:, 1 + layer, :], h_f[:, layer, :], f(h_hi[:, 1 + layer, :]), ALU.subtract)\
                        .then_inc(h_ok, 1)

                routed(0)
                for j in range(KC):
                    dve.wait_ge(act_hi_ok[1], c * 8 + KC + j + 1)
                    tt(act_lo[1][:, j, :], att[:, j, :], f(act_hi[1][:, j, :]), ALU.subtract)\
                        .then_inc(act_ok[1][j], 1)
                take_next(c + 1)
                routed(1)
                for j in range(KC):
                    dve.wait_ge(base_full, c * 8 + KC + j + 1)
                    stt(out=y_acc[:, j, :], in0=att[:, j, :], scalar=ffn_b[:, j:j + 1], in1=x_res[:, j, :],
                        op0=ALU.add, op1=ALU.add).then_inc(f_sum, 1)

        @block.gpsimd
        def _(pool):
            def lo(out, whole, hi):
                return nc.gpsimd.tensor_tensor(out, whole, f(hi), ALU.subtract)

            def split(c, part, j, slot, content, k=0):
                r, n = raw_use(c, part, j, k)
                pool.wait_ge(w_hi_ok[slot], w_count(c, slot, content))
                lo(w_lo_t[slot][:, :], raw[r][:, :], w_hi_t[slot][:, :]).then_inc(w_ok[slot], 1)
                pool.wait_ge(w_ok[slot], w_count(c, slot, content))
                pool.sem_inc(raw_free[r], 1)

            def split_head(c, part, which, of):
                for j, s in enumerate(HEAD_ORDER):
                    if s in which:
                        split(c, part, j, s, CONTENTS[s] * of)

            def hidden(c, fill, at):
                pool.wait_ge(h_hi_ok, c * 6 + fill + 1)
                lo(h_lo[:, at, :], h_f[:, fill % 2, :], h_hi[:, at, :]).then_inc(h_ok, 1)

            def probs_lo(group):
                for b in range(2):
                    rows = slice(T * b, T * b + T)
                    pool.wait_ge(p_hi_ok, group * 4 + b + 1)
                    lo(p_lo[rows, :, b, :], pT[rows, :, :], p_hi[rows, :, b, :]).then_inc(p_ok, 1)
                pool.wait_ge(p_ok, group * 4 + 4)

            for primed in raw_free + [o2_lo_ok]:
                pool.sem_inc(primed, PRIMED)
            def lo_block(i, a, src, count):
                pool.wait_ge(act_hi_ok[i], count + a + 1)
                lo(act_lo[i][:, a, :], src, act_hi[i][:, a, :]).then_inc(act_ok[i][a], 1)

            def take_next(c):
                for a in (0, 2):
                    lo_block(0, a, x_next[a], c * 8)

            take_next(0)
            split_head(0, "prologue", HEAD_ORDER[:LATE], 0)
            pool.wait_ge(zeroed, 2)
            with pool.Fori(0, CHUNKS) as c:
                for j in range(3):
                    hidden(c, j, j)
                split_head(c, "late", HEAD_ORDER[LATE:], 0)

                def step(k, first=False):
                    def qk_lo(name, dst, hi):
                        pool.wait_ge(qk_hi_ok, step_of(c, k) * 5 + QK[name] + 1)
                        lo(dst, roped[:, QK[name] % 2, :], hi).then_inc(qk_ok, 1)

                    qk_lo("k", k_lo[:, :], k_hi[:, :])
                    split(c, "step", 0, 0, k + 1, k)
                    split(c, "step", 1, 1, k + 1, k)
                    for g in range(GROUP):
                        qk_lo(f"q{g}", q_lo[:, g, :], q_hi[:, g, :])
                        split(c, "step", 2 + g, 2 + g, k + 1, k)
                    for j in range(6, SLOTS):
                        s = STEP_ORDER[j]
                        if j == SLOTS - (1 if first else 2):
                            probs_lo(soft(c, k))
                        split(c, "step", j, s, k + WO_FIRST[s], k)

                step(0, True)
                with pool.Fori(1, KVH) as k:
                    step(k)
                def split_epi(j):
                    split(c, "epi", j, EPI_ORDER[j], KVH + WO_FIRST[EPI_ORDER[j]])

                split_epi(0)
                hidden(c, 3, 0)
                for j in range(KC):
                    if j % 2 == 0:
                        lo_block(1, j, y_acc[:, j, :], c * 8)
                    split_epi(1 + j)

                def split_b(s, hb):
                    split(c, "b", s, s, hb + QKV2_FIRST + 1, hb)

                def spread_lo(hb, q):
                    b, n = ring_use(c, "b", 0, hb)
                    pool.wait_ge(ring_free[b], n + 1 + PRIMED)
                    pool.wait_ge(s_full, soft(c, 8 + hb * 2 + q))
                    for h in (1, 2, 3):
                        col = C_HM + GROUP * q + h
                        last = nc.gpsimd.tensor_tensor(q_lo[:, h, :], q2_lo, cst[:, col:col + 1].to_broadcast([P, CT]),
                                                       ALU.mult)
                    last.then_inc(qx_ok, 1)

                def head_block(hb, last=False):
                    probs_lo(soft(c, hb * 2 + 8))
                    if not last:
                        spread_lo(hb + 1, 0)
                        split_b(0, hb + 1)
                        split_b(1, hb + 1)
                    probs_lo(soft(c, hb * 2 + 9))
                    if not last:
                        split_b(2, hb + 1)
                        spread_lo(hb + 1, 1)
                        pool.wait_ge(o2_ok, (c * KC + hb + 1) * 8 + PRIMED)
                        nc.gpsimd.tensor_tensor(o2_f, quad_out[:, 0, :], quad_out[:, 1, :], ALU.add)\
                            .then_inc(o2_sum, 1)
                        pool.wait_ge(o2_hi_ok, c * KC + hb + 1)
                        at = bass.ds(hb, 1)
                        lo(o_lo[:, at, :], o2_f.unsqueeze(1), o_hi[:, at, :]).then_inc(o2_lo_ok, 1)
                        pool.wait_ge(o2_lo_ok, c * KC + hb + 1 + PRIMED)

                spread_lo(0, 0)
                for s in range(3):
                    split_b(s, 0)
                spread_lo(0, 1)
                with pool.Fori(0, KC - 1) as hb:
                    head_block(hb)
                head_block(KC - 1, True)
                for j in (0, 2):
                    lo_block(0, j, x_res[:, j, :], c * 8 + KC)
                for j, (s, content) in enumerate(MID_PIECES):
                    split(c, "mid", j, s, content)
                take_next(c + 1)
                split_head(c, "head", HEAD_ORDER[:4], 1)
                split_head(c, "head", HEAD_ORDER[4:LATE], 1)


def weight_stream(a):
    out = np.zeros((sum(CONTENTS), P, 5, P), np.float32)

    def put(slot, content, blocks, at=0):
        out[SLOT_BASE[slot] + content, :, at:at + len(blocks)] = np.transpose(blocks, (1, 0, 2))

    def rows(w, cols):
        return w[:, cols].reshape(-1, P, P)

    up = {n: a["L0_cond_b" + n].reshape(E * R, -1) for n in "qkvo"}
    down = {n: np.transpose(a["L0_cond_a" + n], (1, 0, 2)).reshape(-1, E * R) for n in "qkvo"}
    for s, n in zip(LORA_A_SLOTS, "kvq"):
        put(s, 0, rows(down[n], slice(None)))
    for k in range(KVH):
        for slot, n, h in [(0, "k", k), (1, "v", k)] + [(2 + g, "q", k * GROUP + g) for g in range(GROUP)]:
            cols = slice(h * HD, (h + 1) * HD)
            put(slot, k, rows(a["L0_cond_w" + n], cols))
            put(slot, k, up[n][None, :, cols], KC)
        mine = slice(k * GROUP * HD, (k + 1) * GROUP * HD)
        for j in range(KC):
            put(6 + j, k + WO_FIRST[6 + j], rows(a["L0_cond_wo"][mine], slice(j * P, (j + 1) * P)))
        put(10, k + WO_FIRST[10], rows(down["o"][mine], slice(None)))
    put(*BO_PIECE, up["o"].reshape(P, KC, P).transpose(1, 0, 2))
    turned = np.arange(DM).reshape(KC, 2, GROUP, HD2).transpose(0, 2, 1, 3).reshape(DM)
    for hb in range(KC):
        for s, n in enumerate("qkv"):
            put(s, QKV2_FIRST + hb, rows(a["L0_attn_w_" + n][turned].T, slice(hb * P, (hb + 1) * P)))
    for j, (s, content) in enumerate(OUT2_PIECES):
        put(s, content, rows(a["L0_attn_w_o"].T[turned], slice(j * P, (j + 1) * P)))
    layers = [("L0_cond2_W", "L0_cond2_Wr", "L0_cond2_A", "L0_cond2_B"),
              ("L0_ffn_W_base", "L0_ffn_W_router", "L0_ffn_A_stack", "L0_ffn_B_stack")]
    for (wb, wr, wa, wu), ((sa, ca), pieces) in zip(layers, ROUTED):
        put(sa, ca, rows(a[wa].reshape(E * R, DM).T, slice(None)))
        router = a[wr].T.reshape(KC, P, E).transpose(1, 0, 2)
        out[SLOT_BASE[sa] + ca, :, KC, 0:KC * E] = router.reshape(P, KC * E)
        up2 = np.transpose(a[wu], (0, 2, 1)).reshape(E * R, DM)
        for j, (s, content) in enumerate(pieces):
            cols = slice(j * P, (j + 1) * P)
            put(s, content, rows(a[wb].T, cols))
            put(s, content, up2[None, :, cols], KC)
    return out.reshape(-1, P, PIECE)


def layouts(a):
    x = a["x"].reshape(CHUNKS, CT, KC, P).transpose(0, 3, 2, 1).reshape(CHUNKS, P, KC * CT)

    def over_partitions(v):
        return np.broadcast_to(v.reshape(CHUNKS, 1, CT), (CHUNKS, P, CT))

    def one_more(v):
        return np.concatenate([v, v[:1]])

    idx = a["itok_B_0_7"]
    idx_tok = np.repeat(idx, T)
    m = a["mask_BxS_bf1"].view(np.uint8).reshape(CHUNKS, TILES, 4, 1, T)
    m = np.broadcast_to(m, (CHUNKS, TILES, 4, T, T)).transpose(0, 2, 3, 1, 4).reshape(CHUNKS, P, TILES * T)
    return {
        "xT": one_more(x),
        "pos": one_more(over_partitions(a["pos_BxS"])),
        "idx": one_more(over_partitions(idx_tok)),
        "idx_tile": one_more(idx_tok.reshape(CHUNKS, TILES, P).transpose(0, 2, 1)),
        "mask": one_more(m),
        "bias": a["L0_ffn_b_base"].reshape(KC, P).T,
        "consts": constants(),
        "stream": weight_stream(a),
    }


def kernel(**inputs):
    from concourse import bacc
    from concourse.bass_utils import run_bass_kernel_spmd

    a = {n: np.asarray(v) for n, v in inputs.items()}
    nc = bacc.Bacc("TRN2", target_bir_lowering=False, num_devices=1)
    arrays, args = {}, {}
    for name, v in layouts(a).items():
        v = np.ascontiguousarray(v)
        arrays[f"in_{name}"] = v
        args[name] = nc.dram_tensor(f"in_{name}", v.shape, mybir.dt.from_np(v.dtype), kind="ExternalInput").ap()
    args["outT"] = nc.dram_tensor("out_T", (CHUNKS, P, KC * CT), F32, kind="ExternalOutput").ap()
    build(nc, **args)
    r = run_bass_kernel_spmd(nc, [arrays], core_ids=[0])
    got = r.results[0]["out_T"].reshape(CHUNKS, P, KC, CT).transpose(0, 3, 2, 1)
    return np.ascontiguousarray(got.reshape(B, T, DM))
```
